# Optimizing a Trainium2 kernel written in Bass

```python
import numpy as np
import jax
import jax.numpy as jnp

def _softmax(x, axis=-1):
    return jax.nn.softmax(x, axis=axis)

def _gelu(x):
    return jax.nn.gelu(x, approximate=True)

def _silu(x):
    return jax.nn.silu(x)

def _sigmoid(x):
    return jax.nn.sigmoid(x)

def _layernorm(x, axis=-1, eps=1e-05):
    m = jnp.mean(x, axis=axis, keepdims=True)
    v = jnp.var(x, axis=axis, keepdims=True)
    return (x - m) / jnp.sqrt(v + eps)

def _scatter_add(tgt, idx, src, axis=0):
    return tgt.at[idx].add(src)

def _segment_sum(src, seg, n):
    return jax.ops.segment_sum(src, seg, n)
kernel_name = 'mk_adaln_attn_ffn_d2_seqx_r4_9a46e1'

def setup_inputs(seed: int=0):
    np.random.seed(seed)
    _w = jnp.asarray

    def _rec_inputs():
        import jax
        import jax.numpy as jnp
        _rk = jax.random.key(seed)
        x = 7.22e-05 + 1 * jax.random.normal(jax.random.fold_in(_rk, 1), (8, 512, 256), jnp.float32)
        _lenS = 512 - jax.random.randint(jax.random.fold_in(_rk, 7), (8,), 0, max(1, 512 // 4) + 1, jnp.int32)
        _lenS2 = 512 - jax.random.randint(jax.random.fold_in(_rk, 8), (8,), 0, max(1, 512 // 4) + 1, jnp.int32)
        cond_512 = 0.0061147 + 1.02565 * jax.random.normal(jax.random.fold_in(_rk, 11), (8, 128), jnp.float32)
        itok_BxS_0_999 = jax.random.randint(jax.random.fold_in(_rk, 12), (8, 512), 0, 250, jnp.int32)
        itok_BxS_0_4 = jax.random.randint(jax.random.fold_in(_rk, 13), (8, 512), 0, 5, jnp.int32)
        cond_64 = 0.0990542 + 1.04422 * jax.random.normal(jax.random.fold_in(_rk, 15), (8, 64), jnp.float32)
        fside_Bx32_0 = -0.136436 + 0.990155 * jax.random.normal(jax.random.fold_in(_rk, 16), (8, 32), jnp.float32)
        _validS = jnp.arange(512)[None, :] < _lenS[:, None]
        _validS2 = jnp.arange(512)[None, :] < _lenS2[:, None]
        _causal = jnp.tril(jnp.ones((512, 512), dtype=bool))
        mask_BxS_ik0 = jnp.where(jnp.broadcast_to(_validS[:, :], (8, 512)), 0, 1).astype(jnp.int32)
        return (x, cond_512, itok_BxS_0_999, itok_BxS_0_4, cond_64, fside_Bx32_0, mask_BxS_ik0)
    x, cond_512, itok_BxS_0_999, itok_BxS_0_4, cond_64, fside_Bx32_0, mask_BxS_ik0 = _rec_inputs()

    def _L0_cond_setup():
        import jax, jax.numpy as jnp
        import numpy as np
        import math
        HEAD_NUM = 16
        EPS = 1e-08

        def modulated_linear(x, s, aff_w, aff_b, w, b):
            style = s @ aff_w.T + aff_b
            w_mod = w[None, :, :] * style[:, None, :]
            demod = jax.lax.rsqrt(jnp.sum(w_mod * w_mod, axis=2) + EPS)
            w_mod = w_mod * demod[:, :, None]
            return jnp.einsum('bni,boi->bno', x, w_mod) + b
        key = jax.random.key(seed)
        ks = jax.random.split(key, 6)
        B, N, F, S = (8, 256, 256, 128)
        return {'x': jax.random.normal(ks[0], (B, N, F), dtype=jnp.float32), 's': jax.random.normal(ks[1], (B, S), dtype=jnp.float32), 'k_aff_w': jax.random.normal(ks[2], (F, S), dtype=jnp.float32) * 0.02, 'k_aff_b': jnp.ones((F,), dtype=jnp.float32), 'k_w': jax.random.normal(ks[3], (F, F), dtype=jnp.float32) * 0.02, 'k_b': jnp.zeros((F,), dtype=jnp.float32), 'o_aff_w': jax.random.normal(ks[4], (F, S), dtype=jnp.float32) * 0.02, 'o_aff_b': jnp.ones((F,), dtype=jnp.float32), 'o_w': jax.random.normal(ks[5], (F, F), dtype=jnp.float32) * 0.02, 'o_b': jnp.zeros((F,), dtype=jnp.float32)}
    _L0_cond_all = _L0_cond_setup()
    _L0_cond_in = {k: v for k, v in _L0_cond_all.items() if k in ('k_aff_w', 'k_aff_b', 'k_w', 'k_b', 'o_aff_w', 'o_aff_b', 'o_w', 'o_b')}
    del _L0_cond_all

    def _L0_attn_setup():
        import jax, jax.numpy as jnp
        import numpy as np
        _J6 = jnp.array([[0, 0, 0, 0, 0, 1], [0, 0, 0, 0, -1, 0], [0, 0, 0, 1, 0, 0], [0, 0, 1, 0, 0, 0], [0, -1, 0, 0, 0, 0], [1, 0, 0, 0, 0, 0]], dtype=jnp.float32)
        _PI = jnp.array([0, 0, 0, 1, 1, 2])
        _PJ = jnp.array([1, 2, 3, 2, 3, 3])

        def exterior(p1, p2):
            L = p1[..., _PI] * p2[..., _PJ] - p1[..., _PJ] * p2[..., _PI]
            n = jnp.clip(jnp.linalg.norm(L, axis=-1, keepdims=True), 1e-12)
            return L / n
        key = jax.random.key(seed)
        ks = jax.random.split(key, 8)
        B, T, D, H = (2, 512, 256, 16)
        pd = 4
        s = 0.02
        return {'x': jax.random.normal(ks[0], (B, T, D), jnp.float32), 'w_qkv': jax.random.normal(ks[1], (3 * D, D), jnp.float32) * s, 'b_qkv': jnp.zeros((3 * D,), jnp.float32), 'w1_write': jax.random.normal(ks[2], (pd * H, D), jnp.float32) * s, 'w2_write': jax.random.normal(ks[3], (pd * H, D), jnp.float32) * s, 'w1_read': jax.random.normal(ks[4], (pd * H, D), jnp.float32) * s, 'w2_read': jax.random.normal(ks[5], (pd * H, D), jnp.float32) * s, 'w_out': jax.random.normal(ks[6], (D, D), jnp.float32) * s, 'b_out': jnp.zeros((D,), jnp.float32), 'decay_logits': jnp.full((H,), 4.6, jnp.float32), 'bias_scale': jnp.full((H,), 0.1, jnp.float32)}
    _L0_attn_all = _L0_attn_setup()
    _L0_attn_in = {k: v for k, v in _L0_attn_all.items() if k in ('w_qkv', 'b_qkv', 'w1_write', 'w2_write', 'w1_read', 'w2_read', 'w_out', 'b_out', 'decay_logits', 'bias_scale')}
    del _L0_attn_all

    def _L0_cond2_setup():
        import jax, jax.numpy as jnp
        import numpy as np
        EPS = 1e-05

        def _ln(x, g, b):
            m = jnp.mean(x, axis=-1, keepdims=True)
            v = jnp.mean((x - m) ** 2, axis=-1, keepdims=True)
            return (x - m) * jax.lax.rsqrt(v + EPS) * g + b

        def _mlp_ln(s, W1, b1, W2, b2, g, b):
            h = jax.nn.silu(s @ W1 + b1) @ W2 + b2
            return _ln(h, g, b)
        key = jax.random.key(seed)
        B, S, D = (4, 512, 256)
        MEM, NOI, RES = (128, 64, 32)
        ks = jax.random.split(key, 40)
        ki = iter(range(40))

        def nrm(shape, scale=0.02):
            return jax.random.normal(ks[next(ki)], shape, jnp.float32) * scale

        def gamma(shape):
            return jnp.ones(shape, jnp.float32) + nrm(shape)
        inp = {'x': jax.random.normal(ks[next(ki)], (B, S, D), jnp.float32), 'pathway_ids': jax.random.randint(ks[next(ki)], (B, S), 0, 250), 'compartment_ids': jax.random.randint(ks[next(ki)], (B, S), 0, 5), 'time_steps': jax.random.randint(ks[next(ki)], (B, S), 0, 5), 'scale_type': jax.random.randint(ks[next(ki)], (B, S), 0, 3), 'memory_state': jax.random.normal(ks[next(ki)], (B, MEM), jnp.float32), 'noise_state': jax.random.normal(ks[next(ki)], (B, NOI), jnp.float32), 'resource_state': jax.random.normal(ks[next(ki)], (B, RES), jnp.float32), 'pw_g': gamma((250, D)), 'pw_b': nrm((250, D)), 'cp_g': gamma((5, D)), 'cp_b': nrm((5, D)), 'tm_g': gamma((5, D)), 'tm_b': nrm((5, D)), 'ms_g': gamma((3, D)), 'ms_b': nrm((3, D)), 'mem_W1': nrm((MEM, D)), 'mem_b1': jnp.zeros((D,)), 'mem_W2': nrm((D, D)), 'mem_b2': jnp.zeros((D,)), 'mem_g': gamma((D,)), 'mem_be': jnp.zeros((D,)), 'noi_W1': nrm((NOI, D)), 'noi_b1': jnp.zeros((D,)), 'noi_W2': nrm((D, D)), 'noi_b2': jnp.zeros((D,)), 'noi_g': gamma((D,)), 'noi_be': jnp.zeros((D,)), 'res_W1': nrm((RES, D)), 'res_b1': jnp.zeros((D,)), 'res_W2': nrm((D, D)), 'res_b2': jnp.zeros((D,)), 'res_g': gamma((D,)), 'res_be': jnp.zeros((D,)), 'int_W1': nrm((6 * D, D)), 'int_b1': jnp.zeros((D,)), 'int_W2': nrm((D, D)), 'int_b2': jnp.zeros((D,)), 'int_g': gamma((D,)), 'int_be': jnp.zeros((D,)), 'aw': jnp.ones((6,), jnp.float32) / 6.0}
        return inp
    _L0_cond2_all = _L0_cond2_setup()
    _L0_cond2_in = {k: v for k, v in _L0_cond2_all.items() if k in ('pw_g', 'pw_b', 'cp_g', 'cp_b', 'tm_g', 'tm_b', 'ms_g', 'ms_b', 'mem_W1', 'mem_b1', 'mem_W2', 'mem_b2', 'mem_g', 'mem_be', 'noi_W1', 'noi_b1', 'noi_W2', 'noi_b2', 'noi_g', 'noi_be', 'res_W1', 'res_b1', 'res_W2', 'res_b2', 'res_g', 'res_be', 'int_W1', 'int_b1', 'int_W2', 'int_b2', 'int_g', 'int_be', 'aw')}
    del _L0_cond2_all

    def _L0_ffn_setup():
        import jax, jax.numpy as jnp
        import numpy as np
        E = 8
        K = 2
        CAPACITY_FACTOR = 1.25
        key = jax.random.key(seed)
        ks = jax.random.split(key, 4)
        B, T, C, H = (8, 512, 256, 1024)
        x = jax.random.normal(ks[0], (B, T, C), jnp.float32)
        Wr = jax.random.normal(ks[1], (C, E), jnp.float32) * 0.02
        br = jnp.zeros((E,), jnp.float32)
        W1 = jax.random.normal(ks[2], (E, C, H), jnp.float32) * 0.02
        b1 = jnp.zeros((E, H), jnp.float32)
        W2 = jax.random.normal(ks[3], (E, H, C), jnp.float32) * 0.02
        b2 = jnp.zeros((E, C), jnp.float32)
        return {'x': x, 'Wr': Wr, 'br': br, 'W1': W1, 'b1': b1, 'W2': W2, 'b2': b2}
    _L0_ffn_all = _L0_ffn_setup()
    _L0_ffn_in = {k: v for k, v in _L0_ffn_all.items() if k in ('Wr', 'br', 'W1', 'b1', 'W2', 'b2')}
    del _L0_ffn_all

    def _L1_cond_setup():
        import jax, jax.numpy as jnp
        import numpy as np
        B, S, D, H, C = (8, 1024, 256, 64, 128)
        INIT_RANGE = 0.01
        key = jax.random.key(seed)
        ks = jax.random.split(key, 6)
        return {'hidden_states': jax.random.normal(ks[0], (B, S, D), dtype=jnp.float32), 'conditions': jax.random.normal(ks[1], (B, C), dtype=jnp.float32), 'down_project': jax.random.normal(ks[2], (D, H), dtype=jnp.float32) * INIT_RANGE, 'down_gamma': jax.random.normal(ks[3], (C, H), dtype=jnp.float32), 'down_beta': jnp.zeros((C, H), dtype=jnp.float32), 'up_project': jax.random.normal(ks[4], (H, D), dtype=jnp.float32) * INIT_RANGE, 'up_gamma': jax.random.normal(ks[5], (C, D), dtype=jnp.float32), 'up_beta': jnp.zeros((C, D), dtype=jnp.float32)}
    _L1_cond_all = _L1_cond_setup()
    _L1_cond_in = {k: v for k, v in _L1_cond_all.items() if k in ('down_project', 'down_gamma', 'down_beta', 'up_project', 'up_gamma', 'up_beta')}
    del _L1_cond_all

    def _L1_attn_setup():
        import jax, jax.numpy as jnp
        import numpy as np
        import math
        D_MODEL = 256
        NHEAD = 16
        M = 64
        D_K = D_MODEL // NHEAD
        EPS = 1e-06

        def create_orf(key, d_k, m):
            k1, k2 = jax.random.split(key)
            n_blocks = math.ceil(m / d_k)
            blocks = jax.random.normal(k1, (n_blocks, d_k, d_k), dtype=jnp.float32)
            q, _ = jnp.linalg.qr(blocks)
            scale = jnp.linalg.norm(jax.random.normal(k2, (m, d_k), dtype=jnp.float32), axis=1)
            return scale[:, None] * q.reshape(-1, d_k)[:m]

        def feature_map(x, orf):
            m, d_k = orf.shape
            proj = x @ orf.T / d_k ** 0.25
            norm = jnp.sum(x * x, axis=-1, keepdims=True) / (2.0 * math.sqrt(d_k))
            return (jnp.exp(proj - norm) + EPS) / math.sqrt(m)
        key = jax.random.key(seed)
        ks = jax.random.split(key, 10)
        s = 1.0 / math.sqrt(D_MODEL)
        inp = {'x': jax.random.normal(ks[0], (4, 1024, D_MODEL), dtype=jnp.float32)}
        names = ['q', 'k', 'v', 'o']
        for i, n in enumerate(names):
            inp[f'W{n}'] = jax.random.uniform(ks[1 + 2 * i], (D_MODEL, D_MODEL), dtype=jnp.float32, minval=-s, maxval=s)
            inp[f'b{n}'] = jax.random.uniform(ks[2 + 2 * i], (D_MODEL,), dtype=jnp.float32, minval=-s, maxval=s)
        inp['orf'] = create_orf(ks[9], D_K, M)
        return inp
    _L1_attn_all = _L1_attn_setup()
    _L1_attn_in = {k: v for k, v in _L1_attn_all.items() if k in ('Wq', 'bq', 'Wk', 'bk', 'Wv', 'bv', 'Wo', 'bo', 'orf')}
    del _L1_attn_all

    def _L1_cond2_setup():
        import jax, jax.numpy as jnp
        import numpy as np
        IN_DIM = 256
        OUT_DIM = 256
        MU_DIM = 128
        K = 30
        key = jax.random.key(seed)
        k1, k2, k3, k4, k5 = jax.random.split(key, 5)
        B, S = (16, 512)
        x = jax.random.normal(k1, (B, S, IN_DIM), dtype=jnp.float32)
        mu = jax.random.normal(k2, (B, MU_DIM), dtype=jnp.float32)
        W_dec = jax.random.normal(k3, (MU_DIM, (IN_DIM + 1) * K), dtype=jnp.float32) / np.sqrt(MU_DIM)
        b_dec = jax.random.normal(k4, ((IN_DIM + 1) * K,), dtype=jnp.float32) * 0.01
        V = jax.random.normal(k5, (K, OUT_DIM), dtype=jnp.float32) / np.sqrt(K)
        return {'x': x, 'mu': mu, 'W_dec': W_dec, 'b_dec': b_dec, 'V': V}
    _L1_cond2_all = _L1_cond2_setup()
    _L1_cond2_in = {k: v for k, v in _L1_cond2_all.items() if k in ('W_dec', 'b_dec', 'V')}
    del _L1_cond2_all

    def _L1_ffn_setup():
        import jax, jax.numpy as jnp
        import numpy as np
        B, S, IN, OUT = (4, 2048, 256, 256)
        EPS = 1e-06

        def _xla_quantized_matmul(x2d, weight_q, weight_scale):
            amax = jnp.max(jnp.abs(x2d), axis=-1, keepdims=True)
            x_scale = jnp.maximum(amax, EPS) / 127.0
            x_q = jnp.clip(jnp.round(x2d / x_scale), -128, 127).astype(jnp.int8)
            acc = jax.lax.dot_general(x_q, weight_q, (((1,), (1,)), ((), ())), preferred_element_type=jnp.int32)
            return acc.astype(jnp.float32) * x_scale * weight_scale[None, :]
        key = jax.random.key(seed)
        k1, k2, k3, k4 = jax.random.split(key, 4)
        x = jax.random.normal(k1, (B, S, IN), dtype=jnp.float32)
        weight_q = jax.random.randint(k2, (OUT, IN), -128, 128, dtype=jnp.int32).astype(jnp.int8)
        weight_scale = jax.random.uniform(k3, (OUT,), dtype=jnp.float32, minval=0.001, maxval=0.01)
        bias = jax.random.normal(k4, (OUT,), dtype=jnp.float32) * 0.01
        return {'x': x, 'weight_q': weight_q, 'weight_scale': weight_scale, 'bias': bias}
    _L1_ffn_all = _L1_ffn_setup()
    _L1_ffn_in = {k: v for k, v in _L1_ffn_all.items() if k in ('weight_q', 'weight_scale', 'bias')}
    del _L1_ffn_all
    return {'x': x, 'cond_512': cond_512, 'itok_BxS_0_999': itok_BxS_0_999, 'itok_BxS_0_4': itok_BxS_0_4, 'cond_64': cond_64, 'fside_Bx32_0': fside_Bx32_0, 'mask_BxS_ik0': mask_BxS_ik0, 'L0_cond_k_aff_w': _L0_cond_in['k_aff_w'], 'L0_cond_k_aff_b': _L0_cond_in['k_aff_b'], 'L0_cond_k_w': _L0_cond_in['k_w'], 'L0_cond_k_b': _L0_cond_in['k_b'], 'L0_cond_o_aff_w': _L0_cond_in['o_aff_w'], 'L0_cond_o_aff_b': _L0_cond_in['o_aff_b'], 'L0_cond_o_w': _L0_cond_in['o_w'], 'L0_cond_o_b': _L0_cond_in['o_b'], 'L0_attn_w_qkv': _L0_attn_in['w_qkv'], 'L0_attn_b_qkv': _L0_attn_in['b_qkv'], 'L0_attn_w1_write': _L0_attn_in['w1_write'], 'L0_attn_w2_write': _L0_attn_in['w2_write'], 'L0_attn_w1_read': _L0_attn_in['w1_read'], 'L0_attn_w2_read': _L0_attn_in['w2_read'], 'L0_attn_w_out': _L0_attn_in['w_out'], 'L0_attn_b_out': _L0_attn_in['b_out'], 'L0_attn_decay_logits': _L0_attn_in['decay_logits'], 'L0_attn_bias_scale': _L0_attn_in['bias_scale'], 'L0_cond2_pw_g': _L0_cond2_in['pw_g'], 'L0_cond2_pw_b': _L0_cond2_in['pw_b'], 'L0_cond2_cp_g': _L0_cond2_in['cp_g'], 'L0_cond2_cp_b': _L0_cond2_in['cp_b'], 'L0_cond2_tm_g': _L0_cond2_in['tm_g'], 'L0_cond2_tm_b': _L0_cond2_in['tm_b'], 'L0_cond2_ms_g': _L0_cond2_in['ms_g'], 'L0_cond2_ms_b': _L0_cond2_in['ms_b'], 'L0_cond2_mem_W1': _L0_cond2_in['mem_W1'], 'L0_cond2_mem_b1': _L0_cond2_in['mem_b1'], 'L0_cond2_mem_W2': _L0_cond2_in['mem_W2'], 'L0_cond2_mem_b2': _L0_cond2_in['mem_b2'], 'L0_cond2_mem_g': _L0_cond2_in['mem_g'], 'L0_cond2_mem_be': _L0_cond2_in['mem_be'], 'L0_cond2_noi_W1': _L0_cond2_in['noi_W1'], 'L0_cond2_noi_b1': _L0_cond2_in['noi_b1'], 'L0_cond2_noi_W2': _L0_cond2_in['noi_W2'], 'L0_cond2_noi_b2': _L0_cond2_in['noi_b2'], 'L0_cond2_noi_g': _L0_cond2_in['noi_g'], 'L0_cond2_noi_be': _L0_cond2_in['noi_be'], 'L0_cond2_res_W1': _L0_cond2_in['res_W1'], 'L0_cond2_res_b1': _L0_cond2_in['res_b1'], 'L0_cond2_res_W2': _L0_cond2_in['res_W2'], 'L0_cond2_res_b2': _L0_cond2_in['res_b2'], 'L0_cond2_res_g': _L0_cond2_in['res_g'], 'L0_cond2_res_be': _L0_cond2_in['res_be'], 'L0_cond2_int_W1': _L0_cond2_in['int_W1'], 'L0_cond2_int_b1': _L0_cond2_in['int_b1'], 'L0_cond2_int_W2': _L0_cond2_in['int_W2'], 'L0_cond2_int_b2': _L0_cond2_in['int_b2'], 'L0_cond2_int_g': _L0_cond2_in['int_g'], 'L0_cond2_int_be': _L0_cond2_in['int_be'], 'L0_cond2_aw': _L0_cond2_in['aw'], 'L0_ffn_Wr': _L0_ffn_in['Wr'], 'L0_ffn_br': _L0_ffn_in['br'], 'L0_ffn_W1': _L0_ffn_in['W1'], 'L0_ffn_b1': _L0_ffn_in['b1'], 'L0_ffn_W2': _L0_ffn_in['W2'], 'L0_ffn_b2': _L0_ffn_in['b2'], 'L1_cond_down_project': _L1_cond_in['down_project'], 'L1_cond_down_gamma': _L1_cond_in['down_gamma'], 'L1_cond_down_beta': _L1_cond_in['down_beta'], 'L1_cond_up_project': _L1_cond_in['up_project'], 'L1_cond_up_gamma': _L1_cond_in['up_gamma'], 'L1_cond_up_beta': _L1_cond_in['up_beta'], 'L1_attn_Wq': _L1_attn_in['Wq'], 'L1_attn_bq': _L1_attn_in['bq'], 'L1_attn_Wk': _L1_attn_in['Wk'], 'L1_attn_bk': _L1_attn_in['bk'], 'L1_attn_Wv': _L1_attn_in['Wv'], 'L1_attn_bv': _L1_attn_in['bv'], 'L1_attn_Wo': _L1_attn_in['Wo'], 'L1_attn_bo': _L1_attn_in['bo'], 'L1_attn_orf': _L1_attn_in['orf'], 'L1_cond2_W_dec': _L1_cond2_in['W_dec'], 'L1_cond2_b_dec': _L1_cond2_in['b_dec'], 'L1_cond2_V': _L1_cond2_in['V'], 'L1_ffn_weight_q': _L1_ffn_in['weight_q'], 'L1_ffn_weight_scale': _L1_ffn_in['weight_scale'], 'L1_ffn_bias': _L1_ffn_in['bias']}

def reference(x, cond_512, itok_BxS_0_999, itok_BxS_0_4, cond_64, fside_Bx32_0, mask_BxS_ik0, L0_cond_k_aff_w, L0_cond_k_aff_b, L0_cond_k_w, L0_cond_k_b, L0_cond_o_aff_w, L0_cond_o_aff_b, L0_cond_o_w, L0_cond_o_b, L0_attn_w_qkv, L0_attn_b_qkv, L0_attn_w1_write, L0_attn_w2_write, L0_attn_w1_read, L0_attn_w2_read, L0_attn_w_out, L0_attn_b_out, L0_attn_decay_logits, L0_attn_bias_scale, L0_cond2_pw_g, L0_cond2_pw_b, L0_cond2_cp_g, L0_cond2_cp_b, L0_cond2_tm_g, L0_cond2_tm_b, L0_cond2_ms_g, L0_cond2_ms_b, L0_cond2_mem_W1, L0_cond2_mem_b1, L0_cond2_mem_W2, L0_cond2_mem_b2, L0_cond2_mem_g, L0_cond2_mem_be, L0_cond2_noi_W1, L0_cond2_noi_b1, L0_cond2_noi_W2, L0_cond2_noi_b2, L0_cond2_noi_g, L0_cond2_noi_be, L0_cond2_res_W1, L0_cond2_res_b1, L0_cond2_res_W2, L0_cond2_res_b2, L0_cond2_res_g, L0_cond2_res_be, L0_cond2_int_W1, L0_cond2_int_b1, L0_cond2_int_W2, L0_cond2_int_b2, L0_cond2_int_g, L0_cond2_int_be, L0_cond2_aw, L0_ffn_Wr, L0_ffn_br, L0_ffn_W1, L0_ffn_b1, L0_ffn_W2, L0_ffn_b2, L1_cond_down_project, L1_cond_down_gamma, L1_cond_down_beta, L1_cond_up_project, L1_cond_up_gamma, L1_cond_up_beta, L1_attn_Wq, L1_attn_bq, L1_attn_Wk, L1_attn_bk, L1_attn_Wv, L1_attn_bv, L1_attn_Wo, L1_attn_bo, L1_attn_orf, L1_cond2_W_dec, L1_cond2_b_dec, L1_cond2_V, L1_ffn_weight_q, L1_ffn_weight_scale, L1_ffn_bias):
    import jax
    import jax.numpy as jnp

    def _L0_cond_ref(x, s, k_aff_w, k_aff_b, k_w, k_b, o_aff_w, o_aff_b, o_w, o_b):
        import jax, jax.numpy as jnp
        import numpy as np
        import math
        HEAD_NUM = 16
        EPS = 1e-08

        def modulated_linear(x, s, aff_w, aff_b, w, b):
            style = s @ aff_w.T + aff_b
            w_mod = w[None, :, :] * style[:, None, :]
            demod = jax.lax.rsqrt(jnp.sum(w_mod * w_mod, axis=2) + EPS)
            w_mod = w_mod * demod[:, :, None]
            return jnp.einsum('bni,boi->bno', x, w_mod) + b
        B, N, F = x.shape
        H = HEAD_NUM
        D = F // H
        kx = modulated_linear(x, s, k_aff_w, k_aff_b, k_w, k_b)
        kx = kx.reshape(B, N, H, D)
        q = k = v = kx
        scores = jnp.einsum('bnhd,bnjd->bnhj', q, k) / math.sqrt(D)
        A = jax.nn.softmax(scores, axis=-1)
        out = jnp.einsum('bnhj,bnjd->bnhd', A, v).reshape(B, N, F)
        out = modulated_linear(out, s, o_aff_w, o_aff_b, o_w, o_b)
        return out

    def _L0_attn_ref(x, w_qkv, b_qkv, w1_write, w2_write, w1_read, w2_read, w_out, b_out, decay_logits, bias_scale):
        import jax, jax.numpy as jnp
        import numpy as np
        _J6 = jnp.array([[0, 0, 0, 0, 0, 1], [0, 0, 0, 0, -1, 0], [0, 0, 0, 1, 0, 0], [0, 0, 1, 0, 0, 0], [0, -1, 0, 0, 0, 0], [1, 0, 0, 0, 0, 0]], dtype=jnp.float32)
        _PI = jnp.array([0, 0, 0, 1, 1, 2])
        _PJ = jnp.array([1, 2, 3, 2, 3, 3])

        def exterior(p1, p2):
            L = p1[..., _PI] * p2[..., _PJ] - p1[..., _PJ] * p2[..., _PI]
            n = jnp.clip(jnp.linalg.norm(L, axis=-1, keepdims=True), 1e-12)
            return L / n
        B, T, D = x.shape
        H = decay_logits.shape[0]
        dh = D // H
        pd = w1_write.shape[0] // H
        scale = dh ** (-0.5)
        qkv = (x @ w_qkv.T + b_qkv).reshape(B, T, 3, H, dh)
        qkv = jnp.transpose(qkv, (2, 0, 3, 1, 4))
        q, k, v = (qkv[0], qkv[1], qkv[2])
        std_logits = jnp.einsum('bhqd,bhkd->bhqk', q, k) * scale
        x_prev = jnp.concatenate([jnp.zeros((B, 1, D), x.dtype), x[:, :-1]], axis=1)
        w1 = (x_prev @ w1_write.T).reshape(B, T, H, pd)
        w2 = (x @ w2_write.T).reshape(B, T, H, pd)
        write_lines = exterior(w1, w2)
        r1 = (x @ w1_read.T).reshape(B, T, H, pd)
        r2 = (x @ w2_read.T).reshape(B, T, H, pd)
        read_lines = exterior(r1, r2)
        J_write = jnp.einsum('bthi,ij->bthj', write_lines, _J6)
        incidence = jnp.einsum('bqhp,bkhp->bhqk', read_lines, J_write)
        decays = jax.nn.sigmoid(decay_logits)
        pos = jnp.arange(T, dtype=x.dtype)
        diffs = pos[:, None] - pos[None, :]
        past = diffs > 0
        diffs_pos = jnp.where(past, diffs, 0.0)
        weights = decays[:, None, None] ** diffs_pos[None] * past[None].astype(x.dtype)
        bias = incidence * weights[None] * bias_scale[None, :, None, None]
        logits = std_logits + bias
        causal_mask = diffs < 0
        logits = jnp.where(causal_mask[None, None], -jnp.inf, logits)
        attn = jax.nn.softmax(logits, axis=-1)
        out = jnp.einsum('bhqk,bhkd->bqhd', attn, v).reshape(B, T, D)
        return out @ w_out.T + b_out

    def _L0_cond2_ref(x, pathway_ids, compartment_ids, time_steps, scale_type, memory_state, noise_state, resource_state, pw_g, pw_b, cp_g, cp_b, tm_g, tm_b, ms_g, ms_b, mem_W1, mem_b1, mem_W2, mem_b2, mem_g, mem_be, noi_W1, noi_b1, noi_W2, noi_b2, noi_g, noi_be, res_W1, res_b1, res_W2, res_b2, res_g, res_be, int_W1, int_b1, int_W2, int_b2, int_g, int_be, aw):
        import jax, jax.numpy as jnp
        import numpy as np
        EPS = 1e-05

        def _ln(x, g, b):
            m = jnp.mean(x, axis=-1, keepdims=True)
            v = jnp.mean((x - m) ** 2, axis=-1, keepdims=True)
            return (x - m) * jax.lax.rsqrt(v + EPS) * g + b

        def _mlp_ln(s, W1, b1, W2, b2, g, b):
            h = jax.nn.silu(s @ W1 + b1) @ W2 + b2
            return _ln(h, g, b)
        h = _ln(x, pw_g[pathway_ids], pw_b[pathway_ids])
        h = _ln(h, cp_g[compartment_ids], cp_b[compartment_ids])
        t = _ln(x, tm_g[time_steps], tm_b[time_steps])
        m = x + _mlp_ln(memory_state, mem_W1, mem_b1, mem_W2, mem_b2, mem_g, mem_be)[:, None, :]
        n = x + _mlp_ln(noise_state, noi_W1, noi_b1, noi_W2, noi_b2, noi_g, noi_be)[:, None, :]
        r = x + _mlp_ln(resource_state, res_W1, res_b1, res_W2, res_b2, res_g, res_be)[:, None, :]
        s = _ln(x, ms_g[scale_type], ms_b[scale_type])
        w = jax.nn.softmax(aw)
        cat = jnp.concatenate([w[0] * h, w[1] * t, w[2] * m, w[3] * n, w[4] * r, w[5] * s], axis=-1)
        return _mlp_ln(cat, int_W1, int_b1, int_W2, int_b2, int_g, int_be)

    def _L0_ffn_ref(x, Wr, br, W1, b1, W2, b2):
        import jax, jax.numpy as jnp
        import numpy as np
        E = 8
        K = 2
        CAPACITY_FACTOR = 1.25
        B, T, C = x.shape
        cap = max(1, int(T / E * CAPACITY_FACTOR))
        probs = jax.nn.softmax(x @ Wr + br, axis=-1)
        topk_p, topk_e = jax.lax.top_k(probs, K)
        e_flat = topk_e.reshape(B, T * K)
        p_flat = topk_p.reshape(B, T * K)
        oh = jax.nn.one_hot(e_flat, E, dtype=jnp.int32)
        pos_all = jnp.cumsum(oh, axis=1) - oh
        pos = jnp.take_along_axis(pos_all, e_flat[:, :, None], axis=2)[:, :, 0]
        keep = pos < cap
        b_idx = jnp.arange(B)[:, None]
        flat_idx = (e_flat * B + b_idx) * cap + jnp.minimum(pos, cap - 1)
        x_rep = jnp.broadcast_to(x[:, :, None, :], (B, T, K, C)).reshape(B, T * K, C)
        buf = jnp.zeros((E * B * cap, C), x.dtype).at[flat_idx.reshape(-1)].add((x_rep * keep[:, :, None].astype(x.dtype)).reshape(-1, C))
        buf = buf.reshape(E, B * cap, C)
        h = jax.nn.relu(jnp.einsum('enc,ech->enh', buf, W1) + b1[:, None, :])
        y = jnp.einsum('enh,ehc->enc', h, W2) + b2[:, None, :]
        y_tok = y.reshape(E * B * cap, C)[flat_idx.reshape(-1)].reshape(B, T * K, C)
        y_tok = y_tok * (p_flat * keep.astype(x.dtype))[:, :, None]
        return y_tok.reshape(B, T, K, C).sum(axis=2)

    def _L1_cond_ref(hidden_states, conditions, down_project, down_gamma, down_beta, up_project, up_gamma, up_beta):
        import jax, jax.numpy as jnp
        import numpy as np
        B, S, D, H, C = (8, 1024, 256, 64, 128)
        INIT_RANGE = 0.01
        dg = conditions @ down_gamma
        db = conditions @ down_beta
        ug = conditions @ up_gamma
        ub = conditions @ up_beta
        w_down = down_project[None, :, :] * dg[:, None, :] + db[:, None, :]
        down = jnp.einsum('bsd,bdh->bsh', hidden_states, w_down)
        act = jax.nn.relu(down)
        w_up = up_project[None, :, :] * ug[:, None, :] + ub[:, None, :]
        up = jnp.einsum('bsh,bhd->bsd', act, w_up)
        return up + hidden_states

    def _L1_attn_ref(x, Wq, bq, Wk, bk, Wv, bv, Wo, bo, orf):
        import jax, jax.numpy as jnp
        import numpy as np
        import math
        D_MODEL = 256
        NHEAD = 16
        M = 64
        D_K = D_MODEL // NHEAD
        EPS = 1e-06

        def create_orf(key, d_k, m):
            k1, k2 = jax.random.split(key)
            n_blocks = math.ceil(m / d_k)
            blocks = jax.random.normal(k1, (n_blocks, d_k, d_k), dtype=jnp.float32)
            q, _ = jnp.linalg.qr(blocks)
            scale = jnp.linalg.norm(jax.random.normal(k2, (m, d_k), dtype=jnp.float32), axis=1)
            return scale[:, None] * q.reshape(-1, d_k)[:m]

        def feature_map(x, orf):
            m, d_k = orf.shape
            proj = x @ orf.T / d_k ** 0.25
            norm = jnp.sum(x * x, axis=-1, keepdims=True) / (2.0 * math.sqrt(d_k))
            return (jnp.exp(proj - norm) + EPS) / math.sqrt(m)
        B, L, D = x.shape
        H, dh = (NHEAD, D // NHEAD)

        def split(y):
            return y.reshape(B, L, H, dh).transpose(0, 2, 1, 3).reshape(B * H, L, dh)
        q = feature_map(split(x @ Wq.T + bq), orf)
        k = feature_map(split(x @ Wk.T + bk), orf)
        v = split(x @ Wv.T + bv)
        kv = jnp.einsum('nlm,nld->nmd', k, v)
        ksum = jnp.sum(k, axis=1)
        buf = jnp.concatenate([kv, ksum[..., None]], axis=-1)
        out = jnp.einsum('nlm,nmd->nld', q, buf)
        out = out[..., :-1] / out[..., -1:]
        out = out.reshape(B, H, L, dh).transpose(0, 2, 1, 3).reshape(B, L, D)
        return out @ Wo.T + bo

    def _L1_cond2_ref(x, mu, W_dec, b_dec, V):
        import jax, jax.numpy as jnp
        import numpy as np
        IN_DIM = 256
        OUT_DIM = 256
        MU_DIM = 128
        K = 30
        B = mu.shape[0]
        U = (mu @ W_dec + b_dec).reshape(B, IN_DIM + 1, K)
        param = jnp.einsum('bik,kj->bij', U, V)
        weight = param[:, :-1, :]
        bias = param[:, -1, :]
        out = jnp.einsum('bsd,bde->bse', x, weight)
        out = out + bias[:, None, :]
        return out

    def _L1_ffn_ref(x, weight_q, weight_scale, bias):
        import jax, jax.numpy as jnp
        import numpy as np
        B, S, IN, OUT = (4, 2048, 256, 256)
        EPS = 1e-06

        def _xla_quantized_matmul(x2d, weight_q, weight_scale):
            amax = jnp.max(jnp.abs(x2d), axis=-1, keepdims=True)
            x_scale = jnp.maximum(amax, EPS) / 127.0
            x_q = jnp.clip(jnp.round(x2d / x_scale), -128, 127).astype(jnp.int8)
            acc = jax.lax.dot_general(x_q, weight_q, (((1,), (1,)), ((), ())), preferred_element_type=jnp.int32)
            return acc.astype(jnp.float32) * x_scale * weight_scale[None, :]
        orig_shape = x.shape
        x2d = x.reshape(-1, orig_shape[-1])
        out = _xla_quantized_matmul(x2d, weight_q, weight_scale)
        out = out.reshape(*orig_shape[:-1], out.shape[-1])
        out = out + bias
        return out
    x = x + _L0_attn_ref(_L0_cond_ref(x, cond_512, L0_cond_k_aff_w, L0_cond_k_aff_b, L0_cond_k_w, L0_cond_k_b, L0_cond_o_aff_w, L0_cond_o_aff_b, L0_cond_o_w, L0_cond_o_b), L0_attn_w_qkv, L0_attn_b_qkv, L0_attn_w1_write, L0_attn_w2_write, L0_attn_w1_read, L0_attn_w2_read, L0_attn_w_out, L0_attn_b_out, L0_attn_decay_logits, L0_attn_bias_scale)
    x = x + _L0_ffn_ref(_L0_cond2_ref(x, itok_BxS_0_999, itok_BxS_0_4, itok_BxS_0_4, mask_BxS_ik0, cond_512, cond_64, fside_Bx32_0, L0_cond2_pw_g, L0_cond2_pw_b, L0_cond2_cp_g, L0_cond2_cp_b, L0_cond2_tm_g, L0_cond2_tm_b, L0_cond2_ms_g, L0_cond2_ms_b, L0_cond2_mem_W1, L0_cond2_mem_b1, L0_cond2_mem_W2, L0_cond2_mem_b2, L0_cond2_mem_g, L0_cond2_mem_be, L0_cond2_noi_W1, L0_cond2_noi_b1, L0_cond2_noi_W2, L0_cond2_noi_b2, L0_cond2_noi_g, L0_cond2_noi_be, L0_cond2_res_W1, L0_cond2_res_b1, L0_cond2_res_W2, L0_cond2_res_b2, L0_cond2_res_g, L0_cond2_res_be, L0_cond2_int_W1, L0_cond2_int_b1, L0_cond2_int_W2, L0_cond2_int_b2, L0_cond2_int_g, L0_cond2_int_be, L0_cond2_aw), L0_ffn_Wr, L0_ffn_br, L0_ffn_W1, L0_ffn_b1, L0_ffn_W2, L0_ffn_b2)
    x = x + _L1_attn_ref(_L1_cond_ref(x, cond_512, L1_cond_down_project, L1_cond_down_gamma, L1_cond_down_beta, L1_cond_up_project, L1_cond_up_gamma, L1_cond_up_beta), L1_attn_Wq, L1_attn_bq, L1_attn_Wk, L1_attn_bk, L1_attn_Wv, L1_attn_bv, L1_attn_Wo, L1_attn_bo, L1_attn_orf)
    x = x + _L1_ffn_ref(_L1_cond2_ref(x, cond_512, L1_cond2_W_dec, L1_cond2_b_dec, L1_cond2_V), L1_ffn_weight_q, L1_ffn_weight_scale, L1_ffn_bias)
    return x

_drawn_inputs = setup_inputs


def setup_inputs(seed=0):
    import zlib

    import numpy as np

    out = dict(_drawn_inputs(seed))
    spreads = {'L0_cond_k_aff_b': (1.0, 0.2),
     'L0_cond_k_b': (0.0, 0.1),
     'L0_cond_o_aff_b': (1.0, 0.2),
     'L0_cond_o_b': (0.0, 0.1),
     'L0_attn_b_qkv': (0.0, 0.1),
     'L0_attn_b_out': (0.0, 0.1),
     'L0_attn_decay_logits': (4.599999904632568, 0.2),
     'L0_attn_bias_scale': (0.10000000149011612, 0.2),
     'L0_cond2_mem_b1': (0.0, 0.1),
     'L0_cond2_mem_b2': (0.0, 0.1),
     'L0_cond2_mem_be': (0.0, 0.1),
     'L0_cond2_noi_b1': (0.0, 0.1),
     'L0_cond2_noi_b2': (0.0, 0.1),
     'L0_cond2_noi_be': (0.0, 0.1),
     'L0_cond2_res_b1': (0.0, 0.1),
     'L0_cond2_res_b2': (0.0, 0.1),
     'L0_cond2_res_be': (0.0, 0.1),
     'L0_cond2_int_b1': (0.0, 0.1),
     'L0_cond2_int_b2': (0.0, 0.1),
     'L0_cond2_int_be': (0.0, 0.1),
     'L0_cond2_aw': (0.1666666716337204, 0.2),
     'L0_ffn_br': (0.0, 0.1),
     'L0_ffn_b1': (0.0, 0.1),
     'L0_ffn_b2': (0.0, 0.1),
     'L1_cond_down_beta': (0.0, 0.1),
     'L1_cond_up_beta': (0.0, 0.1)}
    factors = {}
    for name, (base, spread) in spreads.items():
        noise = np.random.default_rng([zlib.crc32(name.encode()), seed]).standard_normal(out[name].shape)
        drawn = base * np.exp(spread * noise) if base else spread * noise
        out[name] = jnp.asarray(drawn.astype(out[name].dtype))
    for name, factor in factors.items():
        out[name] = (out[name] * factor).astype(out[name].dtype)
    return out
```

```python
from contextlib import ExitStack

import numpy as np

import concourse.bass as bass
from concourse import mybir

F32 = mybir.dt.float32
BF16 = mybir.dt.bfloat16
I32 = mybir.dt.int32
I8 = mybir.dt.int8
U32 = mybir.dt.uint32
ALU = mybir.AluOpType
ACT = mybir.ActivationFunctionType
X = mybir.AxisListType.X

P = 128
B, S, D = 8, 512, 256
T = S // P
K2 = D // P
H, DH = 16, 16
HG = 4
E, CAP, HID = 8, 80, 1024
SLOTS = E * CAP
ROWS = B * CAP
ST = ROWS // P
KH = HID // P
M = 64
LN_EPS = 1e-5
MASKED = -1.0e30
ROUND = 12582912.0
NOFF = 6
KR = 30

ROWS0 = [("kb", D), ("bqk", 2 * D), ("bv", D), ("bout", D), ("b2", D), ("g", D), ("be", D),
         ("br", E), ("aw", 6), ("dl", H), ("bs", H)]
ROWS1 = [("bv", D), ("bo", D), ("ws", D), ("bias", D)]


def offsets(fields):
    out, at = {}, 0
    for name, n in fields:
        out[name] = (at, at + n)
        at += n
    return out, at


def spread(ap, at, n, step=0):
    dims = [list(d) for d in ap.ap]
    dims.insert(at, [step, n])
    return bass.AP(ap.tensor, ap.offset, dims)


def program(nc, a, out, scratch_kind="Internal", parts="ABC"):
    R0, n0 = offsets(ROWS0)
    R1, n1 = offsets(ROWS1)
    x1_d = nc.dram_tensor("x1_d", [B, P, T, D], F32, kind=scratch_kind).ap()
    gate_d = nc.dram_tensor("gate_d", [B, P, 4 * T], F32, kind=scratch_kind).ap()
    buf_d = nc.dram_tensor("buf_d", [E, P, K2, B, CAP], F32, kind=scratch_kind).ap()
    y_d = nc.dram_tensor("y_d", [E * ROWS, D], F32, kind=scratch_kind).ap()
    prow_d = nc.dram_tensor("prow_d", [B, 2 * D + 2 * M + 2 * D], F32, kind=scratch_kind).ap()
    wdec_d = nc.dram_tensor("wdec_d", [B, P, K2, D], F32, kind=scratch_kind).ap()
    PR = {"demk": (0, D), "dg": (D, D + M), "db": (D + M, D + 2 * M), "ug": (D + 2 * M, 2 * D + 2 * M),
          "ub": (2 * D + 2 * M, 3 * D + 2 * M), "bias": (3 * D + 2 * M, 4 * D + 2 * M)}

    top = ExitStack()
    with top:
        def sb_in(ctx, name, shape, dt=F32):
            return ctx.enter_context(nc.sbuf_tensor(name, shape, dt))

        bank = [top.enter_context(nc.psum_tensor(f"bank{i}", [P, 512], F32)) for i in range(8)]

        ident = sb_in(top, "ident", [P, P])
        pcol = sb_in(top, "pcol", [P, B, 8])
        eps_ln = sb_in(top, "eps_ln", [P, 2])

        class Sems:

            def __init__(self, ctx, prefix):
                self.ctx, self.prefix, self.by = ctx, prefix, {}

            def __call__(self, name):
                if name not in self.by:
                    self.by[name] = self.ctx.enter_context(nc.semaphore(f"{self.prefix}_{name}"))
                return self.by[name]

            def clear(self):
                nums = [s.num for s in self.by.values()]
                nc.all_engine_barrier(sems_to_clear=range(min(nums), max(nums) + 1))

        def chain_of(eng, sem):
            n = [0]

            def done(ins):
                n[0] += 1
                ins.then_inc(sem, 1)
                return n[0]

            def settle():
                eng.wait_ge(sem, n[0])

            return done, settle

        if True:
            l0 = ExitStack()
            with l0:
                sb = lambda name, shape, dt=F32: sb_in(l0, name, shape, dt)
                kow = sb("kow", [P, 2, K2, D])
                wqk = sb("wqk", [P, K2, 2 * D])
                wvl = sb("wvl", [P, K2, 2 * D])
                wout = sb("wout", [P, K2, D])
                wint = sb("wint", [P, 4 * K2, D])
                wint2 = sb("wint2", [P, K2, D])
                wr = sb("wr", [P, K2, E])
                rows = sb("rows", [P, n0])
                obcol = sb("obcol", [P, K2])
                tri = sb("tri", [P, P])
                ones = sb("ones", [P, P])
                negb = sb("negb", [P, P], BF16)
                identb = sb("identb", [P, P], BF16)
                iota = sb("iota", [P, SLOTS])
                wdiag = sb("wdiag", [P, H, P])
                facr = sb("facr", [P, H])
                facw = sb("facw", [P, H])
                fack = sb("fack", [P, HG, 4])
                sign = sb("sign", [P, 2 * H, NOFF])
                row = lambda f: rows[:, R0[f][0]:R0[f][1]]

                st = ExitStack()
                with st:
                    sbt = lambda name, shape, dt=F32: sb_in(st, name, shape, dt)
                    cond = sbt("cond", [P, 3, B])
                    affw = sbt("affw", [P, 2, K2, P])
                    affb = sbt("affb", [P, 2, K2])
                    w1all = sbt("w1all", [P, 6 * K2, D])
                    m1 = sbt("m1", [P, 3, D])
                    m2 = sbt("m2", [P, 3, K2, D])
                    mrow = sbt("mrow", [B, 3, 4, D])
                    ib1 = sbt("ib1", [P, K2])
                    cst = sbt("cst", [P, 8])
                    posd = sbt("posd", [P, P])
                    low = sbt("low", [P, P])
                    dlr = sbt("dlr", [P, H + HG])
                    lnd = sbt("lnd", [P, H + HG])
                    tmp = sbt("tmp", [P, H + HG])
                    tmp2 = sbt("tmp2", [P, H + HG])
                    aws = sbt("aws", [P, 6])
                    awr = sbt("awr", [P, 4])
                    style2 = sbt("style2", [P, 2, K2, B])
                    kow2 = sbt("kow2", [P, 2, K2, D])
                    drow = sbt("drow", [B, D])
                    dco = sbt("dco", [P, K2, B])
                    g1 = sbt("g1", [B, 3, D])
                    g1t = sbt("g1t", [P, 3, K2, B])
                    g2 = sbt("g2", [B, 3, D])
                    g2t = sbt("g2t", [P, 3, K2, B])
                    mstat = sbt("mstat", [B, 3, 6])
                    mmv = sbt("mmv", [B, 3, 4])
                    dgu = sbt("dgu", [P, 2 * M + 2 * D])
                    dguo = sbt("dguo", [B, 2 * M + 2 * D])
                    wdc = sbt("wdc", [P, KR, D + 1])
                    bdc = sbt("bdc", [P, K2, KR])
                    bdl = sbt("bdl", [KR, 1])
                    vv = sbt("vv", [KR, D])
                    uu = sbt("uu", [P, K2, B, KR])
                    ul = sbt("ul", [KR, B])
                    ut = sbt("ut", [KR, 2, P])
                    wde = sbt("wde", [P, 2, D])
                    brow = sbt("brow", [B, D])
                    sctx = ExitStack()
                    with sctx:
                        s = Sems(sctx, "s0")
                        with nc.Block() as block:
                            @block.sync
                            def _(sp):
                                for dst, name in ((cond, "cond"), (affw, "affw"), (affb, "affb"), (kow, "kow"),
                                                  (dlr, "dlr"), (cst, "cst"), (ident, "ident")):
                                    sp.dma_start(dst[:], a[name]).then_inc(s("load1"), 16)
                                sp.dma_start(rows[:], spread(a["rows0"], 0, P)).then_inc(s("load1"), 16)
                                for dst, name in ((posd, "posd"), (low, "low"), (w1all, "w1all"), (m1, "m1"), (m2, "m2"),
                                                  (ib1, "ib1"), (wqk, "wqk")):
                                    sp.dma_start(dst[:], a[name]).then_inc(s("load2"), 16)
                                sp.dma_start(mrow[:], spread(a["mrow"], 0, B)).then_inc(s("load2"), 16)
                                for dst, name in ((dgu, "dgu"), (wdc, "wdc"), (bdc, "bdc"), (bdl, "bdl"), (vv, "vv")):
                                    sp.dma_start(dst[:], a[name]).then_inc(s("load3"), 16)
                                for dst, name in ((wvl, "wvl"), (wout, "wout"), (wint2, "wint2"), (wr, "wr"),
                                                  (obcol, "obcol"), (tri, "tri"), (negb, "negb"), (identb, "identb")):
                                    sp.dma_start(dst[:], a[name]).then_inc(s("load4"), 16)
                                sp.dma_start(iota[:], spread(a["iota"], 0, P)).then_inc(s("load4"), 16)
                                sp.dma_start(sign[:], spread(a["sign"], 0, P)).then_inc(s("load4"), 16)
                                sp.wait_ge(s("drow_ok"), 1)
                                sp.dma_start(prow_d[:, 0:D], drow[:]).then_inc(s("stored"), 16)
                                sp.wait_ge(s("dguo_ok"), 1)
                                sp.dma_start(prow_d[:, D:3 * D + 2 * M], dguo[:]).then_inc(s("stored"), 16)
                                sp.wait_ge(s("brow_ok"), 1)
                                sp.dma_start(prow_d[:, 3 * D + 2 * M:], brow[:]).then_inc(s("stored"), 16)
                                for n in range(B * K2):
                                    sp.wait_ge(s("wde_ok"), n + 1)
                                    sp.dma_start(wdec_d[n // K2, :, n % K2, :], wde[:, n % 2, :]).then_inc(s(f"wstored{n % 2}"), 16)
                                sp.wait_ge(s("stored"), 48)
                                sp.wait_ge(s("wstored0"), 8 * B * K2)
                                sp.wait_ge(s("wstored1"), 8 * B * K2)
                                sp.wait_ge(s("load4"), 160)
                                sp.wait_ge(s("load1"), 128)
                                sp.wait_ge(s("load2"), 128)
                                sp.wait_ge(s("load3"), 80)

                            @block.gpsimd
                            def _(pool):
                                pool.memset(ones[:], 1.0).then_inc(s("ones_ok"), 1)
                                pool.memset(eps_ln[:, 0:1], LN_EPS).then_inc(s("ones_ok"), 1)
                                pool.memset(eps_ln[:, 1:2], 1e-8).then_inc(s("ones_ok"), 1)

                            @block.tensor
                            def _(pe):
                                pe.wait_ge(s("load1"), 128)
                                for w in range(2):
                                    for m in range(K2):
                                        mm = pe.matmul(bank[0][:, (w * K2 + m) * B:(w * K2 + m + 1) * B], affw[:, w, m, :],
                                                       cond[:, 0, :], start=True, stop=True)
                                mm.then_inc(s("style_mm"), 1)
                                pe.wait_ge(s("sq_ok"), 2)
                                for m in range(K2):
                                    mm = pe.matmul(bank[1][0:B, 0:D], style2[:, 0, m, :], kow2[:, 0, m, :],
                                                   start=(m == 0), stop=(m == K2 - 1))
                                mm.then_inc(s("dem_mm"), 1)
                                for o in range(K2):
                                    for m in range(K2):
                                        mm = pe.matmul(bank[2][:, o * B:(o + 1) * B], kow2[:, 1, m, o * P:(o + 1) * P],
                                                       style2[:, 1, m, :], start=(m == 0), stop=(m == K2 - 1))
                                mm.then_inc(s("dem_mm"), 1)
                                pe.wait_ge(s("load2"), 128)
                                for j, k in enumerate((P, 64, 32)):
                                    mm = pe.matmul(bank[3 + j][0:B, 0:D], cond[0:k, j, :], m1[0:k, j, :], start=True, stop=True)
                                    mm.then_inc(s("m1_mm"), 1)
                                pe.wait_ge(s("g1_ok"), 1)
                                for j in range(3):
                                    for m in range(K2):
                                        mm = pe.transpose(bank[6][:, (j * K2 + m) * B:(j * K2 + m + 1) * B],
                                                          g1[:, j, m * P:(m + 1) * P], ident[0:B, 0:B])
                                mm.then_inc(s("g1t_mm"), 1)
                                pe.wait_ge(s("g1t_ok"), 1)
                                for j in range(3):
                                    for m in range(K2):
                                        mm = pe.matmul(bank[3 + j][0:B, 0:D], g1t[:, j, m, :], m2[:, j, m, :],
                                                       start=(m == 0), stop=(m == K2 - 1))
                                mm.then_inc(s("m2_mm"), 1)
                                pe.wait_ge(s("g2_ok"), 1)
                                for j in range(3):
                                    for m in range(K2):
                                        mm = pe.transpose(bank[6][:, (j * K2 + m) * B:(j * K2 + m + 1) * B],
                                                          g2[:, j, m * P:(m + 1) * P], ident[0:B, 0:B])
                                mm.then_inc(s("g2t_mm"), 1)
                                pe.wait_ge(s("g2t_ok"), 1)
                                for o in range(K2):
                                    for n in range(3 * K2):
                                        j, m = n // K2, n % K2
                                        mm = pe.matmul(bank[7][:, o * B:(o + 1) * B],
                                                       w1all[:, (2 + j) * K2 + m, o * P:(o + 1) * P], g2t[:, j, m, :],
                                                       start=(n == 0), stop=(n == 3 * K2 - 1))
                                mm.then_inc(s("cvec_mm"), 1)
                                pe.wait_ge(s("load3"), 80)
                                hw = M + D
                                for n in range(2):
                                    mm = pe.matmul(bank[3 + n][0:B, 0:hw], cond[:, 0, :], dgu[:, n * hw:(n + 1) * hw],
                                                   start=True, stop=True)
                                mm.then_inc(s("dgu_mm"), 1)
                                for m in range(K2):
                                    for k in range(KR):
                                        mm = pe.matmul(bank[m][:, k * B:(k + 1) * B], wdc[:, k, m * P:(m + 1) * P],
                                                       cond[:, 0, :], start=True, stop=True)
                                mm = pe.matmul(bank[2][0:KR, 0:B], wdc[:, :, D], cond[:, 0, :], start=True, stop=True)
                                mm.then_inc(s("u_mm"), 1)
                                pe.wait_ge(s("u_ok"), 1)
                                pe.matmul(bank[5][0:B, 0:D], ul[:, :], vv[:, :], start=True, stop=True).then_inc(s("brow_mm"), 1)
                                for n in range(B * K2):
                                    if n >= 2:
                                        pe.wait_ge(s("ut_ok"), n - 1)
                                    pe.transpose(bank[n % 2][0:KR, 0:P], uu[:, n % K2, n // K2, :], ident[:, :]).then_inc(s("ut_mm"), 1)
                                    pe.wait_ge(s("ut_ok"), n + 1)
                                    if n >= 2:
                                        pe.wait_ge(s("wde_ok"), n - 1)
                                    pe.matmul(bank[6 + n % 2][:, 0:D], ut[:, n % 2, :], vv[:, :], start=True, stop=True)\
                                        .then_inc(s("wde_mm"), 1)

                            @block.scalar
                            def _(act):
                                done, settle = chain_of(act, s("act_own"))
                                act.wait_ge(s("ones_ok"), 3)
                                act.wait_ge(s("load1"), 128)
                                act.activation(kow2[:], kow[:], ACT.Square).then_inc(s("sq_ok"), 1)
                                act.wait_ge(s("absx"), 1)
                                act.activation(tmp[:], tmp[:], ACT.Exp, scale=-1.0).then_inc(s("expx"), 1)
                                act.wait_ge(s("awsub"), 1)
                                done(act.activation(aws[:], aws[:], ACT.Exp, accum_out=awr[:, 0:1]))
                                settle()
                                act.activation(tmp2[:], tmp[:], ACT.Ln, bias=1.0).then_inc(s("lnx"), 1)
                                act.wait_ge(s("lnd_ok"), 1)
                                act.wait_ge(s("load2"), 128)
                                for h in range(H):
                                    act.activation(wdiag[:, h, :], posd[:], ACT.Exp, scale=lnd[:, h:h + 1])
                                act.activation(facr[:], lnd[:, 0:H], ACT.Exp, scale=cst[:, 0:1])
                                act.activation(facw[:], lnd[:, 0:H], ACT.Exp, scale=cst[:, 1:2])
                                for v in range(3):
                                    last = act.activation(fack[:, :, v], lnd[:, H:H + HG], ACT.Exp, scale=float(P * v))
                                last.then_inc(s("pow_ok"), 1)
                                act.wait_ge(s("dem_mm"), 2)
                                act.activation(drow[:], bank[1][0:B, 0:D], ACT.Sqrt, bias=eps_ln[0:B, 1:2])
                                act.activation(dco[:], bank[2][:, 0:K2 * B].rearrange("p (o b) -> p o b", b=B), ACT.Sqrt,
                                               bias=eps_ln[:, 1:2]).then_inc(s("dem_sq"), 1)
                                act.wait_ge(s("g1_pre"), 1)
                                act.activation(g1[:], g1[:], ACT.Silu).then_inc(s("g1_ok"), 1)
                                act.wait_ge(s("mvar"), 1)
                                act.activation(mmv[:, :, 2:3], mmv[:, :, 1:2], ACT.Sqrt, bias=eps_ln[0:B, 0:1]).then_inc(s("msd"), 1)
                                for n in range(B * K2):
                                    act.wait_ge(s("ut_mm"), n + 1)
                                    if n >= 2:
                                        act.wait_ge(s("wde_mm"), n - 1)
                                    act.copy(ut[:, n % 2, :], bank[n % 2][0:KR, 0:P]).then_inc(s("ut_ok"), 1)

                            @block.vector
                            def _(dve):
                                done, settle = chain_of(dve, s("dve_own"))
                                dve.wait_ge(s("load1"), 128)
                                dve.tensor_scalar(tmp2[:], dlr[:], -1.0, None, ALU.mult).then_inc(s("neg"), 1)
                                done(dve.tensor_reduce(awr[:, 1:2], row("aw"), X, ALU.max))
                                dve.wait_ge(s("neg"), 1)
                                dve.tensor_tensor(tmp[:], dlr[:], tmp2[:], ALU.max).then_inc(s("absx"), 1)
                                settle()
                                dve.tensor_scalar(aws[:], row("aw"), awr[:, 1:2], None, ALU.subtract).then_inc(s("awsub"), 1)
                                done(dve.tensor_scalar(lnd[:], dlr[:], 0.0, None, ALU.min))
                                dve.wait_ge(s("style_mm"), 1)
                                for w in range(2):
                                    for m in range(K2):
                                        n = w * K2 + m
                                        done(dve.tensor_scalar(pcol[:, :, n], bank[0][:, n * B:(n + 1) * B],
                                                               affb[:, w, m:m + 1], None, ALU.add))
                                settle()
                                sty = pcol[:, :, 0:4].rearrange("p b (w m) -> p w m b", w=2)
                                for w in range(2):
                                    last = dve.tensor_tensor(style2[:, w], sty[:, w], sty[:, w], ALU.mult)
                                last.then_inc(s("sq_ok"), 1)
                                dve.wait_ge(s("lnx"), 1)
                                dve.tensor_tensor(lnd[:], lnd[:], tmp2[:], ALU.subtract).then_inc(s("lnd_ok"), 1)
                                dve.wait_ge(s("dem_sq"), 1)
                                dve.reciprocal(drow[:], drow[:]).then_inc(s("drow_ok"), 1)
                                dve.reciprocal(pcol[:, :, 4:6].rearrange("p b o -> p o b"), dco[:])
                                done(dve.reciprocal(awr[:, 2:3], awr[:, 0:1]))
                                settle()
                                done(dve.tensor_scalar(aws[:], aws[:], awr[:, 2:3], None, ALU.mult))
                                settle()
                                dve.wait_ge(s("load2"), 128)
                                for j in range(2, 5):
                                    done(dve.tensor_scalar(w1all[:, K2 * j:K2 * j + K2, :], w1all[:, K2 * j:K2 * j + K2, :],
                                                           aws[:, j:j + 1], None, ALU.mult))
                                for at, j in ((2, 5), (4, 1), (6, 0)):
                                    done(dve.tensor_scalar(wint[:, at:at + K2, :], w1all[:, K2 * j:K2 * j + K2, :],
                                                           aws[:, j:j + 1], None, ALU.mult))
                                settle()
                                done(dve.tensor_tensor(wint[:, 0:K2, :], w1all[:, 4:6, :], w1all[:, 6:8, :], ALU.add))
                                settle()
                                done(dve.tensor_tensor(wint[:, 0:K2, :], wint[:, 0:K2, :], w1all[:, 8:10, :], ALU.add))
                                done(dve.tensor_scalar(wqk[:, :, 0:D], wqk[:, :, 0:D], 0.25, None, ALU.mult))
                                q0 = R0["bqk"][0]
                                done(dve.tensor_scalar(rows[:, q0:q0 + D], rows[:, q0:q0 + D], 0.25, None, ALU.mult))
                                dve.wait_ge(s("pow_ok"), 1)
                                done(dve.tensor_tensor(wdiag[:], wdiag[:], spread(low[:], 1, H), ALU.mult))
                                done(dve.tensor_tensor(facr[:], facr[:], row("bs"), ALU.mult))
                                done(dve.tensor_scalar(fack[:, :, 0:3], fack[:, :, 0:3], cst[:, 3:4], cst[:, 2:3], ALU.mult, ALU.add))
                                done(dve.tensor_copy(fack[:, :, 3], spread(cst[:, 4:5], 1, HG)[:, :, 0]))
                                dve.wait_ge(s("m1_mm"), 3)
                                for j in range(3):
                                    last = dve.tensor_tensor(g1[:, j, :], bank[3 + j][0:B, 0:D], mrow[:, j, 0, :], ALU.add)
                                last.then_inc(s("g1_pre"), 1)
                                dve.wait_ge(s("g1t_mm"), 1)
                                dve.tensor_copy(g1t[:].rearrange("p j m b -> p (j m b)"), bank[6][:, 0:3 * K2 * B]).then_inc(s("g1t_ok"), 1)
                                dve.wait_ge(s("m2_mm"), 1)
                                for j in range(3):
                                    done(dve.tensor_tensor(g2[:, j, :], bank[3 + j][0:B, 0:D], mrow[:, j, 1, :], ALU.add))
                                settle()
                                for j in range(3):
                                    done(dve.bn_stats(mstat[:, j, :], g2[:, j, :]))
                                settle()
                                for j in range(3):
                                    last = dve.bn_aggr(mmv[:, j, 0:2], mstat[:, j, :])
                                last.then_inc(s("mvar"), 1)
                                dve.wait_ge(s("msd"), 1)
                                done(dve.reciprocal(mmv[:, :, 3:4], mmv[:, :, 2:3]))
                                settle()
                                for j in range(3):
                                    done(dve.tensor_scalar(g2[:, j, :], g2[:, j, :], mmv[:, j, 0:1], mmv[:, j, 3:4],
                                                           ALU.subtract, ALU.mult))
                                settle()
                                done(dve.tensor_tensor(g2[:], g2[:], mrow[:, :, 2, :], ALU.mult))
                                settle()
                                dve.tensor_tensor(g2[:], g2[:], mrow[:, :, 3, :], ALU.add).then_inc(s("g2_ok"), 1)
                                dve.wait_ge(s("g2t_mm"), 1)
                                dve.tensor_copy(g2t[:].rearrange("p j m b -> p (j m b)"), bank[6][:, 0:3 * K2 * B]).then_inc(s("g2t_ok"), 1)
                                dve.wait_ge(s("cvec_mm"), 1)
                                for o in range(K2):
                                    dve.tensor_scalar(pcol[:, :, 6 + o], bank[7][:, o * B:(o + 1) * B], ib1[:, o:o + 1], None, ALU.add)
                                dve.wait_ge(s("dgu_mm"), 1)
                                hw = M + D
                                dve.tensor_copy(dguo[:, 0:hw], bank[3][0:B, 0:hw])
                                dve.tensor_copy(dguo[:, hw:2 * hw], bank[4][0:B, 0:hw]).then_inc(s("dguo_ok"), 1)
                                dve.wait_ge(s("u_mm"), 1)
                                for m in range(K2):
                                    dve.tensor_tensor(uu[:, m].rearrange("p b k -> p k b"),
                                                      bank[m][:, 0:KR * B].rearrange("p (k b) -> p k b", b=B),
                                                      spread(bdc[:, m, :], 2, B), ALU.add)
                                dve.tensor_scalar(ul[:], bank[2][0:KR, 0:B], bdl[:, 0:1], None, ALU.add).then_inc(s("u_ok"), 1)
                                dve.wait_ge(s("brow_mm"), 1)
                                dve.tensor_copy(brow[:], bank[5][0:B, 0:D]).then_inc(s("brow_ok"), 1)
                                for n in range(B * K2):
                                    dve.wait_ge(s("wde_mm"), n + 1)
                                    if n >= 2:
                                        dve.wait_ge(s(f"wstored{n % 2}"), 16 * (n // 2))
                                    dve.tensor_copy(wde[:, n % 2, :], bank[6 + n % 2][:, 0:D]).then_inc(s("wde_ok"), 1)
                        s.clear()

                xT = sb("xT", [P, K2, S])
                xN = sb("xN", [P, T, D])
                ids = sb("ids", [P, 3 * T], I32)
                demk = sb("demk", [P, D])
                pc = sb("pc", [P, 8])
                boff = sb("boff", [P, 1])
                wk = sb("wk", [P, K2, D])
                wo = sb("wo", [P, K2, D])
                cT = sb("cT", [P, K2, S + 1])
                aT = sb("aT", [P, K2, S])
                x1 = sb("x1", [P, T, D])
                nA = sb("nA", [P, T, D])
                nB = sb("nB", [P, T, D])
                stat = sb("stat", [P, T, 6])
                mv = sb("mv", [P, T, 4])

                def layer0_loop():
                    lctx = ExitStack()
                    with nc.Fori(0, B) as b, lctx:
                        s = Sems(lctx, "a")
                        p1 = ExitStack()
                        with p1:
                            kx = sb_in(p1, "kx", [P, T, 2 * D])
                            prod = sb_in(p1, "prod", [P, 9, D])
                            sc = sb_in(p1, "sc", [P, T, H, 2 * H])
                            ex = sb_in(p1, "ex", [P, T, H, H])
                            mx = sb_in(p1, "mx", [P, T, H])
                            rs = sb_in(p1, "rs", [P, T, H])
                            pv = sb_in(p1, "pv", [P, 2, H, D])
                            with nc.Block() as block:
                                @block.sync
                                def _(sp):
                                    sp.dma_start(xT[:], a["xT"][b]).then_inc(s("x_in"), 16)
                                    sp.dma_start(demk[:], spread(prow_d[b, 0:D], 0, P)).then_inc(s("x_in"), 16)
                                    sp.dma_start(xN[:], a["xN"][b]).then_inc(s("xn_in"), 16)
                                    sp.dma_start(ids[:], a["ids"][b]).then_inc(s("xn_in"), 16)
                                    sp.dma_start(boff[:], spread(a["boff"][b, :], 0, P)).then_inc(s("xn_in"), 16)
                                    sp.wait_ge(s("xn_in"), 48)

                                @block.tensor
                                def _(pe):
                                    pe.wait_ge(s("x_in"), 32)
                                    pe.wait_ge(s("wk_ok"), 1)
                                    for t in range(T):
                                        for m in range(K2):
                                            mm = pe.matmul(bank[t // 2][:, (t % 2) * D:(t % 2 + 1) * D],
                                                           xT[:, m, t * P:(t + 1) * P], wk[:, m, :],
                                                           start=(m == 0), stop=(m == K2 - 1))
                                    mm.then_inc(s("kx_mm"), 1)
                                    pe.wait_ge(s("on_ok"), 1)
                                    for m in range(K2):
                                        for t in range(T):
                                            mm = pe.transpose(bank[2 + m][:, t * P:(t + 1) * P], nA[:, t, m * P:(m + 1) * P], ident[:])
                                        mm.then_inc(s("aT_mm"), 1)
                                    pe.wait_ge(s("aT_ok"), 2)
                                    for o in range(K2):
                                        for m in range(K2):
                                            mm = pe.matmul(bank[4 + o][:], wo[:, m, o * P:(o + 1) * P], aT[:, m, :],
                                                           start=(m == 0), stop=(m == K2 - 1))
                                        mm.then_inc(s("c_mm"), 1)

                                @block.scalar
                                def _(act):
                                    done, settle = chain_of(act, s("act_own"))
                                    act.wait_ge(s("kx_half"), 1)
                                    act.copy(kx[:, :, D:2 * D], kx[:, :, 0:D]).then_inc(s("kx_dup"), 1)
                                    act.wait_ge(s("sc_low"), T)
                                    done(act.copy(sc[:, :, 1:8, H:2 * H], sc[:, :, 1:8, 0:H]))
                                    settle()
                                    for d in range(1, 8):
                                        last = act.copy(sc[:, :, H - d, 0:H], sc[:, :, d, H - d:2 * H - d])
                                    last.then_inc(s("sc_full"), 1)
                                    act.wait_ge(s("ex_in"), 1)
                                    act.activation(ex[:], ex[:], ACT.Exp, scale=0.25).then_inc(s("ex_ok"), 1)
                                    for m in range(K2):
                                        act.wait_ge(s("aT_mm"), m + 1)
                                        act.copy(aT[:, m, :], bank[2 + m][:]).then_inc(s("aT_ok"), 1)
                                    act.wait_ge(s("wk_ok"), 1)
                                    for o in range(K2):
                                        act.wait_ge(s("c_mm"), o + 1)
                                        act.activation(cT[:, o, 1:S + 1], bank[4 + o][:], ACT.Identity,
                                                       bias=obcol[:, o:o + 1], scale=pc[:, 4 + o:5 + o])

                                @block.gpsimd
                                def _(pool):
                                    pool.wait_ge(s("ex_ok"), 1)
                                    for t in range(T):
                                        if t >= 2:
                                            pool.wait_ge(s("pv_used"), t - 1)
                                        kv = kx[:, t, 0:D].rearrange("p (h d) -> p h d", d=DH)
                                        pool.tensor_tensor(pv[:, t % 2].rearrange("p o (h d) -> p o h d", d=DH),
                                                           spread(ex[:, t], 3, DH), spread(kv, 1, H, DH), ALU.mult)\
                                            .then_inc(s("pv_ok"), 1)

                                @block.vector
                                def _(dve):
                                    done, settle = chain_of(dve, s("dve_own"))
                                    done(dve.tensor_copy(pc[:], pcol[:, b, :]))
                                    settle()
                                    for m in range(K2):
                                        done(dve.tensor_scalar(wk[:, m, :], kow[:, 0, m, :], pc[:, m:m + 1], None, ALU.mult))
                                        dve.tensor_scalar(wo[:, m, :], kow[:, 1, m, :], pc[:, 2 + m:3 + m], None, ALU.mult)
                                    settle()
                                    dve.wait_ge(s("x_in"), 32)
                                    dve.tensor_tensor(wk[:], wk[:], spread(demk[:], 1, K2), ALU.mult).then_inc(s("wk_ok"), 1)
                                    dve.wait_ge(s("kx_mm"), 1)
                                    for c in range(2):
                                        last = dve.tensor_tensor(kx[:, 2 * c:2 * c + 2, 0:D],
                                                                 bank[c][:].rearrange("p (t f) -> p t f", t=2),
                                                                 spread(row("kb"), 1, 2), ALU.add)
                                    last.then_inc(s("kx_half"), 1)
                                    dve.wait_ge(s("kx_dup"), 1)
                                    for t in range(T):
                                        k0 = kx[:, t, 0:D]
                                        if t:
                                            dve.wait_ge(s("sc_low"), t)
                                        done(dve.tensor_tensor(prod[:], spread(k0, 1, 9), spread(k0, 1, 9, DH), ALU.mult))
                                        settle()
                                        dve.tensor_reduce(sc[:, t, 0:9, 0:H], prod[:].rearrange("p o (h d) -> p o h d", d=DH),
                                                          X, ALU.add).then_inc(s("sc_low"), 1)
                                    dve.wait_ge(s("sc_full"), 1)
                                    for t in range(T):
                                        done(dve.tensor_reduce(mx[:, t, :], sc[:, t, :, 0:H].rearrange("p o h -> p h o"), X, ALU.max))
                                    settle()
                                    for t in range(T):
                                        last = dve.tensor_tensor(ex[:, t], sc[:, t, :, 0:H], spread(mx[:, t, :], 1, H), ALU.subtract)
                                    last.then_inc(s("ex_in"), 1)
                                    dve.wait_ge(s("ex_ok"), 1)
                                    for t in range(T):
                                        done(dve.tensor_reduce(mx[:, t, :], ex[:, t].rearrange("p o h -> p h o"), X, ALU.add))
                                    settle()
                                    done(dve.reciprocal(rs[:], mx[:]))
                                    for t in range(T):
                                        dve.wait_ge(s("pv_ok"), t + 1)
                                        last = dve.tensor_reduce(nA[:, t, :], pv[:, t % 2].rearrange("p o f -> p f o"), X, ALU.add)
                                        last.then_inc(s("pv_used"), 1)
                                    settle()
                                    dve.wait_ge(s("pv_used"), T)
                                    nv = nA[:].rearrange("p t (h d) -> p (t h) d", d=DH)
                                    dve.tensor_tensor(nv, nv, spread(rs[:].rearrange("p t h -> p (t h)"), 2, DH), ALU.mult)\
                                        .then_inc(s("on_ok"), 1)

                        p2 = ExitStack()
                        with p2:
                            vn = sb_in(p2, "vn", [P, T, D])
                            vls = sb_in(p2, "vls", [P, T, 2 * D])
                            qk = sb_in(p2, "qk", [P, T, 2, H, 32])
                            la = sb_in(p2, "la", [P, T, 2 * H, NOFF])
                            lb = sb_in(p2, "lb", [P, T, 2 * H, NOFF])
                            ln = sb_in(p2, "ln", [P, T, 2 * H])
                            lf = sb_in(p2, "lf", [P, 4, T, H])
                            qT = sb_in(p2, "qT", [P, HG, S])
                            k0T = sb_in(p2, "k0T", [P, HG, S])
                            k1T = sb_in(p2, "k1T", [P, HG, 2 * P])
                            k2T = sb_in(p2, "k2T", [P, HG, P])
                            kiT = sb_in(p2, "kiT", [P, HG, S])
                            dbias = sb_in(p2, "dbias", [P, 2, T, P])
                            nmax = sb_in(p2, "nmax", [P, 4])
                            rsum = sb_in(p2, "rsum", [P, T, H])
                            rinv = sb_in(p2, "rinv", [P, T, H])
                            pr = sb_in(p2, "pr", [P, 3, S])
                            prT = sb_in(p2, "prT", [P, 3, S])
                            xb = sb_in(p2, "xb", [P, T, D])
                            units = [(h, i) for h in range(H) for i in range(T)]
                            with nc.Block() as block:
                                @block.sync
                                def _(sp):
                                    sp.wait_ge(s("x1_ok"), 1)
                                    sp.dma_start(x1_d[b], x1[:]).then_inc(s("x1_out"), 16)
                                    sp.wait_ge(s("x1_out"), 16)

                                @block.gpsimd
                                def _(pool):
                                    pool.memset(cT[:, :, 0:1], 0.0).then_inc(s("c0_ok"), 1)
                                    pool.memset(qk[:, :, :, :, 28:32], 0.0).then_inc(s("pad_ok"), 1)
                                    pool.tensor_tensor(xb[:], xN[:], spread(row("bout"), 1, T), ALU.add).then_inc(s("xb_ok"), 1)
                                    pool.wait_ge(s("vl_ok"), T)
                                    pool.tensor_tensor(vn[:], vls[:, :, 0:D], spread(row("bv"), 1, T), ALU.add).then_inc(s("v_ok"), 1)

                                @block.tensor
                                def _(pe):
                                    pe.wait_ge(s("c0_ok"), 1)
                                    for t in range(T):
                                        if t >= 2:
                                            pe.wait_ge(s("qk_ev"), t - 1)
                                            pe.wait_ge(s("vl_ok"), t - 1)
                                        bq, bl = bank[2 * (t % 2)], bank[2 * (t % 2) + 1]
                                        now = lambda m: cT[:, m, 1 + t * P:1 + (t + 1) * P]
                                        before = lambda m: cT[:, m, t * P:(t + 1) * P]
                                        for m in range(K2):
                                            pe.matmul(bq[:], now(m), wqk[:, m, :], start=(m == 0), stop=(m == K2 - 1))
                                        for lo, hi, at in ((0, 320, now), (320, 384, before), (384, 512, now)):
                                            for m in range(K2):
                                                mm = pe.matmul(bl[:, lo:hi], at(m), wvl[:, m, lo:hi],
                                                               start=(m == 0), stop=(m == K2 - 1))
                                        mm.then_inc(s("proj_mm"), 1)
                                    pe.wait_ge(s("qk_ok"), 1)
                                    pe.wait_ge(s("pad_ok"), 1)
                                    for g in range(HG):
                                        for side in range(2):
                                            n = 2 * g + side
                                            if n >= 4:
                                                pe.wait_ge(s("qkT_ok"), n - 3)
                                            for t in range(T):
                                                src = qk[:, t, side, HG * g:HG * g + HG, :].rearrange("p h r -> p (h r)")
                                                mm = pe.transpose(bank[4 + n % 4][:, t * P:(t + 1) * P], src, ident[:])
                                            mm.then_inc(s("qkT_mm"), 1)
                                    pe.wait_ge(s("qkT_ok"), 8)
                                    pe.wait_ge(s("v_ok"), 1)

                                    def score(u):
                                        h, i = units[u]
                                        g, r = h // HG, 32 * (h % HG)
                                        if i == 0:
                                            if h >= 2:
                                                pe.wait_ge(s("dbias_ok"), h - 1)
                                            for j in range(T):
                                                mm = pe.matmul(bank[2 + h % 2][:, j * P:(j + 1) * P], qT[r:r + 32, g, j * P:(j + 1) * P],
                                                               kiT[r:r + 32, g, j * P:(j + 1) * P], start=True, stop=True)
                                            mm.then_inc(s("inc_mm"), 1)
                                        if u >= 2:
                                            pe.wait_ge(s("exp_ok"), u - 1)
                                        lg = bank[u % 2]
                                        q = lambda n: qT[r:r + n, g, i * P:(i + 1) * P]
                                        for j in range(i):
                                            kk = (k0T, k1T, k2T)[i - 1 - j]
                                            pe.matmul(lg[:, j * P:(j + 1) * P], q(32), kk[r:r + 32, g, j * P:(j + 1) * P],
                                                      start=True, stop=True)
                                        pe.matmul(lg[:, i * P:(i + 1) * P], q(DH), k0T[r:r + DH, g, i * P:(i + 1) * P],
                                                  start=True, stop=False)
                                        pe.matmul(lg[:, i * P:(i + 1) * P], identb[:], negb[:], start=False, stop=True)\
                                            .then_inc(s("score_mm"), 1)

                                    def turn(u):
                                        h, i = units[u]
                                        pe.wait_ge(s("exp_ok"), u + 1)
                                        if u >= 2:
                                            pe.wait_ge(s("prT_ok"), u - 1)
                                        for j in range(i + 1):
                                            mm = pe.transpose(bank[4 + u % 2][:, j * P:(j + 1) * P], pr[:, u % 3, j * P:(j + 1) * P], ident[:])
                                        mm.then_inc(s("turn_mm"), 1)

                                    def values(u):
                                        h, i = units[u]
                                        pe.wait_ge(s("prT_ok"), u + 1)
                                        o = bank[6 + i // 2][:, (i % 2) * D + h * DH:(i % 2) * D + (h + 1) * DH]
                                        for j in range(i + 1):
                                            mm = pe.matmul(o, prT[:, u % 3, j * P:(j + 1) * P], vn[:, j, h * DH:(h + 1) * DH],
                                                           start=(j == 0), stop=(j == i))
                                        mm.then_inc(s("val_mm"), 1)

                                    N = len(units)
                                    score(0)
                                    score(1)
                                    for u in range(N):
                                        turn(u)
                                        if u + 2 < N:
                                            score(u + 2)
                                        if u >= 1:
                                            values(u - 1)
                                    values(N - 1)
                                    pe.wait_ge(s("att_ok"), 1)
                                    for m in range(K2):
                                        for t in range(T):
                                            mm = pe.transpose(bank[m][:, t * P:(t + 1) * P], nA[:, t, m * P:(m + 1) * P], ident[:])
                                        mm.then_inc(s("oT_mm"), 1)
                                    pe.wait_ge(s("oT_ok"), 2)
                                    for t in range(T):
                                        for m in range(K2):
                                            mm = pe.matmul(bank[2 + t // 2][:, (t % 2) * D:(t % 2 + 1) * D], aT[:, m, t * P:(t + 1) * P],
                                                           wout[:, m, :], start=(m == 0), stop=(m == K2 - 1))
                                    mm.then_inc(s("out_mm"), 1)

                                @block.scalar
                                def _(act):
                                    for t in range(T):
                                        act.wait_ge(s("proj_mm"), t + 1)
                                        act.copy(vls[:, t, :], bank[2 * (t % 2) + 1][:]).then_inc(s("vl_ok"), 1)
                                    act.wait_ge(s("len2"), 1)
                                    act.activation(ln[:], ln[:], ACT.Sqrt).then_inc(s("len_ok"), 1)
                                    for g in range(HG):
                                        act.wait_ge(s("qkT_mm"), 2 * g + 1)
                                        act.copy(qT[:, g, :], bank[4 + (2 * g) % 4][:]).then_inc(s("qkT_ok"), 1)
                                        act.wait_ge(s("qkT_mm"), 2 * g + 2)
                                        src = bank[4 + (2 * g + 1) % 4]
                                        act.activation(k0T[:, g, :], src[:], ACT.Copy, scale=fack[:, g, 0:1])
                                        act.activation(k1T[:, g, :], src[:, 0:2 * P], ACT.Copy, scale=fack[:, g, 1:2])
                                        act.activation(k2T[:, g, :], src[:, 0:P], ACT.Copy, scale=fack[:, g, 2:3])
                                        act.activation(kiT[:, g, :], src[:], ACT.Copy, scale=fack[:, g, 3:4]).then_inc(s("qkT_ok"), 1)

                                    def exps(u):
                                        h, i = units[u]
                                        n = (i + 1) * P
                                        act.wait_ge(s("max_ok"), u + 1)
                                        if u >= 3:
                                            act.wait_ge(s("turn_mm"), u - 2)
                                        act.activation(pr[:, u % 3, 0:n], bank[u % 2][:, 0:n], ACT.Exp, bias=nmax[:, u % 4:u % 4 + 1],
                                                       accum_out=rsum[:, i, h:h + 1]).then_inc(s("exp_ok"), 1)

                                    def turned(u):
                                        n = (units[u][1] + 1) * P
                                        act.wait_ge(s("turn_mm"), u + 1)
                                        if u >= 3:
                                            act.wait_ge(s("val_mm"), u - 2)
                                        act.copy(prT[:, u % 3, 0:n], bank[4 + u % 2][:, 0:n]).then_inc(s("prT_ok"), 1)

                                    N = len(units)
                                    exps(0)
                                    for u in range(N):
                                        if u + 1 < N:
                                            exps(u + 1)
                                        turned(u)
                                    for m in range(K2):
                                        act.wait_ge(s("oT_mm"), m + 1)
                                        act.copy(aT[:, m, :], bank[m][:]).then_inc(s("oT_ok"), 1)

                                @block.vector
                                def _(dve):
                                    done, settle = chain_of(dve, s("dve_own2"))
                                    for t in range(T):
                                        dve.wait_ge(s("proj_mm"), t + 1)
                                        dve.tensor_tensor(qk[:, t, :, :, 0:DH].rearrange("p s h d -> p (s h) d"),
                                                          bank[2 * (t % 2)][:].rearrange("p (s d) -> p s d", d=DH),
                                                          row("bqk").rearrange("p (s d) -> p s d", d=DH), ALU.add)\
                                            .then_inc(s("qk_ev"), 1)
                                    dve.wait_ge(s("vl_ok"), T)
                                    pa = vls[:, :, D:D + P].rearrange("p t (s c) -> p t s c", c=4)
                                    pb = vls[:, :, D + P:D + 2 * P].rearrange("p t (s c) -> p t s c", c=4)
                                    for dst, u, v in ((la, pa, pb), (lb, pb, pa)):
                                        for c, lo, n in ((0, 0, 3), (1, 3, 2), (2, 5, 1)):
                                            uc = u[:, :, :, c]
                                            uc = spread(uc, 3, n)
                                            done(dve.tensor_tensor(dst[:, :, :, lo:lo + n], uc, v[:, :, :, c + 1:4], ALU.mult))
                                    settle()
                                    done(dve.tensor_tensor(la[:], la[:], lb[:], ALU.subtract))
                                    settle()
                                    done(dve.tensor_tensor(lb[:], la[:], la[:], ALU.mult))
                                    settle()
                                    dve.tensor_reduce(ln[:], lb[:], X, ALU.add).then_inc(s("len2"), 1)
                                    done(dve.tensor_tensor(la[:], la[:], spread(sign[:], 1, T), ALU.mult))
                                    dve.wait_ge(s("len_ok"), 1)
                                    done(dve.tensor_scalar(ln[:], ln[:], 1e-12, None, ALU.max))
                                    settle()
                                    done(dve.reciprocal(ln[:], ln[:]))
                                    settle()
                                    done(dve.tensor_tensor(lf[:, 0], ln[:, :, 0:H], spread(facr[:], 1, T), ALU.mult))
                                    done(dve.tensor_tensor(lf[:, 1], ln[:, :, 0:H], spread(row("bs"), 1, T), ALU.mult))
                                    done(dve.tensor_tensor(lf[:, 2], ln[:, :, H:2 * H], spread(facw[:], 1, T), ALU.mult))
                                    done(dve.tensor_copy(lf[:, 3], ln[:, :, H:2 * H]))
                                    settle()
                                    for n in range(4):
                                        side, at = n // 2, DH + NOFF * (n % 2)
                                        src = la[:, :, H * side:H * side + H, :]
                                        if side:
                                            src = src[:, :, :, ::-1]
                                        for t in range(T):
                                            last = dve.tensor_tensor(qk[:, t, side, :, at:at + NOFF], src[:, t],
                                                                     spread(lf[:, n, t, :], 2, NOFF), ALU.mult)
                                    last.then_inc(s("qk_ok"), 1)
                                    for u, (h, i) in enumerate(units):
                                        if i == 0:
                                            dve.wait_ge(s("inc_mm"), h + 1)
                                            dve.tensor_tensor(dbias[:, h % 2], bank[2 + h % 2][:].rearrange("p (i k) -> p i k", k=P),
                                                              spread(wdiag[:, h, :], 1, T), ALU.mult).then_inc(s("dbias_ok"), 1)
                                            dve.wait_ge(s("dbias_ok"), h + 1)
                                        dve.wait_ge(s("score_mm"), u + 1)
                                        dg = bank[u % 2][:, i * P:(i + 1) * P]
                                        done(dve.tensor_tensor(dg, dg, dbias[:, h % 2, i, :], ALU.add))
                                        settle()
                                        if u >= 4:
                                            dve.wait_ge(s("exp_ok"), u - 3)
                                        dve.tensor_reduce(nmax[:, u % 4:u % 4 + 1], bank[u % 2][:, 0:(i + 1) * P], X, ALU.max,
                                                          negate=True).then_inc(s("max_ok"), 1)
                                    dve.wait_ge(s("exp_ok"), len(units))
                                    done(dve.reciprocal(rinv[:], rsum[:]))
                                    settle()
                                    dve.wait_ge(s("val_mm"), len(units))
                                    for c in range(2):
                                        last = dve.tensor_tensor(nA[:, 2 * c:2 * c + 2, :].rearrange("p t (h d) -> p (t h) d", d=DH),
                                                                 bank[6 + c][:].rearrange("p (h d) -> p h d", d=DH),
                                                                 spread(rinv[:, 2 * c:2 * c + 2, :].rearrange("p t h -> p (t h)"), 2, DH),
                                                                 ALU.mult)
                                    last.then_inc(s("att_ok"), 1)
                                    dve.wait_ge(s("out_mm"), 1)
                                    dve.wait_ge(s("xb_ok"), 1)
                                    for c in range(2):
                                        last = dve.tensor_tensor(x1[:, 2 * c:2 * c + 2, :], bank[2 + c][:].rearrange("p (t f) -> p t f", t=2),
                                                                 xb[:, 2 * c:2 * c + 2, :], ALU.add)
                                    last.then_inc(s("x1_ok"), 1)

                        p3 = ExitStack()
                        with p3:
                            ga = sb_in(p3, "ga", [P, T, 2 * D])
                            gb = sb_in(p3, "gb", [P, T, 4 * D])
                            gc = sb_in(p3, "gc", [P, T, 2 * D])
                            tt = sb_in(p3, "tt", [P, T, D])
                            ss = sb_in(p3, "ss", [P, T, D])
                            cat = sb_in(p3, "cat", [P, 8, S])
                            hT = sb_in(p3, "hT", [P, K2, S])
                            pe8 = sb_in(p3, "pe8", [P, 8, T, E])
                            sm = sb_in(p3, "sm", [P, 16, T])
                            gi = sb_in(p3, "gi", [P, 4, T])
                            disp = sb_in(p3, "disp", [P, T, SLOTS])
                            bfT = sb_in(p3, "bfT", [P, K2, SLOTS])
                            with nc.Block() as block:
                                @block.sync
                                def _(sp):
                                    sp.wait_ge(s("gi_ok"), 1)
                                    sp.dma_start(gate_d[b], gi[:].rearrange("p k t -> p (k t)")).then_inc(s("p3_out"), 16)
                                    for m in range(K2):
                                        sp.wait_ge(s("bf_ok"), 2 * m + 2)
                                        sp.dma_start(buf_d[:, :, m, b, :].rearrange("e p c -> p e c"),
                                                     bfT[:, m, :].rearrange("p (e c) -> p e c", c=CAP)).then_inc(s("p3_out"), 16)
                                    sp.wait_ge(s("p3_out"), 48)

                                @block.gpsimd
                                def _(pool):
                                    for src, dst, k in ((a["pw"], ga, 0), (a["cptm"], gb, 1), (a["ms"], gc, 2)):
                                        for t in range(T):
                                            if k:
                                                pool.wait_ge(s(f"gath{t}"), 16 * k)
                                            pool.indirect_dma_start(
                                                out=dst[:, t, :], out_offset=None, in_=src,
                                                in_offset=bass.IndirectOffsetOnAxis(ap=ids[:, k * T + t:k * T + t + 1].bitcast(U32), axis=0))\
                                                .then_inc(s(f"gath{t}"), 16)
                                    for t in range(T):
                                        pool.wait_ge(s(f"gath{t}"), 48)
                                    pool.wait_ge(s("z_ok"), T)
                                    pool.tensor_tensor(tt[:], nA[:], gb[:, :, 2 * D:3 * D], ALU.mult).then_inc(s("pool_own"), 1)
                                    pool.tensor_tensor(ss[:], nA[:], gc[:, :, 0:D], ALU.mult).then_inc(s("pool_own"), 1)
                                    pool.wait_ge(s("pool_own"), 2)
                                    pool.tensor_tensor(tt[:], tt[:], gb[:, :, 3 * D:4 * D], ALU.add).then_inc(s("tt_ok"), 1)
                                    pool.tensor_tensor(ss[:], ss[:], gc[:, :, D:2 * D], ALU.add).then_inc(s("ss_ok"), 1)
                                    for t in range(T):
                                        pool.dma_reset(range(s(f"gath{t}").num, s(f"gath{t}").num + 1))

                                @block.tensor
                                def _(pe):
                                    for n, (src, ready) in enumerate(((x1, None), (tt, "tt_ok"), (ss, "ss_ok"), (nB, "h_ok"))):
                                        if ready:
                                            pe.wait_ge(s(ready), 1)
                                        for m in range(K2):
                                            for t in range(T):
                                                mm = pe.transpose(bank[2 * n + m][:, t * P:(t + 1) * P], src[:, t, m * P:(m + 1) * P], ident[:])
                                            mm.then_inc(s("cat_mm"), 1)
                                    pe.wait_ge(s("cat_ok"), 8)
                                    order = (0, 1, 4, 5, 2, 3, 6, 7)
                                    for o in range(K2):
                                        for n in range(8):
                                            mm = pe.matmul(bank[o][:], wint[:, order[n], o * P:(o + 1) * P], cat[:, n, :],
                                                           start=(n == 0), stop=(n == 7))
                                        mm.then_inc(s("u_mm"), 1)
                                    pe.wait_ge(s("u_ok"), 2)
                                    for t in range(T):
                                        for m in range(K2):
                                            mm = pe.matmul(bank[2 + t // 2][:, (t % 2) * D:(t % 2 + 1) * D], aT[:, m, t * P:(t + 1) * P],
                                                           wint2[:, m, :], start=(m == 0), stop=(m == K2 - 1))
                                    mm.then_inc(s("y_mm"), 1)
                                    pe.wait_ge(s("f_ok"), 1)
                                    for m in range(K2):
                                        for t in range(T):
                                            mm = pe.transpose(bank[4 + m][:, t * P:(t + 1) * P], nB[:, t, m * P:(m + 1) * P], ident[:])
                                        mm.then_inc(s("fT_mm"), 1)
                                    pe.wait_ge(s("fT_ok"), 2)
                                    for t in range(T):
                                        for m in range(K2):
                                            mm = pe.matmul(bank[6][:, t * E:(t + 1) * E], hT[:, m, t * P:(t + 1) * P], wr[:, m, :],
                                                           start=(m == 0), stop=(m == K2 - 1))
                                    mm.then_inc(s("r_mm"), 1)
                                    pe.wait_ge(s("pick_ok"), 1)
                                    for t in range(T):
                                        for j in range(t + 1):
                                            mm = pe.matmul(bank[7][:, t * E:(t + 1) * E], (tri if j == t else ones)[:], pe8[:, 5, j, :],
                                                           start=(j == 0), stop=(j == t))
                                    mm.then_inc(s("pos_mm"), 1)
                                    pe.wait_ge(s("disp_ok"), T)
                                    for m in range(K2):
                                        for c in range(2):
                                            w = SLOTS // 2
                                            for t in range(T):
                                                mm = pe.matmul(bank[2 * m + c][:, 0:w], nB[:, t, m * P:(m + 1) * P],
                                                               disp[:, t, c * w:(c + 1) * w], start=(t == 0), stop=(t == T - 1))
                                            mm.then_inc(s("bf_mm"), 1)

                                @block.scalar
                                def _(act):
                                    act.wait_ge(s("var1"), 1)
                                    act.activation(mv[:, :, 2:3], mv[:, :, 1:2], ACT.Sqrt, bias=eps_ln[:, 0:1]).then_inc(s("sd1"), 1)
                                    act.wait_ge(s("var2"), 1)
                                    act.activation(mv[:, :, 2:3], mv[:, :, 1:2], ACT.Sqrt, bias=eps_ln[:, 0:1]).then_inc(s("sd2"), 1)
                                    for n in range(8):
                                        act.wait_ge(s("cat_mm"), n + 1)
                                        act.copy(cat[:, n, :], bank[n][:]).then_inc(s("cat_ok"), 1)
                                    for o in range(K2):
                                        act.wait_ge(s("u_mm"), o + 1)
                                        act.activation(aT[:, o, :], bank[o][:], ACT.Silu, bias=pc[:, 6 + o:7 + o]).then_inc(s("u_ok"), 1)
                                    act.wait_ge(s("var3"), 1)
                                    act.activation(mv[:, :, 2:3], mv[:, :, 1:2], ACT.Sqrt, bias=eps_ln[:, 0:1]).then_inc(s("sd3"), 1)
                                    for m in range(K2):
                                        act.wait_ge(s("fT_mm"), m + 1)
                                        act.copy(hT[:, m, :], bank[4 + m][:]).then_inc(s("fT_ok"), 1)
                                    act.wait_ge(s("re_in"), 1)
                                    act.activation(pe8[:, 0], pe8[:, 0], ACT.Exp).then_inc(s("re_ok"), 1)
                                    for n in range(4):
                                        act.wait_ge(s("bf_mm"), n + 1)
                                        w = SLOTS // 2
                                        act.copy(bfT[:, n // 2, (n % 2) * w:(n % 2 + 1) * w], bank[n][:, 0:w]).then_inc(s("bf_ok"), 1)

                                @block.vector
                                def _(dve):
                                    done, settle = chain_of(dve, s("dve_own3"))

                                    def moments(src, var):
                                        for t in range(T):
                                            done(dve.bn_stats(stat[:, t, :], src[:, t, :]))
                                        settle()
                                        for t in range(T):
                                            last = dve.bn_aggr(mv[:, t, 0:2], stat[:, t, :])
                                        last.then_inc(s(var), 1)

                                    def normed(dst, src, sd, ready=None):
                                        dve.wait_ge(s(sd), 1)
                                        done(dve.reciprocal(mv[:, :, 3:4], mv[:, :, 2:3]))
                                        settle()
                                        for t in range(T):
                                            ins = dve.tensor_scalar(dst[:, t, :], src[:, t, :], mv[:, t, 0:1], mv[:, t, 3:4],
                                                                    ALU.subtract, ALU.mult)
                                            ins.then_inc(s(ready), 1) if ready else done(ins)
                                        if ready:
                                            dve.wait_ge(s(ready), T)
                                        else:
                                            settle()

                                    def affine(dst, src, gain, off, ready=None):
                                        done(dve.tensor_tensor(dst[:], src, gain, ALU.mult))
                                        settle()
                                        ins = dve.tensor_tensor(dst[:], dst[:], off, ALU.add)
                                        ins.then_inc(s(ready), 1) if ready else done(ins)
                                        if not ready:
                                            settle()

                                    moments(x1, "var1")
                                    normed(nA, x1, "sd1", "z_ok")
                                    for t in range(T):
                                        dve.wait_ge(s(f"gath{t}"), 16)
                                    affine(nB, nA[:], ga[:, :, 0:D], ga[:, :, D:2 * D])
                                    moments(nB, "var2")
                                    normed(nB, nB, "sd2")
                                    for t in range(T):
                                        dve.wait_ge(s(f"gath{t}"), 32)
                                    affine(nB, nB[:], gb[:, :, 0:D], gb[:, :, D:2 * D], "h_ok")
                                    dve.wait_ge(s("y_mm"), 1)
                                    for c in range(2):
                                        done(dve.tensor_tensor(nB[:, 2 * c:2 * c + 2, :], bank[2 + c][:].rearrange("p (t f) -> p t f", t=2),
                                                               spread(row("b2"), 1, 2), ALU.add))
                                    settle()
                                    moments(nB, "var3")
                                    normed(nB, nB, "sd3")
                                    affine(nB, nB[:], spread(row("g"), 1, T), spread(row("be"), 1, T), "f_ok")
                                    q = lambda k: pe8[:, k]
                                    step = lambda ins: (done(ins), settle())
                                    dve.wait_ge(s("r_mm"), 1)
                                    step(dve.tensor_tensor(q(0), bank[6][:, 0:T * E].rearrange("p (t e) -> p t e", e=E),
                                                           spread(row("br"), 1, T), ALU.add))
                                    step(dve.tensor_reduce(sm[:, 0], q(0), X, ALU.max))
                                    dve.tensor_tensor(q(0), q(0), spread(sm[:, 0], 2, E), ALU.subtract).then_inc(s("re_in"), 1)
                                    dve.wait_ge(s("re_ok"), 1)
                                    step(dve.tensor_reduce(sm[:, 1], q(0), X, ALU.add))
                                    step(dve.reciprocal(sm[:, 1], sm[:, 1]))
                                    step(dve.tensor_tensor(q(0), q(0), spread(sm[:, 1], 2, E), ALU.mult))
                                    io = spread(iota[:, 0:E], 1, T)
                                    for k in range(2):
                                        pk, mk, ix, oh = q(0 if k == 0 else 3), sm[:, 2 + k], sm[:, 4 + k], q(1 + k)
                                        step(dve.tensor_reduce(mk, pk, X, ALU.max))
                                        step(dve.tensor_tensor(q(4), pk, spread(mk, 2, E), ALU.is_ge))
                                        step(dve.tensor_scalar(q(4), q(4), -float(E), float(E), ALU.mult, ALU.add))
                                        step(dve.tensor_tensor(q(4), q(4), io, ALU.add))
                                        step(dve.tensor_reduce(ix, q(4), X, ALU.min))
                                        step(dve.tensor_tensor(oh, io, spread(ix, 2, E), ALU.is_equal))
                                        if k == 0:
                                            step(dve.tensor_scalar(q(4), oh, -2.0, None, ALU.mult))
                                            step(dve.tensor_tensor(q(3), pk, q(4), ALU.add))
                                    dve.tensor_tensor(q(5), q(1), q(2), ALU.add).then_inc(s("pick_ok"), 1)
                                    dve.wait_ge(s("pos_mm"), 1)
                                    step(dve.tensor_copy(q(6), bank[7][:, 0:T * E].rearrange("p (t e) -> p t e", e=E)))
                                    for k in range(2):
                                        at, keep, slot = sm[:, 6 + k], sm[:, 8 + k], sm[:, 10 + k]
                                        step(dve.tensor_tensor(q(7), q(6), q(1 + k), ALU.mult))
                                        step(dve.tensor_reduce(at, q(7), X, ALU.add))
                                        step(dve.tensor_scalar(keep, at, float(CAP), None, ALU.is_lt))
                                        step(dve.tensor_scalar(at, at, float(CAP - 1), None, ALU.min))
                                        step(dve.tensor_scalar(slot, sm[:, 4 + k], float(CAP), 1.0, ALU.mult, ALU.add))
                                        step(dve.tensor_tensor(slot, slot, at, ALU.add))
                                        step(dve.tensor_tensor(slot, slot, keep, ALU.mult))
                                        step(dve.tensor_scalar(slot, slot, -1.0, None, ALU.add))
                                        done(dve.tensor_tensor(gi[:, k], sm[:, 2 + k], keep, ALU.mult))
                                        step(dve.tensor_scalar(sm[:, 12], sm[:, 4 + k], float(ROWS), boff[:, 0:1], ALU.mult, ALU.add))
                                        last = dve.tensor_tensor(gi[:, 2 + k], sm[:, 12], at, ALU.add)
                                        if k == 0:
                                            step(last)
                                        else:
                                            last.then_inc(s("gi_ok"), 1)
                                    for t in range(T):
                                        step(dve.tensor_scalar(disp[:, t, :], iota[:], sm[:, 10, t:t + 1], None, ALU.is_equal))
                                        dve.scalar_tensor_tensor(disp[:, t, :], iota[:], sm[:, 11, t:t + 1], disp[:, t, :],
                                                                 ALU.is_equal, ALU.add).then_inc(s("disp_ok"), 1)
                        s.clear()

                if "A" in parts:
                    layer0_loop()

        def expert_loop():
            ctx = ExitStack()
            with ctx:
                sb = lambda name, shape, dt=F32: sb_in(ctx, name, shape, dt)
                ew1 = sb("ew1", [P, 2, K2, HID])
                ew2 = sb("ew2", [P, 2, KH, D])
                eb1 = sb("eb1", [P, 2, KH])
                eb2 = sb("eb2", [P, 2, D])
                eb = sb("eb", [P, 2, K2, ROWS])
                hid = sb("hid", [P, KH, ROWS])
                yy = sb("yy", [P, 2, ST, D])
                W = ROWS // 2
                with nc.Fori(0, E // 2) as e2:
                    sctx = ExitStack()
                    with sctx:
                        s = Sems(sctx, "e")
                        with nc.Block() as block:
                            @block.sync
                            def _(sp):
                                for k in range(2):
                                    for dst, src in ((ew1[:, k], a["eW1"][2 * e2 + k]), (eb[:, k].rearrange("p m r -> p (m r)"),
                                                     buf_d[2 * e2 + k].rearrange("p m b c -> p (m b c)")),
                                                     (eb1[:, k], a["eb1"][2 * e2 + k]), (ew2[:, k], a["eW2"][2 * e2 + k]),
                                                     (eb2[:, k], spread(a["eb2"][2 * e2 + k, :], 0, P))):
                                        sp.dma_start(dst, src).then_inc(s(f"w_in{k}"), 16)
                                for k in range(2):
                                    sp.wait_ge(s("y_ok"), ST * (k + 1))
                                    sp.dma_start(y_d.rearrange("(e t p) d -> e p t d", p=P, t=ST)[2 * e2 + k], yy[:, k]).then_inc(s("y_out"), 16)
                                sp.wait_ge(s("y_out"), 32)

                            @block.tensor
                            def _(pe):
                                for k in range(2):
                                    pe.wait_ge(s(f"w_in{k}"), 80)
                                    for n in range(2 * KH):
                                        o, c = n // 2, n % 2
                                        if k * 2 * KH + n >= 4:
                                            pe.wait_ge(s("h_ok"), k * 2 * KH + n - 3)
                                        for m in range(K2):
                                            mm = pe.matmul(bank[n % 4][:, 0:W], ew1[:, k, m, o * P:(o + 1) * P],
                                                           eb[:, k, m, c * W:(c + 1) * W], start=(m == 0), stop=(m == K2 - 1))
                                        mm.then_inc(s("h_mm"), 1)
                                    pe.wait_ge(s("h_ok"), 2 * KH * (k + 1))
                                    for t in range(ST):
                                        n = k * ST + t
                                        if n >= 4:
                                            pe.wait_ge(s("y_ok"), n - 3)
                                        for m in range(KH):
                                            mm = pe.matmul(bank[4 + n % 4][:, 0:D], hid[:, m, t * P:(t + 1) * P], ew2[:, k, m, :],
                                                           start=(m == 0), stop=(m == KH - 1))
                                        mm.then_inc(s("y_mm"), 1)

                            @block.scalar
                            def _(act):
                                for k in range(2):
                                    act.wait_ge(s(f"w_in{k}"), 80)
                                    if k:
                                        act.wait_ge(s("y_mm"), ST * k)
                                    for n in range(2 * KH):
                                        act.wait_ge(s("h_mm"), k * 2 * KH + n + 1)
                                        act.activation(hid[:, n // 2, (n % 2) * W:(n % 2 + 1) * W], bank[n % 4][:, 0:W], ACT.Relu,
                                                       bias=eb1[:, k, n // 2:n // 2 + 1]).then_inc(s("h_ok"), 1)

                            @block.vector
                            def _(dve):
                                for k in range(2):
                                    dve.wait_ge(s(f"w_in{k}"), 80)
                                    for t in range(ST):
                                        n = k * ST + t
                                        dve.wait_ge(s("y_mm"), n + 1)
                                        dve.tensor_tensor(yy[:, k, t, :], bank[4 + n % 4][:, 0:D], eb2[:, k, :], ALU.add)\
                                            .then_inc(s("y_ok"), 1)
                        s.clear()

        if "B" in parts:
            expert_loop()
        if "C" in parts:
            layer1(nc, a, out, bank, ident, sb_in, Sems, chain_of, x1_d, gate_d, y_d, prow_d, wdec_d, PR, R1, n1)


def layer1(nc, a, out, bank, ident, sb_in, Sems, chain_of, x1_d, gate_d, y_d, prow_d, wdec_d, PR, R1, n1):
    NP = H // 2
    V1 = DH + 1
    l1 = ExitStack()
    with l1:
        sb = lambda name, shape, dt=F32: sb_in(l1, name, shape, dt)
        dup = sb("dup", [P, K2, M])
        upp = sb("upp", [M, D])
        wqkv = sb("wqkv", [P, 3, K2, D])
        wo1 = sb("wo1", [P, K2, D])
        qkcol = sb("qkcol", [P, 2, K2])
        orfk = sb("orfk", [P, 2 * 256])
        nrmk = sb("nrmk", [P, 8])
        nrmq = sb("nrmq", [P, P])
        wq8 = sb("wq8", [P, K2, D // 4], I32)
        wqb = sb("wqb", [P, K2, D], BF16)
        rows = sb("rows1", [P, n1])
        identb = sb("identb1", [P, P], BF16)
        row = lambda f: rows[:, R1[f][0]:R1[f][1]]
        sctx = ExitStack()
        with sctx:
            s = Sems(sctx, "s1")
            with nc.Block() as block:
                @block.sync
                def _(sp):
                    loads = [(dup, "dup"), (upp, "upp"), (wqkv, "wqkv"), (wo1, "wo1"), (qkcol, "qkcol"), (orfk, "orfk"),
                             (nrmk, "nrmk"), (nrmq, "nrmq"), (identb, "identb"), (wq8, "wq8")]
                    for dst, name in loads:
                        sp.dma_start(dst[:], a[name]).then_inc(s("load"), 16)
                    sp.dma_start(rows[:], spread(a["rows1"], 0, P)).then_inc(s("load"), 16)
                    sp.wait_ge(s("load"), 16 * (len(loads) + 1))

                @block.vector
                def _(dve):
                    dve.wait_ge(s("load"), 16 * 11)
                    dve.tensor_copy(wqb[:], wq8[:].bitcast(I8)).then_inc(s("w_ok"), 1)
                    dve.tensor_scalar(orfk[:], orfk[:], 0.5, None, ALU.mult).then_inc(s("w_ok"), 1)
            s.clear()

        x2 = sb("x2", [P, T, D])
        gi = sb("gi1", [P, 4, T])
        gidx = sb("gidx", [P, 2, T], I32)
        yg = sb("yg", [P, 2, T, D])
        dgb = sb("dgb", [P, 2, M])
        ugb = sb("ugb", [M, 2, D])
        brow = sb("brow1", [P, D])
        wdn = sb("wdn", [P, K2, M])
        wup = sb("wup", [M, D])
        wde = sb("wde1", [P, K2, D])
        xT = sb("xT1", [P, K2, S])
        dT = sb("dT1", [M, S])
        hcT = sb("hcT", [P, K2, S])
        qT = sb("qT1", [P, K2, S])
        kT = sb("kT1", [P, K2, S])
        q2 = sb("q2", [P, K2, S])
        k2 = sb("k2", [P, K2, S])
        vn = sb("vn1", [P, T, H, V1])
        kn = sb("kn", [P, T, 2, 8])
        kf = sb("kf", [P, T, H, M])
        qf = sb("qf", [P, NP, S])
        kv = sb("kv", [P, NP, 2 * V1])
        den = sb("den", [P, T, H])
        on = sb("on", [P, T, D])
        xb = sb("xb1", [P, T, D])
        x3 = sb("x3", [P, T, D])
        ab = sb("ab", [P, 3, T])
        yq = sb("yq", [P, T, D])
        yb = sb("yb", [P, T, D], BF16)
        qbT = sb("qbT", [P, K2, S], BF16)
        fo = sb("fo", [P, T, D])

        def transposes(pe, src, banks, s, name):
            for m in range(K2):
                for t in range(T):
                    mm = pe.transpose(bank[banks[m]][:, t * P:(t + 1) * P], src[:, t, m * P:(m + 1) * P], ident[:])
                mm.then_inc(s(name), 1)

        with nc.Fori(0, B) as b:
            sctx = ExitStack()
            with sctx:
                s = Sems(sctx, "c")
                with nc.Block() as block:
                    @block.sync
                    def _(sp):
                        sp.dma_start(gi[:].rearrange("p k t -> p (k t)"), gate_d[b]).then_inc(s("gi_in"), 16)
                        sp.dma_start(x2[:], x1_d[b]).then_inc(s("x_in"), 16)
                        sp.dma_start(dgb[:].rearrange("p k h -> p (k h)"), spread(prow_d[b, PR["dg"][0]:PR["db"][1]], 0, P)).then_inc(s("p_in"), 16)
                        sp.dma_start(ugb[:].rearrange("p k h -> p (k h)"), spread(prow_d[b, PR["ug"][0]:PR["ub"][1]], 0, M)).then_inc(s("p_in"), 16)
                        sp.dma_start(brow[:], spread(prow_d[b, PR["bias"][0]:PR["bias"][1]], 0, P)).then_inc(s("p_in"), 16)
                        sp.dma_start(wde[:], wdec_d[b]).then_inc(s("p_in"), 16)
                        sp.wait_ge(s("fin"), 1)
                        sp.dma_start(out[b].rearrange("(t p) d -> p t d", p=P), fo[:]).then_inc(s("out"), 16)
                        sp.wait_ge(s("out"), 16)

                    @block.gpsimd
                    def _(pool):
                        pool.wait_ge(s("idx_ok"), 1)
                        for k in range(2):
                            for t in range(T):
                                pool.indirect_dma_start(out=yg[:, k, t, :], out_offset=None, in_=y_d,
                                                        in_offset=bass.IndirectOffsetOnAxis(ap=gidx[:, k, t:t + 1].bitcast(U32), axis=0))\
                                    .then_inc(s(f"y_in{k}{t}"), 16)
                        pool.memset(vn[:, :, :, DH:V1], 1.0).then_inc(s("one_ok"), 1)
                        pool.memset(kv[:], 0.0).then_inc(s("kv0"), 1)
                        pool.wait_ge(s("x2_ok"), 1)
                        pool.tensor_tensor(xb[:], x2[:], spread(row("bo"), 1, T), ALU.add).then_inc(s("xb_ok"), 1)
                        for n in range(8):
                            pool.wait_ge(s("kf_in"), n + 1)
                            pool.tensor_scalar(kf[:, n // 2, 8 * (n % 2):8 * (n % 2) + 8, :], kf[:, n // 2, 8 * (n % 2):8 * (n % 2) + 8, :],
                                               1e-6, None, ALU.add).then_inc(s("kf_ok"), 1)
                        for n in range(NP):
                            pool.wait_ge(s("qf_in"), n + 1)
                            pool.tensor_scalar(qf[:, n, :], qf[:, n, :], 1e-6, None, ALU.add).then_inc(s("qf_ok"), 1)
                        for k in range(2):
                            for t in range(T):
                                pool.wait_ge(s(f"y_in{k}{t}"), 16)
                                pool.dma_reset(range(s(f"y_in{k}{t}").num, s(f"y_in{k}{t}").num + 1))
                        pool.wait_ge(s("x3_ok"), 1)
                        pool.tensor_tensor(xb[:], x3[:], spread(row("bias"), 1, T), ALU.add).then_inc(s("x3b_ok"), 1)

                    @block.tensor
                    def _(pe):
                        pe.wait_ge(s("x2_ok"), 1)
                        transposes(pe, x2, (0, 1), s, "xT_mm")
                        pe.wait_ge(s("xT_ok"), 2)
                        pe.wait_ge(s("wud_ok"), 1)
                        for m in range(K2):
                            mm = pe.matmul(bank[2][0:M, :], wdn[:, m, :], xT[:, m, :], start=(m == 0), stop=(m == K2 - 1))
                        mm.then_inc(s("dn_mm"), 1)
                        pe.wait_ge(s("dn_ok"), 1)
                        for m in range(K2):
                            pe.matmul(bank[3 + m][:], wup[:, m * P:(m + 1) * P], dT[:], start=True, stop=True).then_inc(s("up_mm"), 1)
                        pe.wait_ge(s("hc_ok"), 2)
                        for n in range(4):
                            w, o = 1 - n // 2, n % 2
                            for m in range(K2):
                                mm = pe.matmul(bank[(5, 6, 7, 0)[n]][:], wqkv[:, w, m, o * P:(o + 1) * P], hcT[:, m, :],
                                               start=(m == 0), stop=(m == K2 - 1))
                            mm.then_inc(s("qk_mm"), 1)
                        for t in range(T):
                            for m in range(K2):
                                mm = pe.matmul(bank[1 + t // 2][:, (t % 2) * D:(t % 2 + 1) * D], hcT[:, m, t * P:(t + 1) * P],
                                               wqkv[:, 2, m, :], start=(m == 0), stop=(m == K2 - 1))
                        mm.then_inc(s("v_mm"), 1)
                        pe.wait_ge(s("sq_ok"), 2)
                        for t in range(T):
                            for m in range(K2):
                                mm = pe.matmul(bank[3][:, (2 * t + m) * 8:(2 * t + m + 1) * 8], k2[:, m, t * P:(t + 1) * P], nrmk[:],
                                               start=True, stop=True)
                        mm.then_inc(s("kn_mm"), 1)
                        for n in range(8):
                            t, m = n // 2, n % 2
                            if n >= 2:
                                pe.wait_ge(s("kf_sub"), n - 1)
                            pe.matmul(bank[4 + n % 2][:], kT[:, m, t * P:(t + 1) * P], orfk[:], start=True, stop=True)\
                                .then_inc(s("kf_mm"), 1)
                        pe.wait_ge(s("sq_ok"), 4)
                        for n in range(NP):
                            m, r = n // 4, 32 * (n % 4)
                            bk = (6, 7, 0)[n % 3]
                            if n >= 3:
                                pe.wait_ge(s("qf_in"), n - 2)
                            pe.matmul(bank[bk][:], orfk[r:r + 32, (n % 4) * P:(n % 4 + 1) * P], qT[r:r + 32, m, :], start=True, stop=False)
                            pe.matmul(bank[bk][:], nrmq[r:r + 32, :], q2[r:r + 32, m, :], start=False, stop=True).then_inc(s("qf_mm"), 1)
                        pe.wait_ge(s("kf_ok"), 8)
                        pe.wait_ge(s("v_ok"), 1)
                        for n in range(NP):
                            for t in range(T):
                                mm = pe.matmul(bank[1][:, n * 2 * V1:(n + 1) * 2 * V1], kf[:, t, 2 * n:2 * n + 2, :].rearrange("p h m -> p (h m)"),
                                               vn[:, t, 2 * n:2 * n + 2, :].rearrange("p h d -> p (h d)"), start=(t == 0), stop=(t == T - 1))
                        mm.then_inc(s("kv_mm"), 1)
                        pe.wait_ge(s("kv_ok"), 1)
                        pe.wait_ge(s("qf_ok"), NP)
                        for t in range(T):
                            for n in range(NP):
                                mm = pe.matmul(bank[2 + t][:, n * 2 * V1:(n + 1) * 2 * V1], qf[:, n, t * P:(t + 1) * P], kv[:, n, :],
                                               start=True, stop=True)
                            mm.then_inc(s("o_mm"), 1)
                        pe.wait_ge(s("on_ok"), T)
                        transposes(pe, on, (6, 7), s, "oT_mm")
                        pe.wait_ge(s("oT_ok"), 2)
                        for t in range(T):
                            for m in range(K2):
                                mm = pe.matmul(bank[t // 2][:, (t % 2) * D:(t % 2 + 1) * D], xT[:, m, t * P:(t + 1) * P], wo1[:, m, :],
                                               start=(m == 0), stop=(m == K2 - 1))
                        mm.then_inc(s("wo_mm"), 1)
                        pe.wait_ge(s("x3_ok"), 1)
                        transposes(pe, x3, (2, 3), s, "x3T_mm")
                        pe.wait_ge(s("x3T_ok"), 2)
                        for t in range(T):
                            for m in range(K2):
                                mm = pe.matmul(bank[4 + t // 2][:, (t % 2) * D:(t % 2 + 1) * D], hcT[:, m, t * P:(t + 1) * P], wde[:, m, :],
                                               start=(m == 0), stop=(m == K2 - 1))
                        mm.then_inc(s("yq_mm"), 1)
                        pe.wait_ge(s("yb_ok"), 1)
                        for m in range(K2):
                            bb = bank[6 + m][:].bitcast(BF16)
                            for t in range(T):
                                mm = pe.transpose(bb[:, t * P:(t + 1) * P], yb[:, t, m * P:(m + 1) * P], identb[:])
                            mm.then_inc(s("qbT_mm"), 1)
                        pe.wait_ge(s("qbT_ok"), 2)
                        for t in range(T):
                            for m in range(K2):
                                mm = pe.matmul(bank[t // 2][:, (t % 2) * D:(t % 2 + 1) * D], qbT[:, m, t * P:(t + 1) * P], wqb[:, m, :],
                                               start=(m == 0), stop=(m == K2 - 1))
                        mm.then_inc(s("acc_mm"), 1)

                    @block.scalar
                    def _(act):
                        for m in range(K2):
                            act.wait_ge(s("xT_mm"), m + 1)
                            act.copy(xT[:, m, :], bank[m][:]).then_inc(s("xT_ok"), 1)
                        act.wait_ge(s("dn_mm"), 1)
                        act.activation(dT[:], bank[2][0:M, :], ACT.Relu).then_inc(s("dn_ok"), 1)
                        for n in range(4):
                            w, o = 1 - n // 2, n % 2
                            src = bank[(5, 6, 7, 0)[n]][:]
                            dst, sq = ((qT, q2), (kT, k2))[w]
                            act.wait_ge(s("qk_mm"), n + 1)
                            act.activation(dst[:, o, :], src, ACT.Identity, bias=qkcol[:, w, o:o + 1])
                            act.activation(sq[:, o, :], src, ACT.Square, bias=qkcol[:, w, o:o + 1]).then_inc(s("sq_ok"), 1)
                        for n in range(8):
                            v = kf[:, n // 2, 8 * (n % 2):8 * (n % 2) + 8, :]
                            act.wait_ge(s("kf_sub"), n + 1)
                            act.activation(v, v, ACT.Exp).then_inc(s("kf_in"), 1)
                        for n in range(NP):
                            act.wait_ge(s("qf_mm"), n + 1)
                            act.activation(qf[:, n, :], bank[(6, 7, 0)[n % 3]][:], ACT.Exp).then_inc(s("qf_in"), 1)
                        for m in range(K2):
                            act.wait_ge(s("oT_mm"), m + 1)
                            act.copy(xT[:, m, :], bank[6 + m][:]).then_inc(s("oT_ok"), 1)
                        for m in range(K2):
                            act.wait_ge(s("x3T_mm"), m + 1)
                            act.copy(hcT[:, m, :], bank[2 + m][:]).then_inc(s("x3T_ok"), 1)
                        for m in range(K2):
                            act.wait_ge(s("qbT_mm"), m + 1)
                            act.copy(qbT[:, m, :], bank[6 + m][:].bitcast(BF16)[:, 0:S]).then_inc(s("qbT_ok"), 1)

                    @block.vector
                    def _(dve):
                        done, settle = chain_of(dve, s("dve_own"))
                        dve.wait_ge(s("gi_in"), 16)
                        dve.tensor_copy(gidx[:], gi[:, 2:4, :]).then_inc(s("idx_ok"), 1)
                        dve.wait_ge(s("p_in"), 64)
                        done(dve.tensor_tensor(wdn[:], dup[:], spread(dgb[:, 0, :], 1, K2), ALU.mult))
                        done(dve.tensor_tensor(wup[:], upp[:], ugb[:, 0, :], ALU.mult))
                        settle()
                        dve.tensor_tensor(wdn[:], wdn[:], spread(dgb[:, 1, :], 1, K2), ALU.add)
                        dve.tensor_tensor(wup[:], wup[:], ugb[:, 1, :], ALU.add).then_inc(s("wud_ok"), 1)
                        dve.wait_ge(s("x_in"), 16)
                        for k in range(2):
                            if k:
                                settle()
                            for t in range(T):
                                dve.wait_ge(s(f"y_in{k}{t}"), 16)
                                ins = dve.scalar_tensor_tensor(x2[:, t, :], yg[:, k, t, :], gi[:, k, t:t + 1], x2[:, t, :], ALU.mult, ALU.add)
                                if k == 0:
                                    done(ins)
                        ins.then_inc(s("x2_ok"), 1)
                        for m in range(K2):
                            dve.wait_ge(s("up_mm"), m + 1)
                            dve.wait_ge(s("xT_ok"), 2)
                            dve.tensor_tensor(hcT[:, m, :], bank[3 + m][:], xT[:, m, :], ALU.add).then_inc(s("hc_ok"), 1)
                        dve.wait_ge(s("v_mm"), 1)
                        dve.wait_ge(s("one_ok"), 1)
                        for c in range(2):
                            last = dve.tensor_tensor(vn[:, 2 * c:2 * c + 2, :, 0:DH].rearrange("p t h d -> p (t h) d"),
                                                     bank[1 + c][:].rearrange("p (h d) -> p h d", d=DH),
                                                     spread(row("bv"), 1, 2).rearrange("p t (h d) -> p t h d", d=DH), ALU.add)
                        last.then_inc(s("v_ok"), 1)
                        dve.wait_ge(s("kn_mm"), 1)
                        done(dve.tensor_copy(kn[:].rearrange("p t m h -> p (t m h)"), bank[3][:, 0:T * H]))
                        settle()
                        for n in range(8):
                            dve.wait_ge(s("kf_mm"), n + 1)
                            dve.tensor_tensor(kf[:, n // 2, 8 * (n % 2):8 * (n % 2) + 8, :],
                                              bank[4 + n % 2][:].rearrange("p (h m) -> p h m", m=M),
                                              spread(kn[:, n // 2, n % 2, :], 2, M), ALU.add).then_inc(s("kf_sub"), 1)
                        dve.wait_ge(s("kv0"), 1)
                        dve.wait_ge(s("kv_mm"), 1)
                        src = bank[1][:, 0:NP * 2 * V1].rearrange("p (n c) -> p n c", c=2 * V1)
                        dve.tensor_copy(kv[0:M, :, 0:V1], src[0:M, :, 0:V1])
                        dve.tensor_copy(kv[M:P, :, V1:2 * V1], src[M:P, :, V1:2 * V1]).then_inc(s("kv_ok"), 1)
                        for t in range(T):
                            o = bank[2 + t][:, 0:NP * 2 * V1].rearrange("p (h c) -> p h c", c=V1)
                            dve.wait_ge(s("o_mm"), t + 1)
                            done(dve.reciprocal(den[:, t, :], o[:, :, DH]))
                            settle()
                            dve.tensor_tensor(on[:, t, :].rearrange("p (h d) -> p h d", d=DH), o[:, :, 0:DH],
                                              spread(den[:, t, :], 2, DH), ALU.mult).then_inc(s("on_ok"), 1)
                        dve.wait_ge(s("wo_mm"), 1)
                        dve.wait_ge(s("xb_ok"), 1)
                        for c in range(2):
                            last = dve.tensor_tensor(x3[:, 2 * c:2 * c + 2, :], bank[c][:].rearrange("p (t f) -> p t f", t=2),
                                                     xb[:, 2 * c:2 * c + 2, :], ALU.add)
                        last.then_inc(s("x3_ok"), 1)
                        dve.wait_ge(s("yq_mm"), 1)
                        for c in range(2):
                            done(dve.tensor_tensor(yq[:, 2 * c:2 * c + 2, :], bank[4 + c][:].rearrange("p (t f) -> p t f", t=2),
                                                   spread(brow[:], 1, 2), ALU.add))
                        settle()
                        done(dve.tensor_reduce(ab[:, 0, :], yq[:], X, ALU.max, apply_absolute_value=True))
                        settle()
                        done(dve.tensor_scalar(ab[:, 1, :], ab[:, 0, :], 1e-6, 1.0 / 127.0, ALU.max, ALU.mult))
                        settle()
                        done(dve.reciprocal(ab[:, 2, :], ab[:, 1, :]))
                        settle()
                        for t in range(T):
                            done(dve.tensor_scalar(yq[:, t, :], yq[:, t, :], ab[:, 2, t:t + 1], ROUND, ALU.mult, ALU.add))
                        settle()
                        dve.tensor_scalar(yb[:], yq[:], ROUND, 127.0, ALU.subtract, ALU.min).then_inc(s("yb_ok"), 1)
                        dve.wait_ge(s("acc_mm"), 1)
                        for t in range(T):
                            done(dve.scalar_tensor_tensor(fo[:, t, :], bank[t // 2][:, (t % 2) * D:(t % 2 + 1) * D], ab[:, 1, t:t + 1],
                                                          row("ws"), ALU.mult, ALU.mult))
                        settle()
                        dve.wait_ge(s("x3b_ok"), 1)
                        dve.tensor_tensor(fo[:], fo[:], xb[:], ALU.add).then_inc(s("fin"), 1)
                s.clear()


def layouts(i):
    f = np.float32

    def tiles(w):
        return w.reshape(-1, P, w.shape[1]).transpose(1, 0, 2)

    def padded(w, rows=P):
        o = np.zeros((rows,) + w.shape[1:], w.dtype)
        o[:w.shape[0]] = w
        return o

    o = {}
    x = i["x"]
    o["xT"] = x.transpose(0, 2, 1).reshape(B, K2, P, S).transpose(0, 2, 1, 3)
    o["xN"] = x.reshape(B, T, P, D).transpose(0, 2, 1, 3)
    o["ids"] = np.concatenate([i[k].reshape(B, T, P).transpose(0, 2, 1)
                               for k in ("itok_BxS_0_999", "itok_BxS_0_4", "mask_BxS_ik0")], 2)
    o["boff"] = (CAP * np.arange(B)).astype(f).reshape(B, 1)
    o["cond"] = np.stack([padded(i[k].T) for k in ("cond_512", "cond_64", "fside_Bx32_0")], 1)
    o["affw"] = np.stack([i[f"L0_cond_{k}_aff_w"].T.reshape(P, K2, P) for k in "ko"], 1)
    o["affb"] = np.stack([i[f"L0_cond_{k}_aff_b"].reshape(K2, P).T for k in "ko"], 1)
    o["kow"] = np.stack([tiles(i[f"L0_cond_{k}_w"].T) for k in "ko"], 1)
    o["obcol"] = i["L0_cond_o_b"].reshape(K2, P).T
    wqkv = i["L0_attn_w_qkv"].T
    bqkv = i["L0_attn_b_qkv"]
    o["wqk"] = tiles(wqkv[:, 0:2 * D])
    o["wvl"] = tiles(np.concatenate([wqkv[:, 2 * D:]] + [i[f"L0_attn_{k}"].T for k in
                                    ("w1_read", "w1_write", "w2_read", "w2_write")], 1))
    o["wout"] = tiles(i["L0_attn_w_out"].T)
    dl, bs = i["L0_attn_decay_logits"], i["L0_attn_bias_scale"]
    o["dlr"] = np.concatenate([np.broadcast_to(dl, (P, H)), np.repeat(dl.reshape(HG, HG).T, 32, 0)], 1)
    aw = i["L0_cond2_aw"]
    c2 = lambda k: i[f"L0_cond2_{k}"]
    o["rows0"] = np.concatenate([i["L0_cond_k_b"], bqkv[0:2 * D], bqkv[2 * D:], i["L0_attn_b_out"], c2("int_b2"),
                                 c2("int_g"), c2("int_be"), i["L0_ffn_br"], aw, dl, bs])
    q = np.arange(P, dtype=f)
    r = np.arange(P) % 32
    o["cst"] = np.stack([q, P - q, (r < DH), (r >= DH) & (r < DH + NOFF), (r >= DH + NOFF) & (r < DH + 2 * NOFF),
                         0 * q, 0 * q, 0 * q], 1).astype(f)
    o["ident"] = np.eye(P, dtype=f)
    o["identb"] = np.eye(P, dtype=mybir.dt.np(BF16))
    dist = q[:, None] - q[None, :]
    o["posd"] = np.maximum(dist, 0).astype(f)
    o["low"] = (dist > 0).astype(f)
    o["tri"] = (dist < 0).astype(f)
    o["negb"] = np.where(dist < 0, MASKED, 0.0).astype(mybir.dt.np(BF16))
    o["iota"] = np.arange(SLOTS, dtype=f)
    sg = np.ones((2 * H, NOFF), f)
    sg[H:, 1] = sg[H:, 4] = -1
    o["sign"] = sg
    o["w1all"] = tiles(c2("int_W1"))
    o["wint2"] = tiles(c2("int_W2"))
    o["ib1"] = c2("int_b1").reshape(K2, P).T
    o["m1"] = np.stack([padded(c2(f"{k}_W1")) for k in ("mem", "noi", "res")], 1)
    o["m2"] = np.stack([tiles(c2(f"{k}_W2")) for k in ("mem", "noi", "res")], 1)
    o["mrow"] = np.stack([np.stack([c2(f"{k}_{n}") for n in ("b1", "b2", "g", "be")]) for k in ("mem", "noi", "res")])
    o["pw"] = np.concatenate([c2("pw_g"), c2("pw_b")], 1)
    o["cptm"] = np.concatenate([c2("cp_g"), c2("cp_b"), c2("tm_g"), c2("tm_b")], 1)
    o["ms"] = np.concatenate([c2("ms_g"), c2("ms_b")], 1)
    o["wr"] = tiles(i["L0_ffn_Wr"])
    o["eW1"] = i["L0_ffn_W1"].reshape(E, K2, P, HID).transpose(0, 2, 1, 3)
    o["eW2"] = i["L0_ffn_W2"].reshape(E, KH, P, D).transpose(0, 2, 1, 3)
    o["eb1"] = i["L0_ffn_b1"].reshape(E, KH, P).transpose(0, 2, 1)
    o["eb2"] = i["L0_ffn_b2"]
    o["dgu"] = np.concatenate([i[f"L1_cond_{k}"] for k in ("down_gamma", "down_beta", "up_gamma", "up_beta")], 1)
    o["wdc"] = i["L1_cond2_W_dec"].reshape(P, D + 1, KR).transpose(0, 2, 1)
    bd = i["L1_cond2_b_dec"].reshape(D + 1, KR)
    o["bdc"] = bd[0:D].reshape(K2, P, KR).transpose(1, 0, 2)
    o["bdl"] = bd[D].reshape(KR, 1)
    o["vv"] = i["L1_cond2_V"]
    o["dup"] = tiles(i["L1_cond_down_project"])
    o["upp"] = i["L1_cond_up_project"]
    o["wqkv"] = np.stack([tiles(i[f"L1_attn_W{k}"].T) for k in "qkv"], 1)
    o["wo1"] = tiles(i["L1_attn_Wo"].T)
    o["qkcol"] = np.stack([i[f"L1_attn_b{k}"].reshape(K2, P).T for k in "qk"], 1)
    orf = np.zeros((8, DH, 8, M), f)
    for h in range(8):
        orf[h, :, h, :] = i["L1_attn_orf"].T
    o["orfk"] = orf.reshape(P, 8 * M)
    nk = np.zeros((P, 8), f)
    nk[np.arange(P), np.arange(P) // DH] = -1.0 / 8
    o["nrmk"] = nk
    nq = np.zeros((P, P), f)
    for p in range(P):
        h = p // DH % 2
        nq[p, h * M:(h + 1) * M] = -1.0 / 8
    o["nrmq"] = nq
    o["wq8"] = np.ascontiguousarray(tiles(i["L1_ffn_weight_q"].T)).view(np.int32)
    o["rows1"] = np.concatenate([i["L1_attn_bv"], i["L1_attn_bo"], i["L1_ffn_weight_scale"], i["L1_ffn_bias"]])
    return {k: np.ascontiguousarray(v) for k, v in o.items()}


def kernel(**inputs):
    import concourse.bacc as bacc
    from concourse.bass_utils import run_bass_kernel_spmd

    nc = bacc.Bacc("TRN2", target_bir_lowering=False, num_devices=1)
    arrays = {f"in_{k}": v for k, v in layouts({k: np.asarray(v) for k, v in inputs.items()}).items()}
    a = {k[3:]: nc.dram_tensor(k, v.shape, mybir.dt.from_np(v.dtype), kind="ExternalInput").ap() for k, v in arrays.items()}
    out = nc.dram_tensor("out_0", (B, S, D), F32, kind="ExternalOutput").ap()
    program(nc, a, out)
    r = run_bass_kernel_spmd(nc, [arrays], core_ids=[0])
    return r.results[0]["out_0"]
```

```python
from contextlib import ExitStack

import numpy as np

import concourse.bass as bass
from concourse import mybir

F32 = mybir.dt.float32
BF16 = mybir.dt.bfloat16
I32 = mybir.dt.int32
I8 = mybir.dt.int8
U32 = mybir.dt.uint32
ALU = mybir.AluOpType
ACT = mybir.ActivationFunctionType
X = mybir.AxisListType.X

P = 128
B, S, D = 8, 512, 256
T = S // P
K2 = D // P
H, DH = 16, 16
HG = 4
E, CAP, HID = 8, 80, 1024
SLOTS = E * CAP
ROWS = B * CAP
ST = ROWS // P
KH = HID // P
M = 64
LN_EPS = 1e-5
MASKED = -1.0e30
ROUND = 12582912.0
NOFF = 6
KR = 30

ROWS0 = [("kb", D), ("bqk", 2 * D), ("bv", D), ("bout", D), ("b2", D), ("g", D), ("be", D),
         ("br", E), ("aw", 6), ("dl", H), ("bs", H)]
ROWS1 = [("bv", D), ("bo", D), ("ws", D), ("bias", D)]


AT = {"kx": 0, "z": 1, "x": 2, "h1": 4, "h2": 5, "t": 7, "h": 9, "s": 13, "u": 15, "y": 21, "f": 27, "pos": 35, "disp": 43,
      "pair": 2, "full": 17, "turn1": 52}


def resume(stream, due):
    yield due
    yield from stream


def offsets(fields):
    out, at = {}, 0
    for name, n in fields:
        out[name] = (at, at + n)
        at += n
    return out, at


def spread(ap, at, n, step=0):
    dims = [list(d) for d in ap.ap]
    dims.insert(at, [step, n])
    return bass.AP(ap.tensor, ap.offset, dims)


def program(nc, a, out, scratch_kind="Internal", parts="ABC"):
    R0, n0 = offsets(ROWS0)
    R1, n1 = offsets(ROWS1)
    x1_d = nc.dram_tensor("x1_d", [B, P, T, D], F32, kind=scratch_kind).ap()
    gate_d = nc.dram_tensor("gate_d", [B, P, 4 * T], F32, kind=scratch_kind).ap()
    buf_d = nc.dram_tensor("buf_d", [E, P, K2, B, CAP], F32, kind=scratch_kind).ap()
    y_d = nc.dram_tensor("y_d", [E * ROWS, D], F32, kind=scratch_kind).ap()
    prow_d = nc.dram_tensor("prow_d", [B, 2 * D + 2 * M + 2 * D], F32, kind=scratch_kind).ap()
    wdec_d = nc.dram_tensor("wdec_d", [B, P, K2, D], F32, kind=scratch_kind).ap()
    PR = {"demk": (0, D), "dg": (D, D + M), "db": (D + M, D + 2 * M), "ug": (D + 2 * M, 2 * D + 2 * M),
          "ub": (2 * D + 2 * M, 3 * D + 2 * M), "bias": (3 * D + 2 * M, 4 * D + 2 * M)}

    top = ExitStack()
    with top:
        def sb_in(ctx, name, shape, dt=F32):
            return ctx.enter_context(nc.sbuf_tensor(name, shape, dt))

        bank = [top.enter_context(nc.psum_tensor(f"bank{i}", [P, 512], F32)) for i in range(8)]

        ident = sb_in(top, "ident", [P, P])
        pcol = sb_in(top, "pcol", [P, B, 8])
        eps_ln = sb_in(top, "eps_ln", [P, 2])

        class Sems:

            def __init__(self, ctx, prefix):
                self.ctx, self.prefix, self.by = ctx, prefix, {}

            def __call__(self, name):
                if name not in self.by:
                    self.by[name] = self.ctx.enter_context(nc.semaphore(f"{self.prefix}_{name}"))
                return self.by[name]

            def clear(self):
                nums = [s.num for s in self.by.values()]
                nc.all_engine_barrier(sems_to_clear=range(min(nums), max(nums) + 1))

        def chain_of(eng, sem):
            n = [0]

            def done(ins):
                n[0] += 1
                ins.then_inc(sem, 1)
                return n[0]

            def settle():
                eng.wait_ge(sem, n[0])

            return done, settle

        if True:
            l0 = ExitStack()
            with l0:
                sb = lambda name, shape, dt=F32: sb_in(l0, name, shape, dt)
                kow = sb("kow", [P, 2, K2, D])
                wqk = sb("wqk", [P, K2, 2 * D])
                wvl = sb("wvl", [P, K2, 2 * D])
                wout = sb("wout", [P, K2, D])
                wint = sb("wint", [P, 4 * K2, D])
                wint2 = sb("wint2", [P, K2, D])
                wr = sb("wr", [P, K2, E])
                rows = sb("rows", [P, n0])
                obcol = sb("obcol", [P, K2])
                tri = sb("tri", [P, P])
                ones = sb("ones", [P, P])
                negb = sb("negb", [P, P], BF16)
                identb = sb("identb", [P, P], BF16)
                iota = sb("iota", [P, SLOTS])
                wdiag = sb("wdiag", [P, H, P])
                facr = sb("facr", [P, H])
                facw = sb("facw", [P, H])
                fack = sb("fack", [P, HG, 4])
                sign = sb("sign", [P, 2 * H, NOFF])
                row = lambda f: rows[:, R0[f][0]:R0[f][1]]

                st = ExitStack()
                with st:
                    sbt = lambda name, shape, dt=F32: sb_in(st, name, shape, dt)
                    cond = sbt("cond", [P, 3, B])
                    affw = sbt("affw", [P, 2, K2, P])
                    affb = sbt("affb", [P, 2, K2])
                    w1all = sbt("w1all", [P, 6 * K2, D])
                    m1 = sbt("m1", [P, 3, D])
                    m2 = sbt("m2", [P, 3, K2, D])
                    mrow = sbt("mrow", [B, 3, 4, D])
                    ib1 = sbt("ib1", [P, K2])
                    cst = sbt("cst", [P, 8])
                    posd = sbt("posd", [P, P])
                    low = sbt("low", [P, P])
                    dlr = sbt("dlr", [P, H + HG])
                    lnd = sbt("lnd", [P, H + HG])
                    tmp = sbt("tmp", [P, H + HG])
                    tmp2 = sbt("tmp2", [P, H + HG])
                    aws = sbt("aws", [P, 6])
                    awr = sbt("awr", [P, 4])
                    style2 = sbt("style2", [P, 2, K2, B])
                    kow2 = sbt("kow2", [P, 2, K2, D])
                    drow = sbt("drow", [B, D])
                    dco = sbt("dco", [P, K2, B])
                    g1 = sbt("g1", [B, 3, D])
                    g1t = sbt("g1t", [P, 3, K2, B])
                    g2 = sbt("g2", [B, 3, D])
                    g2t = sbt("g2t", [P, 3, K2, B])
                    mstat = sbt("mstat", [B, 3, 6])
                    mmv = sbt("mmv", [B, 3, 4])
                    dgu = sbt("dgu", [P, 2 * M + 2 * D])
                    dguo = sbt("dguo", [B, 2 * M + 2 * D])
                    wdc = sbt("wdc", [P, KR, D + 1])
                    bdc = sbt("bdc", [P, K2, KR])
                    bdl = sbt("bdl", [KR, 1])
                    vv = sbt("vv", [KR, D])
                    uu = sbt("uu", [P, K2, B, KR])
                    ul = sbt("ul", [KR, B])
                    ut = sbt("ut", [KR, 2, P])
                    wde = sbt("wde", [P, 2, D])
                    brow = sbt("brow", [B, D])
                    sctx = ExitStack()
                    with sctx:
                        s = Sems(sctx, "s0")
                        with nc.Block() as block:
                            @block.sync
                            def _(sp):
                                for dst, name in ((cond, "cond"), (affw, "affw"), (affb, "affb"), (kow, "kow"),
                                                  (dlr, "dlr"), (cst, "cst"), (ident, "ident")):
                                    sp.dma_start(dst[:], a[name]).then_inc(s("load1"), 16)
                                sp.dma_start(rows[:], spread(a["rows0"], 0, P)).then_inc(s("load1"), 16)
                                for dst, name in ((posd, "posd"), (low, "low"), (w1all, "w1all"), (m1, "m1"), (m2, "m2"),
                                                  (ib1, "ib1"), (wqk, "wqk")):
                                    sp.dma_start(dst[:], a[name]).then_inc(s("load2"), 16)
                                sp.dma_start(mrow[:], spread(a["mrow"], 0, B)).then_inc(s("load2"), 16)
                                for dst, name in ((dgu, "dgu"), (wdc, "wdc"), (bdc, "bdc"), (bdl, "bdl"), (vv, "vv")):
                                    sp.dma_start(dst[:], a[name]).then_inc(s("load3"), 16)
                                for dst, name in ((wvl, "wvl"), (wout, "wout"), (wint2, "wint2"), (wr, "wr"),
                                                  (obcol, "obcol"), (tri, "tri"), (negb, "negb"), (identb, "identb")):
                                    sp.dma_start(dst[:], a[name]).then_inc(s("load4"), 16)
                                sp.dma_start(iota[:], spread(a["iota"], 0, P)).then_inc(s("load4"), 16)
                                sp.dma_start(sign[:], spread(a["sign"], 0, P)).then_inc(s("load4"), 16)
                                sp.wait_ge(s("drow_ok"), 1)
                                sp.dma_start(prow_d[:, 0:D], drow[:]).then_inc(s("stored"), 16)
                                sp.wait_ge(s("dguo_ok"), 1)
                                sp.dma_start(prow_d[:, D:3 * D + 2 * M], dguo[:]).then_inc(s("stored"), 16)
                                sp.wait_ge(s("brow_ok"), 1)
                                sp.dma_start(prow_d[:, 3 * D + 2 * M:], brow[:]).then_inc(s("stored"), 16)
                                for n in range(B * K2):
                                    sp.wait_ge(s("wde_ok"), n + 1)
                                    sp.dma_start(wdec_d[n // K2, :, n % K2, :], wde[:, n % 2, :]).then_inc(s(f"wstored{n % 2}"), 16)
                                sp.wait_ge(s("stored"), 48)
                                sp.wait_ge(s("wstored0"), 8 * B * K2)
                                sp.wait_ge(s("wstored1"), 8 * B * K2)
                                sp.wait_ge(s("load4"), 160)
                                sp.wait_ge(s("load1"), 128)
                                sp.wait_ge(s("load2"), 128)
                                sp.wait_ge(s("load3"), 80)

                            @block.gpsimd
                            def _(pool):
                                pool.memset(ones[:], 1.0).then_inc(s("ones_ok"), 1)
                                pool.memset(eps_ln[:, 0:1], LN_EPS).then_inc(s("ones_ok"), 1)
                                pool.memset(eps_ln[:, 1:2], 1e-8).then_inc(s("ones_ok"), 1)

                            @block.tensor
                            def _(pe):
                                pe.wait_ge(s("load1"), 128)
                                for w in range(2):
                                    for m in range(K2):
                                        mm = pe.matmul(bank[0][:, (w * K2 + m) * B:(w * K2 + m + 1) * B], affw[:, w, m, :],
                                                       cond[:, 0, :], start=True, stop=True)
                                mm.then_inc(s("style_mm"), 1)
                                pe.wait_ge(s("sq_ok"), 2)
                                for m in range(K2):
                                    mm = pe.matmul(bank[1][0:B, 0:D], style2[:, 0, m, :], kow2[:, 0, m, :],
                                                   start=(m == 0), stop=(m == K2 - 1))
                                mm.then_inc(s("dem_mm"), 1)
                                for o in range(K2):
                                    for m in range(K2):
                                        mm = pe.matmul(bank[2][:, o * B:(o + 1) * B], kow2[:, 1, m, o * P:(o + 1) * P],
                                                       style2[:, 1, m, :], start=(m == 0), stop=(m == K2 - 1))
                                mm.then_inc(s("dem_mm"), 1)
                                pe.wait_ge(s("load2"), 128)
                                for j, k in enumerate((P, 64, 32)):
                                    mm = pe.matmul(bank[3 + j][0:B, 0:D], cond[0:k, j, :], m1[0:k, j, :], start=True, stop=True)
                                    mm.then_inc(s("m1_mm"), 1)
                                pe.wait_ge(s("g1_ok"), 1)
                                for j in range(3):
                                    for m in range(K2):
                                        mm = pe.transpose(bank[6][:, (j * K2 + m) * B:(j * K2 + m + 1) * B],
                                                          g1[:, j, m * P:(m + 1) * P], ident[0:B, 0:B])
                                mm.then_inc(s("g1t_mm"), 1)
                                pe.wait_ge(s("g1t_ok"), 1)
                                for j in range(3):
                                    for m in range(K2):
                                        mm = pe.matmul(bank[3 + j][0:B, 0:D], g1t[:, j, m, :], m2[:, j, m, :],
                                                       start=(m == 0), stop=(m == K2 - 1))
                                mm.then_inc(s("m2_mm"), 1)
                                pe.wait_ge(s("g2_ok"), 1)
                                for j in range(3):
                                    for m in range(K2):
                                        mm = pe.transpose(bank[6][:, (j * K2 + m) * B:(j * K2 + m + 1) * B],
                                                          g2[:, j, m * P:(m + 1) * P], ident[0:B, 0:B])
                                mm.then_inc(s("g2t_mm"), 1)
                                pe.wait_ge(s("g2t_ok"), 1)
                                for o in range(K2):
                                    for n in range(3 * K2):
                                        j, m = n // K2, n % K2
                                        mm = pe.matmul(bank[7][:, o * B:(o + 1) * B],
                                                       w1all[:, (2 + j) * K2 + m, o * P:(o + 1) * P], g2t[:, j, m, :],
                                                       start=(n == 0), stop=(n == 3 * K2 - 1))
                                mm.then_inc(s("cvec_mm"), 1)
                                pe.wait_ge(s("load3"), 80)
                                hw = M + D
                                for n in range(2):
                                    mm = pe.matmul(bank[3 + n][0:B, 0:hw], cond[:, 0, :], dgu[:, n * hw:(n + 1) * hw],
                                                   start=True, stop=True)
                                mm.then_inc(s("dgu_mm"), 1)
                                for m in range(K2):
                                    for k in range(KR):
                                        mm = pe.matmul(bank[m][:, k * B:(k + 1) * B], wdc[:, k, m * P:(m + 1) * P],
                                                       cond[:, 0, :], start=True, stop=True)
                                mm = pe.matmul(bank[2][0:KR, 0:B], wdc[:, :, D], cond[:, 0, :], start=True, stop=True)
                                mm.then_inc(s("u_mm"), 1)
                                pe.wait_ge(s("u_ok"), 1)
                                pe.matmul(bank[5][0:B, 0:D], ul[:, :], vv[:, :], start=True, stop=True).then_inc(s("brow_mm"), 1)
                                for n in range(B * K2):
                                    if n >= 2:
                                        pe.wait_ge(s("ut_ok"), n - 1)
                                    pe.transpose(bank[n % 2][0:KR, 0:P], uu[:, n % K2, n // K2, :], ident[:, :]).then_inc(s("ut_mm"), 1)
                                    pe.wait_ge(s("ut_ok"), n + 1)
                                    if n >= 2:
                                        pe.wait_ge(s("wde_ok"), n - 1)
                                    pe.matmul(bank[6 + n % 2][:, 0:D], ut[:, n % 2, :], vv[:, :], start=True, stop=True)\
                                        .then_inc(s("wde_mm"), 1)

                            @block.scalar
                            def _(act):
                                done, settle = chain_of(act, s("act_own"))
                                act.wait_ge(s("ones_ok"), 3)
                                act.wait_ge(s("load1"), 128)
                                act.activation(kow2[:], kow[:], ACT.Square).then_inc(s("sq_ok"), 1)
                                act.wait_ge(s("absx"), 1)
                                act.activation(tmp[:], tmp[:], ACT.Exp, scale=-1.0).then_inc(s("expx"), 1)
                                act.wait_ge(s("awsub"), 1)
                                done(act.activation(aws[:], aws[:], ACT.Exp, accum_out=awr[:, 0:1]))
                                settle()
                                act.activation(tmp2[:], tmp[:], ACT.Ln, bias=1.0).then_inc(s("lnx"), 1)
                                act.wait_ge(s("lnd_ok"), 1)
                                act.wait_ge(s("load2"), 128)
                                for h in range(H):
                                    act.activation(wdiag[:, h, :], posd[:], ACT.Exp, scale=lnd[:, h:h + 1])
                                act.activation(facr[:], lnd[:, 0:H], ACT.Exp, scale=cst[:, 0:1])
                                act.activation(facw[:], lnd[:, 0:H], ACT.Exp, scale=cst[:, 1:2])
                                for v in range(3):
                                    last = act.activation(fack[:, :, v], lnd[:, H:H + HG], ACT.Exp, scale=float(P * v))
                                last.then_inc(s("pow_ok"), 1)
                                act.wait_ge(s("dem_mm"), 2)
                                act.activation(drow[:], bank[1][0:B, 0:D], ACT.Sqrt, bias=eps_ln[0:B, 1:2])
                                act.activation(dco[:], bank[2][:, 0:K2 * B].rearrange("p (o b) -> p o b", b=B), ACT.Sqrt,
                                               bias=eps_ln[:, 1:2]).then_inc(s("dem_sq"), 1)
                                act.wait_ge(s("g1_pre"), 1)
                                act.activation(g1[:], g1[:], ACT.Silu).then_inc(s("g1_ok"), 1)
                                act.wait_ge(s("mvar"), 1)
                                act.activation(mmv[:, :, 2:3], mmv[:, :, 1:2], ACT.Sqrt, bias=eps_ln[0:B, 0:1]).then_inc(s("msd"), 1)
                                for n in range(B * K2):
                                    act.wait_ge(s("ut_mm"), n + 1)
                                    if n >= 2:
                                        act.wait_ge(s("wde_mm"), n - 1)
                                    act.copy(ut[:, n % 2, :], bank[n % 2][0:KR, 0:P]).then_inc(s("ut_ok"), 1)

                            @block.vector
                            def _(dve):
                                done, settle = chain_of(dve, s("dve_own"))
                                dve.wait_ge(s("load1"), 128)
                                dve.tensor_scalar(tmp2[:], dlr[:], -1.0, None, ALU.mult).then_inc(s("neg"), 1)
                                done(dve.tensor_reduce(awr[:, 1:2], row("aw"), X, ALU.max))
                                dve.wait_ge(s("neg"), 1)
                                dve.tensor_tensor(tmp[:], dlr[:], tmp2[:], ALU.max).then_inc(s("absx"), 1)
                                settle()
                                dve.tensor_scalar(aws[:], row("aw"), awr[:, 1:2], None, ALU.subtract).then_inc(s("awsub"), 1)
                                done(dve.tensor_scalar(lnd[:], dlr[:], 0.0, None, ALU.min))
                                dve.wait_ge(s("style_mm"), 1)
                                for w in range(2):
                                    for m in range(K2):
                                        n = w * K2 + m
                                        done(dve.tensor_scalar(pcol[:, :, n], bank[0][:, n * B:(n + 1) * B],
                                                               affb[:, w, m:m + 1], None, ALU.add))
                                settle()
                                sty = pcol[:, :, 0:4].rearrange("p b (w m) -> p w m b", w=2)
                                for w in range(2):
                                    last = dve.tensor_tensor(style2[:, w], sty[:, w], sty[:, w], ALU.mult)
                                last.then_inc(s("sq_ok"), 1)
                                dve.wait_ge(s("lnx"), 1)
                                dve.tensor_tensor(lnd[:], lnd[:], tmp2[:], ALU.subtract).then_inc(s("lnd_ok"), 1)
                                dve.wait_ge(s("dem_sq"), 1)
                                dve.reciprocal(drow[:], drow[:]).then_inc(s("drow_ok"), 1)
                                dve.reciprocal(pcol[:, :, 4:6].rearrange("p b o -> p o b"), dco[:])
                                done(dve.reciprocal(awr[:, 2:3], awr[:, 0:1]))
                                settle()
                                done(dve.tensor_scalar(aws[:], aws[:], awr[:, 2:3], None, ALU.mult))
                                settle()
                                dve.wait_ge(s("load2"), 128)
                                for j in range(2, 5):
                                    done(dve.tensor_scalar(w1all[:, K2 * j:K2 * j + K2, :], w1all[:, K2 * j:K2 * j + K2, :],
                                                           aws[:, j:j + 1], None, ALU.mult))
                                for at, j in ((2, 5), (4, 1), (6, 0)):
                                    done(dve.tensor_scalar(wint[:, at:at + K2, :], w1all[:, K2 * j:K2 * j + K2, :],
                                                           aws[:, j:j + 1], None, ALU.mult))
                                settle()
                                done(dve.tensor_tensor(wint[:, 0:K2, :], w1all[:, 4:6, :], w1all[:, 6:8, :], ALU.add))
                                settle()
                                done(dve.tensor_tensor(wint[:, 0:K2, :], wint[:, 0:K2, :], w1all[:, 8:10, :], ALU.add))
                                done(dve.tensor_scalar(wqk[:, :, 0:D], wqk[:, :, 0:D], 0.25, None, ALU.mult))
                                q0 = R0["bqk"][0]
                                done(dve.tensor_scalar(rows[:, q0:q0 + D], rows[:, q0:q0 + D], 0.25, None, ALU.mult))
                                dve.wait_ge(s("pow_ok"), 1)
                                done(dve.tensor_tensor(wdiag[:], wdiag[:], spread(low[:], 1, H), ALU.mult))
                                done(dve.tensor_tensor(facr[:], facr[:], row("bs"), ALU.mult))
                                done(dve.tensor_scalar(fack[:, :, 0:3], fack[:, :, 0:3], cst[:, 3:4], cst[:, 2:3], ALU.mult, ALU.add))
                                done(dve.tensor_copy(fack[:, :, 3], spread(cst[:, 4:5], 1, HG)[:, :, 0]))
                                dve.wait_ge(s("m1_mm"), 3)
                                for j in range(3):
                                    last = dve.tensor_tensor(g1[:, j, :], bank[3 + j][0:B, 0:D], mrow[:, j, 0, :], ALU.add)
                                last.then_inc(s("g1_pre"), 1)
                                dve.wait_ge(s("g1t_mm"), 1)
                                dve.tensor_copy(g1t[:].rearrange("p j m b -> p (j m b)"), bank[6][:, 0:3 * K2 * B]).then_inc(s("g1t_ok"), 1)
                                dve.wait_ge(s("m2_mm"), 1)
                                for j in range(3):
                                    done(dve.tensor_tensor(g2[:, j, :], bank[3 + j][0:B, 0:D], mrow[:, j, 1, :], ALU.add))
                                settle()
                                for j in range(3):
                                    done(dve.bn_stats(mstat[:, j, :], g2[:, j, :]))
                                settle()
                                for j in range(3):
                                    last = dve.bn_aggr(mmv[:, j, 0:2], mstat[:, j, :])
                                last.then_inc(s("mvar"), 1)
                                dve.wait_ge(s("msd"), 1)
                                done(dve.reciprocal(mmv[:, :, 3:4], mmv[:, :, 2:3]))
                                settle()
                                for j in range(3):
                                    done(dve.tensor_scalar(g2[:, j, :], g2[:, j, :], mmv[:, j, 0:1], mmv[:, j, 3:4],
                                                           ALU.subtract, ALU.mult))
                                settle()
                                done(dve.tensor_tensor(g2[:], g2[:], mrow[:, :, 2, :], ALU.mult))
                                settle()
                                dve.tensor_tensor(g2[:], g2[:], mrow[:, :, 3, :], ALU.add).then_inc(s("g2_ok"), 1)
                                dve.wait_ge(s("g2t_mm"), 1)
                                dve.tensor_copy(g2t[:].rearrange("p j m b -> p (j m b)"), bank[6][:, 0:3 * K2 * B]).then_inc(s("g2t_ok"), 1)
                                dve.wait_ge(s("cvec_mm"), 1)
                                for o in range(K2):
                                    dve.tensor_scalar(pcol[:, :, 6 + o], bank[7][:, o * B:(o + 1) * B], ib1[:, o:o + 1], None, ALU.add)
                                dve.wait_ge(s("dgu_mm"), 1)
                                hw = M + D
                                dve.tensor_copy(dguo[:, 0:hw], bank[3][0:B, 0:hw])
                                dve.tensor_copy(dguo[:, hw:2 * hw], bank[4][0:B, 0:hw]).then_inc(s("dguo_ok"), 1)
                                dve.wait_ge(s("u_mm"), 1)
                                for m in range(K2):
                                    dve.tensor_tensor(uu[:, m].rearrange("p b k -> p k b"),
                                                      bank[m][:, 0:KR * B].rearrange("p (k b) -> p k b", b=B),
                                                      spread(bdc[:, m, :], 2, B), ALU.add)
                                dve.tensor_scalar(ul[:], bank[2][0:KR, 0:B], bdl[:, 0:1], None, ALU.add).then_inc(s("u_ok"), 1)
                                dve.wait_ge(s("brow_mm"), 1)
                                dve.tensor_copy(brow[:], bank[5][0:B, 0:D]).then_inc(s("brow_ok"), 1)
                                for n in range(B * K2):
                                    dve.wait_ge(s("wde_mm"), n + 1)
                                    if n >= 2:
                                        dve.wait_ge(s(f"wstored{n % 2}"), 16 * (n // 2))
                                    dve.tensor_copy(wde[:, n % 2, :], bank[6 + n % 2][:, 0:D]).then_inc(s("wde_ok"), 1)
                        s.clear()

                cT = sb("cT", [P, K2, S + 1])
                x1 = sb("x1", [P, T, D])
                xt_na = sb("xt_na", [P, T * D])
                xT = xt_na[:].rearrange("p (m s) -> p m s", m=K2)
                nA1 = xt_na[:].rearrange("p (t f) -> p t f", t=T)
                kx = sb("kx", [P, T, 2 * D])
                big = sb("big", [P, 9 * D + T * H * 2 * H])
                prod = big[:, 0:9 * D].rearrange("p (o f) -> p o f", f=D)
                wk = big[:, 0:K2 * D].rearrange("p (m f) -> p m f", f=D)
                sc = big[:, 9 * D:].rearrange("p (t o h) -> p t o h", o=H, h=2 * H)
                pv = big[:, 0:H * D].rearrange("p (o f) -> p o f", f=D)
                ex_at = sb("ex_at", [P, T * D])
                ex = ex_at[:].rearrange("p (t o h) -> p t o h", o=H, h=H)
                aT1 = ex_at[:].rearrange("p (m s) -> p m s", m=K2)
                mx = sb("mx", [P, T, H])
                rs = sb("rs", [P, T, H])
                wo = sb("wo", [P, K2, D])
                demk = sb("demk", [P, D])
                pc1 = sb("pc1", [P, 8])
                xN = sb("xN", [P, T, D])
                vls = sb("vls", [P, T, 2 * D])
                att_buf = sb("att_buf", [P, T * 2 * H * 32])
                qk = att_buf[:].rearrange("p (t s h r) -> p t s h r", t=T, s=2, h=H)
                pr = att_buf[:, 0:3 * S].rearrange("p (n s) -> p n s", n=3)
                prT = att_buf[:, 3 * S:6 * S].rearrange("p (n s) -> p n s", n=3)
                dbias = att_buf[:, 6 * S:8 * S].rearrange("p (n i k) -> p n i k", n=2, k=P)
                qT = sb("qT", [P, HG, S])
                k0T = sb("k0T", [P, HG, S])
                k1T = sb("k1T", [P, HG, 2 * P])
                k2T = sb("k2T", [P, HG, P])
                kiT = sb("kiT", [P, HG, S])
                lines = qT[:].rearrange("p g s -> p (g s)")[:, 0:2 * T * 2 * H * NOFF].rearrange("p (n t s c) -> p n t s c", n=2, t=T, c=NOFF)
                la, lb = lines[:, 0], lines[:, 1]
                aT2 = k0T[:, 0:K2, :]
                nA2 = sb("nA2", [P, T, D])
                ln = sb("ln", [P, T, 2 * H])
                lf = sb("lf", [P, 4, T, H])
                nmax = sb("nmax", [P, 4])
                rsum = sb("rsum", [P, T, H])
                rinv = sb("rinv", [P, T, H])
                ids = sb("ids", [P, 3 * T], I32)
                boff = sb("boff", [P, 1])
                pc3 = sb("pc3", [P, 8])
                gac = sb("gac", [P, T, 2 * D])
                bfT = gac[:].rearrange("p t f -> p (t f)")[:, 0:K2 * SLOTS].rearrange("p (m c) -> p m c", m=K2)
                gb = sb("gb", [P, T, 4 * D])
                gbf = gb[:].rearrange("p t f -> p (t f)")
                aT3 = gbf[:, 0:K2 * S].rearrange("p (m s) -> p m s", m=K2)
                hT = gbf[:, K2 * S:2 * K2 * S].rearrange("p (m s) -> p m s", m=K2)
                cat = sb("cat", [P, 8, S])
                disp = cat[:].rearrange("p n s -> p (n s)")[:, 0:T * SLOTS].rearrange("p (t c) -> p t c", t=T)
                nA = sb("nA", [P, T, D])
                nB = sb("nB", [P, T, D])
                stat = sb("stat", [P, T, 6])
                mv = sb("mv", [P, T, 4])
                pe8 = sb("pe8", [P, 8, T, E])
                sm = sb("sm", [P, 16, T])
                gi = sb("gi", [P, 4, T])
                units = [(h, i) for h in range(H) for i in range(T)]
                N = len(units)
                SIDE = (6, 7)

                def iteration(b1, b2, b3):
                    lctx = ExitStack()
                    with lctx:
                        s = Sems(lctx, "a")

                        def interleave(unit, *streams):
                            live = [(g, next(g, None)) for g in streams]
                            for u in range(N):
                                if b2 is not None:
                                    unit(u)
                                for n, (g, due) in enumerate(live):
                                    while due is not None and due <= u:
                                        due = next(g, None)
                                    live[n] = (g, due)
                            assert all(due is None for _, due in live)

                        with nc.Block() as block:
                            @block.sync
                            def _(sp):
                                if b1 is not None:
                                    sp.dma_start(xT, a["xT"][b1].rearrange("p m s -> p m s")).then_inc(s("x_in"), 16)
                                    sp.dma_start(demk[:], spread(prow_d[b1, 0:D], 0, P)).then_inc(s("x_in"), 16)
                                if b3 is not None:
                                    sp.dma_start(ids[:], a["ids"][b3]).then_inc(s("ids_in"), 16)
                                    sp.dma_start(boff[:], spread(a["boff"][b3, :], 0, P)).then_inc(s("ids_in"), 16)
                                if b2 is not None:
                                    sp.dma_start(xN[:], a["xN"][b2]).then_inc(s("xn_in"), 16)
                                if b3 is not None:
                                    sp.wait_ge(s("gi_ok"), 1)
                                    sp.dma_start(gate_d[b3], gi[:].rearrange("p k t -> p (k t)")).then_inc(s("out3"), 16)
                                    for m in range(K2):
                                        sp.wait_ge(s("bf_ok"), 2 * m + 2)
                                        sp.dma_start(buf_d[:, :, m, b3, :].rearrange("e p c -> p e c"),
                                                     bfT[:, m, :].rearrange("p (e c) -> p e c", c=CAP)).then_inc(s("out3"), 16)
                                if b2 is not None:
                                    sp.wait_ge(s("x1_ok"), 1)
                                    sp.dma_start(x1_d[b2], x1[:]).then_inc(s("x1_out"), 16)
                                    sp.wait_ge(s("x1_out"), 16)
                                if b3 is not None:
                                    sp.wait_ge(s("out3"), 48)

                            @block.gpsimd
                            def _(pool):
                                def gather(src, dst, k):
                                    for t in range(T):
                                        if k:
                                            pool.wait_ge(s(f"gath{t}"), 16 * k)
                                        pool.indirect_dma_start(
                                            out=dst[:, t, :], out_offset=None, in_=src,
                                            in_offset=bass.IndirectOffsetOnAxis(ap=ids[:, k * T + t:k * T + t + 1].bitcast(U32), axis=0))\
                                            .then_inc(s(f"gath{t}"), 16)

                                if b2 is not None:
                                    pool.memset(cT[:, :, 0:1], 0.0).then_inc(s("c0_ok"), 1)
                                    pool.memset(qk[:, :, :, :, 28:32], 0.0).then_inc(s("pad_ok"), 1)
                                if b3 is not None:
                                    pool.wait_ge(s("ids_in"), 32)
                                    gather(a["pw"], gac, 0)
                                    gather(a["cptm"], gb, 1)
                                if b2 is not None:
                                    pool.wait_ge(s("vl_ok"), T)
                                    pool.tensor_tensor(vls[:, :, 0:D], vls[:, :, 0:D], spread(row("bv"), 1, T), ALU.add).then_inc(s("v_ok"), 1)
                                    pool.wait_ge(s("xn_in"), 16)
                                    pool.tensor_tensor(xN[:], xN[:], spread(row("bout"), 1, T), ALU.add).then_inc(s("xb_ok"), 1)
                                if b3 is not None:
                                    for t in range(T):
                                        pool.wait_ge(s(f"gath{t}"), 32)
                                    pool.wait_ge(s("z_ok"), T)
                                    tt, ss = gb[:, :, 2 * D:3 * D], gac[:, :, 0:D]
                                    pool.tensor_tensor(tt, nA[:], tt, ALU.mult).then_inc(s("pool_own"), 1)
                                    pool.wait_ge(s("pool_own"), 1)
                                    pool.tensor_tensor(tt, tt, gb[:, :, 3 * D:4 * D], ALU.add).then_inc(s("tt_ok"), 1)
                                    pool.wait_ge(s("h1_ok"), 1)
                                    gather(a["ms"], gac, 2)
                                    for t in range(T):
                                        pool.wait_ge(s(f"gath{t}"), 48)
                                    pool.tensor_tensor(ss, nA[:], ss, ALU.mult).then_inc(s("pool_own"), 1)
                                    pool.wait_ge(s("pool_own"), 2)
                                    pool.tensor_tensor(ss, ss, gac[:, :, D:2 * D], ALU.add).then_inc(s("ss_ok"), 1)
                                    for t in range(T):
                                        pool.dma_reset(range(s(f"gath{t}").num, s(f"gath{t}").num + 1))
                                if b1 is not None:
                                    pool.wait_ge(s("ex_ok"), 1)
                                    for t in range(T):
                                        if t:
                                            pool.wait_ge(s("pv_used"), 2 * t)
                                        kv = kx[:, t, 0:D].rearrange("p (h d) -> p h d", d=DH)
                                        pool.tensor_tensor(pv.rearrange("p o (h d) -> p o h d", d=DH),
                                                           spread(ex[:, t], 3, DH), spread(kv, 1, H, DH), ALU.mult)\
                                            .then_inc(s("pv_ok"), 1)

                            @block.tensor
                            def _(pe):
                                def token_stream():
                                    pe.wait_ge(s("x_in"), 32)
                                    pe.wait_ge(s("wk_ok"), 1)
                                    for t in range(T):
                                        for m in range(K2):
                                            mm = pe.matmul(bank[SIDE[t // 2]][:, (t % 2) * D:(t % 2 + 1) * D],
                                                           xT[:, m, t * P:(t + 1) * P], wk[:, m, :],
                                                           start=(m == 0), stop=(m == K2 - 1))
                                    mm.then_inc(s("kx_mm"), 1)
                                    yield AT["turn1"]
                                    pe.wait_ge(s("on_ok"), 1)
                                    if b3 is not None:
                                        pe.wait_ge(s("bf_ok"), 4)
                                    for m in range(K2):
                                        for t in range(T):
                                            mm = pe.transpose(bank[SIDE[m]][:, t * P:(t + 1) * P], nA1[:, t, m * P:(m + 1) * P], ident[:])
                                        mm.then_inc(s("aT_mm"), 1)
                                    yield AT["turn1"] + 2
                                    pe.wait_ge(s("aT_ok"), 2)
                                    for o in range(K2):
                                        for m in range(K2):
                                            mm = pe.matmul(bank[SIDE[o]][:], wo[:, m, o * P:(o + 1) * P], aT1[:, m, :],
                                                           start=(m == 0), stop=(m == K2 - 1))
                                        mm.then_inc(s("c_mm"), 1)

                                def router_stream():
                                    yield AT["x"]
                                    srcs = ((x1, None, "x"), (gb[:, :, 2 * D:3 * D], "tt_ok", "t"), (nB, "h_ok", "h"),
                                            (gac[:, :, 0:D], "ss_ok", "s"))
                                    for n, (src, ready, at) in enumerate(srcs):
                                        yield AT[at]
                                        if ready:
                                            pe.wait_ge(s(ready), 1)
                                            pe.wait_ge(s("cat_ok"), 2 * n)
                                        elif b1 is not None:
                                            pe.wait_ge(s("kx_half"), 1)
                                        for m in range(K2):
                                            for t in range(T):
                                                mm = pe.transpose(bank[SIDE[m]][:, t * P:(t + 1) * P], src[:, t, m * P:(m + 1) * P], ident[:])
                                            mm.then_inc(s("cat_mm"), 1)
                                    yield AT["u"]
                                    pe.wait_ge(s("cat_ok"), 8)
                                    order = (0, 1, 4, 5, 6, 7, 2, 3)
                                    for o in range(K2):
                                        for n in range(8):
                                            mm = pe.matmul(bank[SIDE[o]][:], wint[:, order[n], o * P:(o + 1) * P], cat[:, n, :],
                                                           start=(n == 0), stop=(n == 7))
                                            if n == 3:
                                                yield AT["u"] + 2 * o + 1
                                        mm.then_inc(s("u_mm"), 1)
                                        yield AT["u"] + 2 * o + 2
                                    yield AT["y"]
                                    pe.wait_ge(s("u_ok"), 2)
                                    for t in range(T):
                                        for m in range(K2):
                                            mm = pe.matmul(bank[SIDE[t // 2]][:, (t % 2) * D:(t % 2 + 1) * D], aT3[:, m, t * P:(t + 1) * P],
                                                           wint2[:, m, :], start=(m == 0), stop=(m == K2 - 1))
                                    mm.then_inc(s("y_mm"), 1)
                                    yield AT["f"]
                                    pe.wait_ge(s("f_ok"), 1)
                                    for m in range(K2):
                                        for t in range(T):
                                            mm = pe.transpose(bank[SIDE[m]][:, t * P:(t + 1) * P], nB[:, t, m * P:(m + 1) * P], ident[:])
                                        mm.then_inc(s("fT_mm"), 1)
                                    yield AT["f"] + 2
                                    pe.wait_ge(s("fT_ok"), 2)
                                    for t in range(T):
                                        for m in range(K2):
                                            mm = pe.matmul(bank[SIDE[0]][:, t * E:(t + 1) * E], hT[:, m, t * P:(t + 1) * P], wr[:, m, :],
                                                           start=(m == 0), stop=(m == K2 - 1))
                                    mm.then_inc(s("r_mm"), 1)
                                    yield AT["pos"]
                                    pe.wait_ge(s("pick_ok"), 1)
                                    for t in range(T):
                                        for j in range(t + 1):
                                            mm = pe.matmul(bank[SIDE[1]][:, t * E:(t + 1) * E], (tri if j == t else ones)[:], pe8[:, 5, j, :],
                                                           start=(j == 0), stop=(j == t))
                                    mm.then_inc(s("pos_mm"), 1)
                                    w = SLOTS // 2
                                    for m in range(K2):
                                        for c in range(2):
                                            yield AT["disp"] + 3 * m + c
                                            pe.wait_ge(s("disp_ok"), T)
                                            if m:
                                                pe.wait_ge(s("bf_ok"), c + 1)
                                            for t in range(T):
                                                mm = pe.matmul(bank[SIDE[c]][:, 0:w], nB[:, t, m * P:(m + 1) * P],
                                                               disp[:, t, c * w:(c + 1) * w], start=(t == 0), stop=(t == T - 1))
                                            mm.then_inc(s("bf_mm"), 1)

                                def project():
                                    pe.wait_ge(s("c0_ok"), 1)
                                    for t in range(T):
                                        if t >= 2:
                                            pe.wait_ge(s("qk_ev"), t - 1)
                                            pe.wait_ge(s("vl_ok"), t - 1)
                                        bq, bl = bank[2 * (t % 2)], bank[2 * (t % 2) + 1]
                                        now = lambda m: cT[:, m, 1 + t * P:1 + (t + 1) * P]
                                        before = lambda m: cT[:, m, t * P:(t + 1) * P]
                                        for lo, hi, at in ((0, 320, now), (320, 384, before), (384, 512, now)):
                                            for m in range(K2):
                                                mm = pe.matmul(bl[:, lo:hi], at(m), wvl[:, m, lo:hi],
                                                               start=(m == 0), stop=(m == K2 - 1))
                                        mm.then_inc(s("vl_mm"), 1)
                                        for m in range(K2):
                                            mm = pe.matmul(bq[:], now(m), wqk[:, m, :], start=(m == 0), stop=(m == K2 - 1))
                                        mm.then_inc(s("qk_mm"), 1)

                                def turn_features():
                                    pe.wait_ge(s("qk_ok"), 1)
                                    pe.wait_ge(s("pad_ok"), 1)
                                    for g in range(HG):
                                        for side in range(2):
                                            n = 2 * g + side
                                            if n >= 4:
                                                pe.wait_ge(s("qkT_ok"), n - 3)
                                            for t in range(T):
                                                src = qk[:, t, side, HG * g:HG * g + HG, :].rearrange("p h r -> p (h r)")
                                                mm = pe.transpose(bank[n % 4][:, t * P:(t + 1) * P], src, ident[:])
                                            mm.then_inc(s("qkT_mm"), 1)
                                    pe.wait_ge(s("qkT_ok"), 8)
                                    pe.wait_ge(s("v_ok"), 1)

                                def score(u):
                                    h, i = units[u]
                                    g, r = h // HG, 32 * (h % HG)
                                    if i == 0:
                                        if h:
                                            pe.wait_ge(s("dbias_ok"), h)
                                        for j in range(T):
                                            mm = pe.matmul(bank[2][:, j * P:(j + 1) * P], qT[r:r + 32, g, j * P:(j + 1) * P],
                                                           kiT[r:r + 32, g, j * P:(j + 1) * P], start=True, stop=True)
                                        mm.then_inc(s("inc_mm"), 1)
                                    if u >= 2:
                                        pe.wait_ge(s("exp_ok"), u - 1)
                                    lg = bank[u % 2]
                                    q = lambda n: qT[r:r + n, g, i * P:(i + 1) * P]
                                    for j in range(i):
                                        kk = (k0T, k1T, k2T)[i - 1 - j]
                                        pe.matmul(lg[:, j * P:(j + 1) * P], q(32), kk[r:r + 32, g, j * P:(j + 1) * P],
                                                  start=True, stop=True)
                                    pe.matmul(lg[:, i * P:(i + 1) * P], q(DH), k0T[r:r + DH, g, i * P:(i + 1) * P],
                                              start=True, stop=False)
                                    pe.matmul(lg[:, i * P:(i + 1) * P], identb[:], negb[:], start=False, stop=True)\
                                        .then_inc(s("score_mm"), 1)

                                def turn(u):
                                    h, i = units[u]
                                    pe.wait_ge(s("exp_ok"), u + 1)
                                    if u >= 2:
                                        pe.wait_ge(s("prT_ok"), u - 1)
                                    for j in range(i + 1):
                                        mm = pe.transpose(bank[3 + u % 2][:, j * P:(j + 1) * P], pr[:, u % 3, j * P:(j + 1) * P], ident[:])
                                    mm.then_inc(s("turn_mm"), 1)

                                def values(u):
                                    h, i = units[u]
                                    pe.wait_ge(s("prT_ok"), u + 1)
                                    if u == N // 2:
                                        pe.wait_ge(s("half_ok"), 1)
                                    o = bank[5][:, i * P + (h % 8) * DH:i * P + (h % 8 + 1) * DH]
                                    for j in range(i + 1):
                                        mm = pe.matmul(o, prT[:, u % 3, j * P:(j + 1) * P], vls[:, j, h * DH:(h + 1) * DH],
                                                       start=(j == 0), stop=(j == i))
                                    mm.then_inc(s("val_mm"), 1)

                                def unit(u):
                                    turn(u)
                                    if u + 2 < N:
                                        score(u + 2)
                                    if u >= 1:
                                        values(u - 1)

                                side = [g for g, on in ((token_stream(), b1), (router_stream(), b3)) if on is not None]
                                if b2 is not None:
                                    project()
                                if b1 is not None:
                                    first = next(side[0])
                                if b2 is not None:
                                    turn_features()
                                    score(0)
                                    score(1)
                                if b1 is not None:
                                    side[0] = resume(side[0], first)
                                interleave(unit, *side)
                                if b2 is not None:
                                    values(N - 1)
                                    pe.wait_ge(s("att_ok"), 1)
                                    for m in range(K2):
                                        for t in range(T):
                                            mm = pe.transpose(bank[m][:, t * P:(t + 1) * P], nA2[:, t, m * P:(m + 1) * P], ident[:])
                                        mm.then_inc(s("oT_mm"), 1)
                                    pe.wait_ge(s("oT_ok"), 2)
                                    for t in range(T):
                                        for m in range(K2):
                                            mm = pe.matmul(bank[2 + t // 2][:, (t % 2) * D:(t % 2 + 1) * D], aT2[:, m, t * P:(t + 1) * P],
                                                           wout[:, m, :], start=(m == 0), stop=(m == K2 - 1))
                                    mm.then_inc(s("out_mm"), 1)

                            @block.scalar
                            def _(act):
                                done, settle = chain_of(act, s("act_own"))

                                def token_stream():
                                    yield AT["kx"] + 1
                                    act.wait_ge(s("kx_half"), 1)
                                    act.copy(kx[:, :, D:2 * D], kx[:, :, 0:D]).then_inc(s("kx_dup"), 1)
                                    yield AT["full"]
                                    act.wait_ge(s("sc_low"), T)
                                    done(act.copy(sc[:, :, 1:8, H:2 * H], sc[:, :, 1:8, 0:H]))
                                    settle()
                                    for d in range(1, 8):
                                        last = act.copy(sc[:, :, H - d, 0:H], sc[:, :, d, H - d:2 * H - d])
                                    last.then_inc(s("sc_full"), 1)
                                    yield AT["full"] + 2
                                    act.wait_ge(s("ex_in"), 1)
                                    act.activation(ex[:], ex[:], ACT.Exp, scale=0.25).then_inc(s("ex_ok"), 1)
                                    yield AT["turn1"] + 1
                                    for m in range(K2):
                                        act.wait_ge(s("aT_mm"), m + 1)
                                        act.copy(aT1[:, m, :], bank[SIDE[m]][:]).then_inc(s("aT_ok"), 1)
                                    yield AT["turn1"] + 3
                                    act.wait_ge(s("wk_ok"), 1)
                                    if b2 is not None:
                                        act.wait_ge(s("qk_mm"), T)
                                    for o in range(K2):
                                        act.wait_ge(s("c_mm"), o + 1)
                                        act.activation(cT[:, o, 1:S + 1], bank[SIDE[o]][:], ACT.Identity,
                                                       bias=obcol[:, o:o + 1], scale=pc1[:, 4 + o:5 + o])

                                def router_stream():
                                    sd = lambda n: act.activation(mv[:, :, 2:3], mv[:, :, 1:2], ACT.Sqrt, bias=eps_ln[:, 0:1])\
                                        .then_inc(s(f"sd{n}"), 1)

                                    def out_of_bank(n):
                                        for m in range(K2):
                                            act.wait_ge(s("cat_mm"), 2 * n + m + 1)
                                            act.copy(cat[:, 2 * n + m, :], bank[SIDE[m]][:]).then_inc(s("cat_ok"), 1)

                                    yield AT["z"] + 1
                                    act.wait_ge(s("var1"), 1)
                                    sd(1)
                                    yield AT["x"] + 1
                                    out_of_bank(0)
                                    yield AT["h2"] + 1
                                    act.wait_ge(s("var2"), 1)
                                    sd(2)
                                    yield AT["t"] + 1
                                    out_of_bank(1)
                                    yield AT["h"] + 1
                                    out_of_bank(2)
                                    yield AT["s"] + 1
                                    out_of_bank(3)
                                    yield AT["u"] + 5
                                    for o in range(K2):
                                        act.wait_ge(s("u_mm"), o + 1)
                                        act.activation(aT3[:, o, :], bank[SIDE[o]][:], ACT.Silu, bias=pc3[:, 6 + o:7 + o]).then_inc(s("u_ok"), 1)
                                    yield AT["y"] + 3
                                    act.wait_ge(s("var3"), 1)
                                    sd(3)
                                    yield AT["f"] + 1
                                    for m in range(K2):
                                        act.wait_ge(s("fT_mm"), m + 1)
                                        act.copy(hT[:, m, :], bank[SIDE[m]][:]).then_inc(s("fT_ok"), 1)
                                    yield AT["f"] + 4
                                    act.wait_ge(s("re_in"), 1)
                                    act.activation(pe8[:, 0], pe8[:, 0], ACT.Exp).then_inc(s("re_ok"), 1)
                                    w = SLOTS // 2
                                    for n in range(4):
                                        yield AT["disp"] + 3 * (n // 2) + n % 2 + 1
                                        act.wait_ge(s("bf_mm"), n + 1)
                                        act.copy(bfT[:, n // 2, (n % 2) * w:(n % 2 + 1) * w], bank[SIDE[n % 2]][:, 0:w]).then_inc(s("bf_ok"), 1)

                                def exps(u):
                                    h, i = units[u]
                                    n = (i + 1) * P
                                    act.wait_ge(s("max_ok"), u + 1)
                                    if u >= 3:
                                        act.wait_ge(s("turn_mm"), u - 2)
                                    act.activation(pr[:, u % 3, 0:n], bank[u % 2][:, 0:n], ACT.Exp, bias=nmax[:, u % 4:u % 4 + 1],
                                                   accum_out=rsum[:, i, h:h + 1]).then_inc(s("exp_ok"), 1)

                                def turned(u):
                                    n = (units[u][1] + 1) * P
                                    act.wait_ge(s("turn_mm"), u + 1)
                                    if u >= 3:
                                        act.wait_ge(s("val_mm"), u - 2)
                                    act.copy(prT[:, u % 3, 0:n], bank[3 + u % 2][:, 0:n]).then_inc(s("prT_ok"), 1)

                                def unit(u):
                                    if u + 1 < N:
                                        exps(u + 1)
                                    turned(u)

                                if b2 is not None:
                                    for t in range(T):
                                        act.wait_ge(s("vl_mm"), t + 1)
                                        act.copy(vls[:, t, :], bank[2 * (t % 2) + 1][:]).then_inc(s("vl_ok"), 1)
                                    act.wait_ge(s("len2"), 1)
                                    act.activation(ln[:], ln[:], ACT.Sqrt).then_inc(s("len_ok"), 1)
                                    for g in range(HG):
                                        act.wait_ge(s("qkT_mm"), 2 * g + 1)
                                        act.copy(qT[:, g, :], bank[(2 * g) % 4][:]).then_inc(s("qkT_ok"), 1)
                                        act.wait_ge(s("qkT_mm"), 2 * g + 2)
                                        src = bank[(2 * g + 1) % 4]
                                        act.activation(k0T[:, g, :], src[:], ACT.Copy, scale=fack[:, g, 0:1])
                                        act.activation(k1T[:, g, :], src[:, 0:2 * P], ACT.Copy, scale=fack[:, g, 1:2])
                                        act.activation(k2T[:, g, :], src[:, 0:P], ACT.Copy, scale=fack[:, g, 2:3])
                                        act.activation(kiT[:, g, :], src[:], ACT.Copy, scale=fack[:, g, 3:4]).then_inc(s("qkT_ok"), 1)
                                    exps(0)
                                side = [g for g, on in ((token_stream(), b1), (router_stream(), b3)) if on is not None]
                                interleave(unit, *side)
                                if b2 is not None:
                                    for m in range(K2):
                                        act.wait_ge(s("oT_mm"), m + 1)
                                        act.copy(aT2[:, m, :], bank[m][:]).then_inc(s("oT_ok"), 1)

                            @block.vector
                            def _(dve):
                                done, settle = chain_of(dve, s("dve_own"))

                                def token_weights():
                                    done(dve.tensor_copy(pc1[:], pcol[:, b1, :]))
                                    settle()
                                    for m in range(K2):
                                        done(dve.tensor_scalar(wk[:, m, :], kow[:, 0, m, :], pc1[:, m:m + 1], None, ALU.mult))
                                        dve.tensor_scalar(wo[:, m, :], kow[:, 1, m, :], pc1[:, 2 + m:3 + m], None, ALU.mult)
                                    settle()
                                    dve.wait_ge(s("x_in"), 32)
                                    dve.tensor_tensor(wk, wk, spread(demk[:], 1, K2), ALU.mult).then_inc(s("wk_ok"), 1)

                                def token_stream():
                                    yield AT["kx"]
                                    dve.wait_ge(s("kx_mm"), 1)
                                    for c in range(2):
                                        last = dve.tensor_tensor(kx[:, 2 * c:2 * c + 2, 0:D],
                                                                 bank[SIDE[c]][:].rearrange("p (t f) -> p t f", t=2),
                                                                 spread(row("kb"), 1, 2), ALU.add)
                                    last.then_inc(s("kx_half"), 1)
                                    for t in range(T):
                                        yield AT["pair"] + 4 * t
                                        dve.wait_ge(s("kx_dup"), 1)
                                        k0 = kx[:, t, 0:D]
                                        if t:
                                            dve.wait_ge(s("sc_low"), t)
                                        done(dve.tensor_tensor(prod, spread(k0, 1, 9), spread(k0, 1, 9, DH), ALU.mult))
                                        yield AT["pair"] + 4 * t + 2
                                        settle()
                                        dve.tensor_reduce(sc[:, t, 0:9, 0:H], prod.rearrange("p o (h d) -> p o h d", d=DH),
                                                          X, ALU.add).then_inc(s("sc_low"), 1)
                                    yield AT["full"] + 1
                                    dve.wait_ge(s("sc_full"), 1)
                                    for t in range(T):
                                        done(dve.tensor_reduce(mx[:, t, :], sc[:, t, :, 0:H].rearrange("p o h -> p h o"), X, ALU.max))
                                    settle()
                                    for t in range(T):
                                        last = dve.tensor_tensor(ex[:, t], sc[:, t, :, 0:H], spread(mx[:, t, :], 1, H), ALU.subtract)
                                    last.then_inc(s("ex_in"), 1)
                                    yield AT["full"] + 3
                                    dve.wait_ge(s("ex_ok"), 1)
                                    for t in range(T):
                                        done(dve.tensor_reduce(mx[:, t, :], ex[:, t].rearrange("p o h -> p h o"), X, ALU.add))
                                    settle()
                                    done(dve.reciprocal(rs[:], mx[:]))
                                    for t in range(T):
                                        for c in range(2):
                                            yield AT["full"] + 6 + 5 * t + c
                                            dve.wait_ge(s("pv_ok"), t + 1)
                                            dve.tensor_reduce(nA1[:, t, c * P:(c + 1) * P], pv[:, :, c * P:(c + 1) * P].rearrange("p o f -> p f o"),
                                                              X, ALU.add).then_inc(s("pv_used"), 1)
                                    yield AT["turn1"] - 1
                                    settle()
                                    dve.wait_ge(s("pv_used"), 2 * T)
                                    nv = nA1.rearrange("p t (h d) -> p (t h) d", d=DH)
                                    dve.tensor_tensor(nv, nv, spread(rs[:].rearrange("p t h -> p (t h)"), 2, DH), ALU.mult)\
                                        .then_inc(s("on_ok"), 1)

                                def moments(src, var):
                                    for t in range(T):
                                        done(dve.bn_stats(stat[:, t, :], src[:, t, :]))
                                    settle()
                                    for t in range(T):
                                        last = dve.bn_aggr(mv[:, t, 0:2], stat[:, t, :])
                                    last.then_inc(s(var), 1)

                                def normed(dst, src, sd, ready=None):
                                    dve.wait_ge(s(sd), 1)
                                    done(dve.reciprocal(mv[:, :, 3:4], mv[:, :, 2:3]))
                                    settle()
                                    for t in range(T):
                                        ins = dve.tensor_scalar(dst[:, t, :], src[:, t, :], mv[:, t, 0:1], mv[:, t, 3:4],
                                                                ALU.subtract, ALU.mult)
                                        ins.then_inc(s(ready), 1) if ready else done(ins)
                                    if ready:
                                        dve.wait_ge(s(ready), T)
                                    else:
                                        settle()

                                def affine(dst, src, gain, off, ready=None):
                                    done(dve.tensor_tensor(dst[:], src, gain, ALU.mult))
                                    settle()
                                    ins = dve.tensor_tensor(dst[:], dst[:], off, ALU.add)
                                    ins.then_inc(s(ready), 1) if ready else done(ins)
                                    if ready:
                                        dve.wait_ge(s(ready), 1)
                                    else:
                                        settle()

                                def router_stream():
                                    yield AT["z"]
                                    done(dve.tensor_copy(pc3[:], pcol[:, b3, :]))
                                    moments(x1, "var1")
                                    yield AT["z"] + 2
                                    normed(nA, x1, "sd1", "z_ok")
                                    yield AT["h1"]
                                    for t in range(T):
                                        dve.wait_ge(s(f"gath{t}"), 16)
                                    affine(nB, nA[:], gac[:, :, 0:D], gac[:, :, D:2 * D], "h1_ok")
                                    yield AT["h2"]
                                    moments(nB, "var2")
                                    yield AT["h2"] + 2
                                    normed(nB, nB, "sd2")
                                    for t in range(T):
                                        dve.wait_ge(s(f"gath{t}"), 32)
                                    affine(nB, nB[:], gb[:, :, 0:D], gb[:, :, D:2 * D], "h_ok")
                                    yield AT["y"] + 1
                                    dve.wait_ge(s("y_mm"), 1)
                                    for c in range(2):
                                        done(dve.tensor_tensor(nB[:, 2 * c:2 * c + 2, :], bank[SIDE[c]][:].rearrange("p (t f) -> p t f", t=2),
                                                               spread(row("b2"), 1, 2), ALU.add))
                                    settle()
                                    yield AT["y"] + 2
                                    moments(nB, "var3")
                                    yield AT["y"] + 4
                                    normed(nB, nB, "sd3")
                                    yield AT["y"] + 5
                                    affine(nB, nB[:], spread(row("g"), 1, T), spread(row("be"), 1, T), "f_ok")
                                    q = lambda k: pe8[:, k]
                                    step = lambda ins: (done(ins), settle())
                                    yield AT["f"] + 3
                                    dve.wait_ge(s("r_mm"), 1)
                                    step(dve.tensor_tensor(q(0), bank[SIDE[0]][:, 0:T * E].rearrange("p (t e) -> p t e", e=E),
                                                           spread(row("br"), 1, T), ALU.add))
                                    step(dve.tensor_reduce(sm[:, 0], q(0), X, ALU.max))
                                    dve.tensor_tensor(q(0), q(0), spread(sm[:, 0], 2, E), ALU.subtract).then_inc(s("re_in"), 1)
                                    yield AT["f"] + 5
                                    dve.wait_ge(s("re_ok"), 1)
                                    step(dve.tensor_reduce(sm[:, 1], q(0), X, ALU.add))
                                    step(dve.reciprocal(sm[:, 1], sm[:, 1]))
                                    step(dve.tensor_tensor(q(0), q(0), spread(sm[:, 1], 2, E), ALU.mult))
                                    io = spread(iota[:, 0:E], 1, T)
                                    for k in range(2):
                                        yield AT["f"] + 6 + k
                                        pk, mk, ix, oh = q(0 if k == 0 else 3), sm[:, 2 + k], sm[:, 4 + k], q(1 + k)
                                        step(dve.tensor_reduce(mk, pk, X, ALU.max))
                                        step(dve.tensor_tensor(q(4), pk, spread(mk, 2, E), ALU.is_ge))
                                        step(dve.tensor_scalar(q(4), q(4), -float(E), float(E), ALU.mult, ALU.add))
                                        step(dve.tensor_tensor(q(4), q(4), io, ALU.add))
                                        step(dve.tensor_reduce(ix, q(4), X, ALU.min))
                                        step(dve.tensor_tensor(oh, io, spread(ix, 2, E), ALU.is_equal))
                                        if k == 0:
                                            step(dve.tensor_scalar(q(4), oh, -2.0, None, ALU.mult))
                                            step(dve.tensor_tensor(q(3), pk, q(4), ALU.add))
                                    dve.tensor_tensor(q(5), q(1), q(2), ALU.add).then_inc(s("pick_ok"), 1)
                                    yield AT["pos"] + 1
                                    dve.wait_ge(s("pos_mm"), 1)
                                    step(dve.tensor_copy(q(6), bank[SIDE[1]][:, 0:T * E].rearrange("p (t e) -> p t e", e=E)))
                                    for k in range(2):
                                        yield AT["pos"] + 1 + k
                                        at, keep, slot = sm[:, 6 + k], sm[:, 8 + k], sm[:, 10 + k]
                                        step(dve.tensor_tensor(q(7), q(6), q(1 + k), ALU.mult))
                                        step(dve.tensor_reduce(at, q(7), X, ALU.add))
                                        step(dve.tensor_scalar(keep, at, float(CAP), None, ALU.is_lt))
                                        step(dve.tensor_scalar(at, at, float(CAP - 1), None, ALU.min))
                                        step(dve.tensor_scalar(slot, sm[:, 4 + k], float(CAP), 1.0, ALU.mult, ALU.add))
                                        step(dve.tensor_tensor(slot, slot, at, ALU.add))
                                        step(dve.tensor_tensor(slot, slot, keep, ALU.mult))
                                        step(dve.tensor_scalar(slot, slot, -1.0, None, ALU.add))
                                        if k == 0:
                                            dve.wait_ge(s("ids_in"), 32)
                                        done(dve.tensor_tensor(gi[:, k], sm[:, 2 + k], keep, ALU.mult))
                                        step(dve.tensor_scalar(sm[:, 12], sm[:, 4 + k], float(ROWS), boff[:, 0:1], ALU.mult, ALU.add))
                                        last = dve.tensor_tensor(gi[:, 2 + k], sm[:, 12], at, ALU.add)
                                        if k == 0:
                                            step(last)
                                        else:
                                            last.then_inc(s("gi_ok"), 1)
                                    for t in range(T):
                                        yield AT["disp"] - T + t
                                        step(dve.tensor_scalar(disp[:, t, :], iota[:], sm[:, 10, t:t + 1], None, ALU.is_equal))
                                        dve.scalar_tensor_tensor(disp[:, t, :], iota[:], sm[:, 11, t:t + 1], disp[:, t, :],
                                                                 ALU.is_equal, ALU.add).then_inc(s("disp_ok"), 1)

                                def features():
                                    for t in range(T):
                                        dve.wait_ge(s("qk_mm"), t + 1)
                                        dve.tensor_tensor(qk[:, t, :, :, 0:DH].rearrange("p s h d -> p (s h) d"),
                                                          bank[2 * (t % 2)][:].rearrange("p (s d) -> p s d", d=DH),
                                                          row("bqk").rearrange("p (s d) -> p s d", d=DH), ALU.add)\
                                            .then_inc(s("qk_ev"), 1)
                                    dve.wait_ge(s("vl_ok"), T)
                                    pa = vls[:, :, D:D + P].rearrange("p t (s c) -> p t s c", c=4)
                                    pb = vls[:, :, D + P:D + 2 * P].rearrange("p t (s c) -> p t s c", c=4)
                                    for dst, u, v in ((la, pa, pb), (lb, pb, pa)):
                                        for c, lo, n in ((0, 0, 3), (1, 3, 2), (2, 5, 1)):
                                            done(dve.tensor_tensor(dst[:, :, :, lo:lo + n], spread(u[:, :, :, c], 3, n), v[:, :, :, c + 1:4], ALU.mult))
                                    settle()
                                    done(dve.tensor_tensor(la, la, lb, ALU.subtract))
                                    settle()
                                    done(dve.tensor_tensor(lb, la, la, ALU.mult))
                                    settle()
                                    dve.tensor_reduce(ln[:], lb, X, ALU.add).then_inc(s("len2"), 1)
                                    done(dve.tensor_tensor(la, la, spread(sign[:], 1, T), ALU.mult))
                                    dve.wait_ge(s("len_ok"), 1)
                                    done(dve.tensor_scalar(ln[:], ln[:], 1e-12, None, ALU.max))
                                    settle()
                                    done(dve.reciprocal(ln[:], ln[:]))
                                    settle()
                                    done(dve.tensor_tensor(lf[:, 0], ln[:, :, 0:H], spread(facr[:], 1, T), ALU.mult))
                                    done(dve.tensor_tensor(lf[:, 1], ln[:, :, 0:H], spread(row("bs"), 1, T), ALU.mult))
                                    done(dve.tensor_tensor(lf[:, 2], ln[:, :, H:2 * H], spread(facw[:], 1, T), ALU.mult))
                                    done(dve.tensor_copy(lf[:, 3], ln[:, :, H:2 * H]))
                                    settle()
                                    for n in range(4):
                                        side, at = n // 2, DH + NOFF * (n % 2)
                                        src = la[:, :, H * side:H * side + H, :]
                                        if side:
                                            src = src[:, :, :, ::-1]
                                        for t in range(T):
                                            last = dve.tensor_tensor(qk[:, t, side, :, at:at + NOFF], src[:, t],
                                                                     spread(lf[:, n, t, :], 2, NOFF), ALU.mult)
                                    last.then_inc(s("qk_ok"), 1)

                                def heads_out(c):
                                    dve.wait_ge(s("exp_ok"), (c + 1) * N // 2)
                                    done(dve.reciprocal(rinv[:, :, 8 * c:8 * c + 8], rsum[:, :, 8 * c:8 * c + 8]))
                                    settle()
                                    dve.wait_ge(s("val_mm"), (c + 1) * N // 2)
                                    for t in range(T):
                                        last = dve.tensor_tensor(nA2[:, t, c * P:(c + 1) * P].rearrange("p (h d) -> p h d", d=DH),
                                                                 bank[5][:, t * P:(t + 1) * P].rearrange("p (h d) -> p h d", d=DH),
                                                                 spread(rinv[:, t, 8 * c:8 * c + 8], 2, DH), ALU.mult)
                                    last.then_inc(s("att_ok" if c else "half_ok"), 1)

                                def unit(u):
                                    h, i = units[u]
                                    if i == 0:
                                        dve.wait_ge(s("inc_mm"), h + 1)
                                        dve.tensor_tensor(dbias[:, h % 2], bank[2][:].rearrange("p (i k) -> p i k", k=P),
                                                          spread(wdiag[:, h, :], 1, T), ALU.mult).then_inc(s("dbias_ok"), 1)
                                        dve.wait_ge(s("dbias_ok"), h + 1)
                                    dve.wait_ge(s("score_mm"), u + 1)
                                    dg = bank[u % 2][:, i * P:(i + 1) * P]
                                    done(dve.tensor_tensor(dg, dg, dbias[:, h % 2, i, :], ALU.add))
                                    settle()
                                    if u >= 4:
                                        dve.wait_ge(s("exp_ok"), u - 3)
                                    dve.tensor_reduce(nmax[:, u % 4:u % 4 + 1], bank[u % 2][:, 0:(i + 1) * P], X, ALU.max,
                                                      negate=True).then_inc(s("max_ok"), 1)
                                    if u == N // 2 + 1:
                                        heads_out(0)

                                if b1 is not None:
                                    token_weights()
                                if b2 is not None:
                                    features()
                                side = [g for g, on in ((token_stream(), b1), (router_stream(), b3)) if on is not None]
                                interleave(unit, *side)
                                if b2 is not None:
                                    heads_out(1)
                                    dve.wait_ge(s("out_mm"), 1)
                                    dve.wait_ge(s("xb_ok"), 1)
                                    if b3 is not None:
                                        dve.wait_ge(s("cat_mm"), 2)
                                    for c in range(2):
                                        last = dve.tensor_tensor(x1[:, 2 * c:2 * c + 2, :], bank[2 + c][:].rearrange("p (t f) -> p t f", t=2),
                                                                 xN[:, 2 * c:2 * c + 2, :], ALU.add)
                                    last.then_inc(s("x1_ok"), 1)
                        s.clear()

                if "A" in parts:
                    iteration(0, None, None)
                    iteration(1, 0, None)
                    with nc.Fori(1, B - 1) as b:
                        iteration(b + 1, b, b - 1)
                    iteration(None, B - 1, B - 2)
                    iteration(None, None, B - 1)

        def expert_loop():
            ctx = ExitStack()
            with ctx:
                sb = lambda name, shape, dt=F32: sb_in(ctx, name, shape, dt)
                ew1 = sb("ew1", [P, 2, K2, HID])
                ew2 = sb("ew2", [P, 2, KH, D])
                eb1 = sb("eb1", [P, 2, KH])
                eb2 = sb("eb2", [P, 2, D])
                eb = sb("eb", [P, 2, K2, ROWS])
                hid = sb("hid", [P, KH, ROWS])
                yy = sb("yy", [P, 2, ST, D])
                W = ROWS // 2
                with nc.Fori(0, E // 2) as e2:
                    sctx = ExitStack()
                    with sctx:
                        s = Sems(sctx, "e")
                        with nc.Block() as block:
                            @block.sync
                            def _(sp):
                                for k in range(2):
                                    for dst, src in ((ew1[:, k], a["eW1"][2 * e2 + k]), (eb[:, k].rearrange("p m r -> p (m r)"),
                                                     buf_d[2 * e2 + k].rearrange("p m b c -> p (m b c)")),
                                                     (eb1[:, k], a["eb1"][2 * e2 + k]), (ew2[:, k], a["eW2"][2 * e2 + k]),
                                                     (eb2[:, k], spread(a["eb2"][2 * e2 + k, :], 0, P))):
                                        sp.dma_start(dst, src).then_inc(s(f"w_in{k}"), 16)
                                for k in range(2):
                                    sp.wait_ge(s("y_ok"), ST * (k + 1))
                                    sp.dma_start(y_d.rearrange("(e t p) d -> e p t d", p=P, t=ST)[2 * e2 + k], yy[:, k]).then_inc(s("y_out"), 16)
                                sp.wait_ge(s("y_out"), 32)

                            @block.tensor
                            def _(pe):
                                for k in range(2):
                                    pe.wait_ge(s(f"w_in{k}"), 80)
                                    for n in range(2 * KH):
                                        o, c = n // 2, n % 2
                                        if k * 2 * KH + n >= 4:
                                            pe.wait_ge(s("h_ok"), k * 2 * KH + n - 3)
                                        for m in range(K2):
                                            mm = pe.matmul(bank[n % 4][:, 0:W], ew1[:, k, m, o * P:(o + 1) * P],
                                                           eb[:, k, m, c * W:(c + 1) * W], start=(m == 0), stop=(m == K2 - 1))
                                        mm.then_inc(s("h_mm"), 1)
                                    pe.wait_ge(s("h_ok"), 2 * KH * (k + 1))
                                    for t in range(ST):
                                        n = k * ST + t
                                        if n >= 4:
                                            pe.wait_ge(s("y_ok"), n - 3)
                                        for m in range(KH):
                                            mm = pe.matmul(bank[4 + n % 4][:, 0:D], hid[:, m, t * P:(t + 1) * P], ew2[:, k, m, :],
                                                           start=(m == 0), stop=(m == KH - 1))
                                        mm.then_inc(s("y_mm"), 1)

                            @block.scalar
                            def _(act):
                                for k in range(2):
                                    act.wait_ge(s(f"w_in{k}"), 80)
                                    if k:
                                        act.wait_ge(s("y_mm"), ST * k)
                                    for n in range(2 * KH):
                                        act.wait_ge(s("h_mm"), k * 2 * KH + n + 1)
                                        act.activation(hid[:, n // 2, (n % 2) * W:(n % 2 + 1) * W], bank[n % 4][:, 0:W], ACT.Relu,
                                                       bias=eb1[:, k, n // 2:n // 2 + 1]).then_inc(s("h_ok"), 1)

                            @block.vector
                            def _(dve):
                                for k in range(2):
                                    dve.wait_ge(s(f"w_in{k}"), 80)
                                    for t in range(ST):
                                        n = k * ST + t
                                        dve.wait_ge(s("y_mm"), n + 1)
                                        dve.tensor_tensor(yy[:, k, t, :], bank[4 + n % 4][:, 0:D], eb2[:, k, :], ALU.add)\
                                            .then_inc(s("y_ok"), 1)
                        s.clear()

        if "B" in parts:
            expert_loop()
        if "C" in parts:
            layer1(nc, a, out, bank, ident, sb_in, Sems, chain_of, x1_d, gate_d, y_d, prow_d, wdec_d, PR, R1, n1)


def layer1(nc, a, out, bank, ident, sb_in, Sems, chain_of, x1_d, gate_d, y_d, prow_d, wdec_d, PR, R1, n1):
    NP = H // 2
    V1 = DH + 1
    l1 = ExitStack()
    with l1:
        sb = lambda name, shape, dt=F32: sb_in(l1, name, shape, dt)
        dup = sb("dup", [P, K2, M])
        upp = sb("upp", [M, D])
        wqkv = sb("wqkv", [P, 3, K2, D])
        wo1 = sb("wo1", [P, K2, D])
        qkcol = sb("qkcol", [P, 2, K2])
        orfk = sb("orfk", [P, 2 * 256])
        nrmk = sb("nrmk", [P, 8])
        nrmq = sb("nrmq", [P, P])
        wq8 = sb("wq8", [P, K2, D // 4], I32)
        wqb = sb("wqb", [P, K2, D], BF16)
        rows = sb("rows1", [P, n1])
        identb = sb("identb1", [P, P], BF16)
        row = lambda f: rows[:, R1[f][0]:R1[f][1]]
        sctx = ExitStack()
        with sctx:
            s = Sems(sctx, "s1")
            with nc.Block() as block:
                @block.sync
                def _(sp):
                    loads = [(dup, "dup"), (upp, "upp"), (wqkv, "wqkv"), (wo1, "wo1"), (qkcol, "qkcol"), (orfk, "orfk"),
                             (nrmk, "nrmk"), (nrmq, "nrmq"), (identb, "identb"), (wq8, "wq8")]
                    for dst, name in loads:
                        sp.dma_start(dst[:], a[name]).then_inc(s("load"), 16)
                    sp.dma_start(rows[:], spread(a["rows1"], 0, P)).then_inc(s("load"), 16)
                    sp.wait_ge(s("load"), 16 * (len(loads) + 1))

                @block.vector
                def _(dve):
                    dve.wait_ge(s("load"), 16 * 11)
                    dve.tensor_copy(wqb[:], wq8[:].bitcast(I8)).then_inc(s("w_ok"), 1)
                    dve.tensor_scalar(orfk[:], orfk[:], 0.5, None, ALU.mult).then_inc(s("w_ok"), 1)
            s.clear()

        x2 = sb("x2", [P, T, D])
        gi = sb("gi1", [P, 4, T])
        gidx = sb("gidx", [P, 2, T], I32)
        yg = sb("yg", [P, 2, T, D])
        dgb = sb("dgb", [P, 2, M])
        ugb = sb("ugb", [M, 2, D])
        brow = sb("brow1", [P, D])
        wdn = sb("wdn", [P, K2, M])
        wup = sb("wup", [M, D])
        wde = sb("wde1", [P, K2, D])
        xT = sb("xT1", [P, K2, S])
        dT = sb("dT1", [M, S])
        hcT = sb("hcT", [P, K2, S])
        qT = sb("qT1", [P, K2, S])
        kT = sb("kT1", [P, K2, S])
        q2 = sb("q2", [P, K2, S])
        k2 = sb("k2", [P, K2, S])
        vn = sb("vn1", [P, T, H, V1])
        kn = sb("kn", [P, T, 2, 8])
        kf = sb("kf", [P, T, H, M])
        qf = sb("qf", [P, NP, S])
        kv = sb("kv", [P, NP, 2 * V1])
        den = sb("den", [P, T, H])
        on = sb("on", [P, T, D])
        xb = sb("xb1", [P, T, D])
        x3 = sb("x3", [P, T, D])
        ab = sb("ab", [P, 3, T])
        yq = sb("yq", [P, T, D])
        yb = sb("yb", [P, T, D], BF16)
        qbT = sb("qbT", [P, K2, S], BF16)
        fo = sb("fo", [P, T, D])

        def transposes(pe, src, banks, s, name):
            for m in range(K2):
                for t in range(T):
                    mm = pe.transpose(bank[banks[m]][:, t * P:(t + 1) * P], src[:, t, m * P:(m + 1) * P], ident[:])
                mm.then_inc(s(name), 1)

        with nc.Fori(0, B) as b:
            sctx = ExitStack()
            with sctx:
                s = Sems(sctx, "c")
                with nc.Block() as block:
                    @block.sync
                    def _(sp):
                        sp.dma_start(gi[:].rearrange("p k t -> p (k t)"), gate_d[b]).then_inc(s("gi_in"), 16)
                        sp.dma_start(x2[:], x1_d[b]).then_inc(s("x_in"), 16)
                        sp.dma_start(dgb[:].rearrange("p k h -> p (k h)"), spread(prow_d[b, PR["dg"][0]:PR["db"][1]], 0, P)).then_inc(s("p_in"), 16)
                        sp.dma_start(ugb[:].rearrange("p k h -> p (k h)"), spread(prow_d[b, PR["ug"][0]:PR["ub"][1]], 0, M)).then_inc(s("p_in"), 16)
                        sp.dma_start(brow[:], spread(prow_d[b, PR["bias"][0]:PR["bias"][1]], 0, P)).then_inc(s("p_in"), 16)
                        sp.dma_start(wde[:], wdec_d[b]).then_inc(s("p_in"), 16)
                        sp.wait_ge(s("fin"), 1)
                        sp.dma_start(out[b].rearrange("(t p) d -> p t d", p=P), fo[:]).then_inc(s("out"), 16)
                        sp.wait_ge(s("out"), 16)

                    @block.gpsimd
                    def _(pool):
                        pool.wait_ge(s("idx_ok"), 1)
                        for k in range(2):
                            for t in range(T):
                                pool.indirect_dma_start(out=yg[:, k, t, :], out_offset=None, in_=y_d,
                                                        in_offset=bass.IndirectOffsetOnAxis(ap=gidx[:, k, t:t + 1].bitcast(U32), axis=0))\
                                    .then_inc(s(f"y_in{k}{t}"), 16)
                        pool.memset(vn[:, :, :, DH:V1], 1.0).then_inc(s("one_ok"), 1)
                        pool.memset(kv[:], 0.0).then_inc(s("kv0"), 1)
                        pool.wait_ge(s("x2_ok"), 1)
                        pool.tensor_tensor(xb[:], x2[:], spread(row("bo"), 1, T), ALU.add).then_inc(s("xb_ok"), 1)
                        for n in range(8):
                            pool.wait_ge(s("kf_in"), n + 1)
                            pool.tensor_scalar(kf[:, n // 2, 8 * (n % 2):8 * (n % 2) + 8, :], kf[:, n // 2, 8 * (n % 2):8 * (n % 2) + 8, :],
                                               1e-6, None, ALU.add).then_inc(s("kf_ok"), 1)
                        for n in range(NP):
                            pool.wait_ge(s("qf_in"), n + 1)
                            pool.tensor_scalar(qf[:, n, :], qf[:, n, :], 1e-6, None, ALU.add).then_inc(s("qf_ok"), 1)
                        for k in range(2):
                            for t in range(T):
                                pool.wait_ge(s(f"y_in{k}{t}"), 16)
                                pool.dma_reset(range(s(f"y_in{k}{t}").num, s(f"y_in{k}{t}").num + 1))
                        pool.wait_ge(s("x3_ok"), 1)
                        pool.tensor_tensor(xb[:], x3[:], spread(row("bias"), 1, T), ALU.add).then_inc(s("x3b_ok"), 1)

                    @block.tensor
                    def _(pe):
                        pe.wait_ge(s("x2_ok"), 1)
                        transposes(pe, x2, (0, 1), s, "xT_mm")
                        pe.wait_ge(s("xT_ok"), 2)
                        pe.wait_ge(s("wud_ok"), 1)
                        for m in range(K2):
                            mm = pe.matmul(bank[2][0:M, :], wdn[:, m, :], xT[:, m, :], start=(m == 0), stop=(m == K2 - 1))
                        mm.then_inc(s("dn_mm"), 1)
                        pe.wait_ge(s("dn_ok"), 1)
                        for m in range(K2):
                            pe.matmul(bank[3 + m][:], wup[:, m * P:(m + 1) * P], dT[:], start=True, stop=True).then_inc(s("up_mm"), 1)
                        pe.wait_ge(s("hc_ok"), 2)
                        for n in range(4):
                            w, o = 1 - n // 2, n % 2
                            for m in range(K2):
                                mm = pe.matmul(bank[(5, 6, 7, 0)[n]][:], wqkv[:, w, m, o * P:(o + 1) * P], hcT[:, m, :],
                                               start=(m == 0), stop=(m == K2 - 1))
                            mm.then_inc(s("qk_mm"), 1)
                        for t in range(T):
                            for m in range(K2):
                                mm = pe.matmul(bank[1 + t // 2][:, (t % 2) * D:(t % 2 + 1) * D], hcT[:, m, t * P:(t + 1) * P],
                                               wqkv[:, 2, m, :], start=(m == 0), stop=(m == K2 - 1))
                        mm.then_inc(s("v_mm"), 1)
                        pe.wait_ge(s("sq_ok"), 2)
                        for t in range(T):
                            for m in range(K2):
                                mm = pe.matmul(bank[3][:, (2 * t + m) * 8:(2 * t + m + 1) * 8], k2[:, m, t * P:(t + 1) * P], nrmk[:],
                                               start=True, stop=True)
                        mm.then_inc(s("kn_mm"), 1)
                        for n in range(8):
                            t, m = n // 2, n % 2
                            if n >= 2:
                                pe.wait_ge(s("kf_sub"), n - 1)
                            pe.matmul(bank[4 + n % 2][:], kT[:, m, t * P:(t + 1) * P], orfk[:], start=True, stop=True)\
                                .then_inc(s("kf_mm"), 1)
                        pe.wait_ge(s("sq_ok"), 4)
                        for n in range(NP):
                            m, r = n // 4, 32 * (n % 4)
                            bk = (6, 7, 0)[n % 3]
                            if n >= 3:
                                pe.wait_ge(s("qf_in"), n - 2)
                            pe.matmul(bank[bk][:], orfk[r:r + 32, (n % 4) * P:(n % 4 + 1) * P], qT[r:r + 32, m, :], start=True, stop=False)
                            pe.matmul(bank[bk][:], nrmq[r:r + 32, :], q2[r:r + 32, m, :], start=False, stop=True).then_inc(s("qf_mm"), 1)
                        pe.wait_ge(s("kf_ok"), 8)
                        pe.wait_ge(s("v_ok"), 1)
                        for n in range(NP):
                            for t in range(T):
                                mm = pe.matmul(bank[1][:, n * 2 * V1:(n + 1) * 2 * V1], kf[:, t, 2 * n:2 * n + 2, :].rearrange("p h m -> p (h m)"),
                                               vn[:, t, 2 * n:2 * n + 2, :].rearrange("p h d -> p (h d)"), start=(t == 0), stop=(t == T - 1))
                        mm.then_inc(s("kv_mm"), 1)
                        pe.wait_ge(s("kv_ok"), 1)
                        pe.wait_ge(s("qf_ok"), NP)
                        for t in range(T):
                            for n in range(NP):
                                mm = pe.matmul(bank[2 + t][:, n * 2 * V1:(n + 1) * 2 * V1], qf[:, n, t * P:(t + 1) * P], kv[:, n, :],
                                               start=True, stop=True)
                            mm.then_inc(s("o_mm"), 1)
                        pe.wait_ge(s("on_ok"), T)
                        transposes(pe, on, (6, 7), s, "oT_mm")
                        pe.wait_ge(s("oT_ok"), 2)
                        for t in range(T):
                            for m in range(K2):
                                mm = pe.matmul(bank[t // 2][:, (t % 2) * D:(t % 2 + 1) * D], xT[:, m, t * P:(t + 1) * P], wo1[:, m, :],
                                               start=(m == 0), stop=(m == K2 - 1))
                        mm.then_inc(s("wo_mm"), 1)
                        pe.wait_ge(s("x3_ok"), 1)
                        transposes(pe, x3, (2, 3), s, "x3T_mm")
                        pe.wait_ge(s("x3T_ok"), 2)
                        for t in range(T):
                            for m in range(K2):
                                mm = pe.matmul(bank[4 + t // 2][:, (t % 2) * D:(t % 2 + 1) * D], hcT[:, m, t * P:(t + 1) * P], wde[:, m, :],
                                               start=(m == 0), stop=(m == K2 - 1))
                        mm.then_inc(s("yq_mm"), 1)
                        pe.wait_ge(s("yb_ok"), 1)
                        for m in range(K2):
                            bb = bank[6 + m][:].bitcast(BF16)
                            for t in range(T):
                                mm = pe.transpose(bb[:, t * P:(t + 1) * P], yb[:, t, m * P:(m + 1) * P], identb[:])
                            mm.then_inc(s("qbT_mm"), 1)
                        pe.wait_ge(s("qbT_ok"), 2)
                        for t in range(T):
                            for m in range(K2):
                                mm = pe.matmul(bank[t // 2][:, (t % 2) * D:(t % 2 + 1) * D], qbT[:, m, t * P:(t + 1) * P], wqb[:, m, :],
                                               start=(m == 0), stop=(m == K2 - 1))
                        mm.then_inc(s("acc_mm"), 1)

                    @block.scalar
                    def _(act):
                        for m in range(K2):
                            act.wait_ge(s("xT_mm"), m + 1)
                            act.copy(xT[:, m, :], bank[m][:]).then_inc(s("xT_ok"), 1)
                        act.wait_ge(s("dn_mm"), 1)
                        act.activation(dT[:], bank[2][0:M, :], ACT.Relu).then_inc(s("dn_ok"), 1)
                        for n in range(4):
                            w, o = 1 - n // 2, n % 2
                            src = bank[(5, 6, 7, 0)[n]][:]
                            dst, sq = ((qT, q2), (kT, k2))[w]
                            act.wait_ge(s("qk_mm"), n + 1)
                            act.activation(dst[:, o, :], src, ACT.Identity, bias=qkcol[:, w, o:o + 1])
                            act.activation(sq[:, o, :], src, ACT.Square, bias=qkcol[:, w, o:o + 1]).then_inc(s("sq_ok"), 1)
                        for n in range(8):
                            v = kf[:, n // 2, 8 * (n % 2):8 * (n % 2) + 8, :]
                            act.wait_ge(s("kf_sub"), n + 1)
                            act.activation(v, v, ACT.Exp).then_inc(s("kf_in"), 1)
                        for n in range(NP):
                            act.wait_ge(s("qf_mm"), n + 1)
                            act.activation(qf[:, n, :], bank[(6, 7, 0)[n % 3]][:], ACT.Exp).then_inc(s("qf_in"), 1)
                        for m in range(K2):
                            act.wait_ge(s("oT_mm"), m + 1)
                            act.copy(xT[:, m, :], bank[6 + m][:]).then_inc(s("oT_ok"), 1)
                        for m in range(K2):
                            act.wait_ge(s("x3T_mm"), m + 1)
                            act.copy(hcT[:, m, :], bank[2 + m][:]).then_inc(s("x3T_ok"), 1)
                        for m in range(K2):
                            act.wait_ge(s("qbT_mm"), m + 1)
                            act.copy(qbT[:, m, :], bank[6 + m][:].bitcast(BF16)[:, 0:S]).then_inc(s("qbT_ok"), 1)

                    @block.vector
                    def _(dve):
                        done, settle = chain_of(dve, s("dve_own"))
                        dve.wait_ge(s("gi_in"), 16)
                        dve.tensor_copy(gidx[:], gi[:, 2:4, :]).then_inc(s("idx_ok"), 1)
                        dve.wait_ge(s("p_in"), 64)
                        done(dve.tensor_tensor(wdn[:], dup[:], spread(dgb[:, 0, :], 1, K2), ALU.mult))
                        done(dve.tensor_tensor(wup[:], upp[:], ugb[:, 0, :], ALU.mult))
                        settle()
                        dve.tensor_tensor(wdn[:], wdn[:], spread(dgb[:, 1, :], 1, K2), ALU.add)
                        dve.tensor_tensor(wup[:], wup[:], ugb[:, 1, :], ALU.add).then_inc(s("wud_ok"), 1)
                        dve.wait_ge(s("x_in"), 16)
                        for k in range(2):
                            if k:
                                settle()
                            for t in range(T):
                                dve.wait_ge(s(f"y_in{k}{t}"), 16)
                                ins = dve.scalar_tensor_tensor(x2[:, t, :], yg[:, k, t, :], gi[:, k, t:t + 1], x2[:, t, :], ALU.mult, ALU.add)
                                if k == 0:
                                    done(ins)
                        ins.then_inc(s("x2_ok"), 1)
                        for m in range(K2):
                            dve.wait_ge(s("up_mm"), m + 1)
                            dve.wait_ge(s("xT_ok"), 2)
                            dve.tensor_tensor(hcT[:, m, :], bank[3 + m][:], xT[:, m, :], ALU.add).then_inc(s("hc_ok"), 1)
                        dve.wait_ge(s("v_mm"), 1)
                        dve.wait_ge(s("one_ok"), 1)
                        for c in range(2):
                            last = dve.tensor_tensor(vn[:, 2 * c:2 * c + 2, :, 0:DH].rearrange("p t h d -> p (t h) d"),
                                                     bank[1 + c][:].rearrange("p (h d) -> p h d", d=DH),
                                                     spread(row("bv"), 1, 2).rearrange("p t (h d) -> p t h d", d=DH), ALU.add)
                        last.then_inc(s("v_ok"), 1)
                        dve.wait_ge(s("kn_mm"), 1)
                        done(dve.tensor_copy(kn[:].rearrange("p t m h -> p (t m h)"), bank[3][:, 0:T * H]))
                        settle()
                        for n in range(8):
                            dve.wait_ge(s("kf_mm"), n + 1)
                            dve.tensor_tensor(kf[:, n // 2, 8 * (n % 2):8 * (n % 2) + 8, :],
                                              bank[4 + n % 2][:].rearrange("p (h m) -> p h m", m=M),
                                              spread(kn[:, n // 2, n % 2, :], 2, M), ALU.add).then_inc(s("kf_sub"), 1)
                        dve.wait_ge(s("kv0"), 1)
                        dve.wait_ge(s("kv_mm"), 1)
                        src = bank[1][:, 0:NP * 2 * V1].rearrange("p (n c) -> p n c", c=2 * V1)
                        dve.tensor_copy(kv[0:M, :, 0:V1], src[0:M, :, 0:V1])
                        dve.tensor_copy(kv[M:P, :, V1:2 * V1], src[M:P, :, V1:2 * V1]).then_inc(s("kv_ok"), 1)
                        for t in range(T):
                            o = bank[2 + t][:, 0:NP * 2 * V1].rearrange("p (h c) -> p h c", c=V1)
                            dve.wait_ge(s("o_mm"), t + 1)
                            done(dve.reciprocal(den[:, t, :], o[:, :, DH]))
                            settle()
                            dve.tensor_tensor(on[:, t, :].rearrange("p (h d) -> p h d", d=DH), o[:, :, 0:DH],
                                              spread(den[:, t, :], 2, DH), ALU.mult).then_inc(s("on_ok"), 1)
                        dve.wait_ge(s("wo_mm"), 1)
                        dve.wait_ge(s("xb_ok"), 1)
                        for c in range(2):
                            last = dve.tensor_tensor(x3[:, 2 * c:2 * c + 2, :], bank[c][:].rearrange("p (t f) -> p t f", t=2),
                                                     xb[:, 2 * c:2 * c + 2, :], ALU.add)
                        last.then_inc(s("x3_ok"), 1)
                        dve.wait_ge(s("yq_mm"), 1)
                        for c in range(2):
                            done(dve.tensor_tensor(yq[:, 2 * c:2 * c + 2, :], bank[4 + c][:].rearrange("p (t f) -> p t f", t=2),
                                                   spread(brow[:], 1, 2), ALU.add))
                        settle()
                        done(dve.tensor_reduce(ab[:, 0, :], yq[:], X, ALU.max, apply_absolute_value=True))
                        settle()
                        done(dve.tensor_scalar(ab[:, 1, :], ab[:, 0, :], 1e-6, 1.0 / 127.0, ALU.max, ALU.mult))
                        settle()
                        done(dve.reciprocal(ab[:, 2, :], ab[:, 1, :]))
                        settle()
                        for t in range(T):
                            done(dve.tensor_scalar(yq[:, t, :], yq[:, t, :], ab[:, 2, t:t + 1], ROUND, ALU.mult, ALU.add))
                        settle()
                        dve.tensor_scalar(yb[:], yq[:], ROUND, 127.0, ALU.subtract, ALU.min).then_inc(s("yb_ok"), 1)
                        dve.wait_ge(s("acc_mm"), 1)
                        for t in range(T):
                            done(dve.scalar_tensor_tensor(fo[:, t, :], bank[t // 2][:, (t % 2) * D:(t % 2 + 1) * D], ab[:, 1, t:t + 1],
                                                          row("ws"), ALU.mult, ALU.mult))
                        settle()
                        dve.wait_ge(s("x3b_ok"), 1)
                        dve.tensor_tensor(fo[:], fo[:], xb[:], ALU.add).then_inc(s("fin"), 1)
                s.clear()


def layouts(i):
    f = np.float32

    def tiles(w):
        return w.reshape(-1, P, w.shape[1]).transpose(1, 0, 2)

    def padded(w, rows=P):
        o = np.zeros((rows,) + w.shape[1:], w.dtype)
        o[:w.shape[0]] = w
        return o

    o = {}
    x = i["x"]
    o["xT"] = x.transpose(0, 2, 1).reshape(B, K2, P, S).transpose(0, 2, 1, 3)
    o["xN"] = x.reshape(B, T, P, D).transpose(0, 2, 1, 3)
    o["ids"] = np.concatenate([i[k].reshape(B, T, P).transpose(0, 2, 1)
                               for k in ("itok_BxS_0_999", "itok_BxS_0_4", "mask_BxS_ik0")], 2)
    o["boff"] = (CAP * np.arange(B)).astype(f).reshape(B, 1)
    o["cond"] = np.stack([padded(i[k].T) for k in ("cond_512", "cond_64", "fside_Bx32_0")], 1)
    o["affw"] = np.stack([i[f"L0_cond_{k}_aff_w"].T.reshape(P, K2, P) for k in "ko"], 1)
    o["affb"] = np.stack([i[f"L0_cond_{k}_aff_b"].reshape(K2, P).T for k in "ko"], 1)
    o["kow"] = np.stack([tiles(i[f"L0_cond_{k}_w"].T) for k in "ko"], 1)
    o["obcol"] = i["L0_cond_o_b"].reshape(K2, P).T
    wqkv = i["L0_attn_w_qkv"].T
    bqkv = i["L0_attn_b_qkv"]
    o["wqk"] = tiles(wqkv[:, 0:2 * D])
    o["wvl"] = tiles(np.concatenate([wqkv[:, 2 * D:]] + [i[f"L0_attn_{k}"].T for k in
                                    ("w1_read", "w1_write", "w2_read", "w2_write")], 1))
    o["wout"] = tiles(i["L0_attn_w_out"].T)
    dl, bs = i["L0_attn_decay_logits"], i["L0_attn_bias_scale"]
    o["dlr"] = np.concatenate([np.broadcast_to(dl, (P, H)), np.repeat(dl.reshape(HG, HG).T, 32, 0)], 1)
    aw = i["L0_cond2_aw"]
    c2 = lambda k: i[f"L0_cond2_{k}"]
    o["rows0"] = np.concatenate([i["L0_cond_k_b"], bqkv[0:2 * D], bqkv[2 * D:], i["L0_attn_b_out"], c2("int_b2"),
                                 c2("int_g"), c2("int_be"), i["L0_ffn_br"], aw, dl, bs])
    q = np.arange(P, dtype=f)
    r = np.arange(P) % 32
    o["cst"] = np.stack([q, P - q, (r < DH), (r >= DH) & (r < DH + NOFF), (r >= DH + NOFF) & (r < DH + 2 * NOFF),
                         0 * q, 0 * q, 0 * q], 1).astype(f)
    o["ident"] = np.eye(P, dtype=f)
    o["identb"] = np.eye(P, dtype=mybir.dt.np(BF16))
    dist = q[:, None] - q[None, :]
    o["posd"] = np.maximum(dist, 0).astype(f)
    o["low"] = (dist > 0).astype(f)
    o["tri"] = (dist < 0).astype(f)
    o["negb"] = np.where(dist < 0, MASKED, 0.0).astype(mybir.dt.np(BF16))
    o["iota"] = np.arange(SLOTS, dtype=f)
    sg = np.ones((2 * H, NOFF), f)
    sg[H:, 1] = sg[H:, 4] = -1
    o["sign"] = sg
    o["w1all"] = tiles(c2("int_W1"))
    o["wint2"] = tiles(c2("int_W2"))
    o["ib1"] = c2("int_b1").reshape(K2, P).T
    o["m1"] = np.stack([padded(c2(f"{k}_W1")) for k in ("mem", "noi", "res")], 1)
    o["m2"] = np.stack([tiles(c2(f"{k}_W2")) for k in ("mem", "noi", "res")], 1)
    o["mrow"] = np.stack([np.stack([c2(f"{k}_{n}") for n in ("b1", "b2", "g", "be")]) for k in ("mem", "noi", "res")])
    o["pw"] = np.concatenate([c2("pw_g"), c2("pw_b")], 1)
    o["cptm"] = np.concatenate([c2("cp_g"), c2("cp_b"), c2("tm_g"), c2("tm_b")], 1)
    o["ms"] = np.concatenate([c2("ms_g"), c2("ms_b")], 1)
    o["wr"] = tiles(i["L0_ffn_Wr"])
    o["eW1"] = i["L0_ffn_W1"].reshape(E, K2, P, HID).transpose(0, 2, 1, 3)
    o["eW2"] = i["L0_ffn_W2"].reshape(E, KH, P, D).transpose(0, 2, 1, 3)
    o["eb1"] = i["L0_ffn_b1"].reshape(E, KH, P).transpose(0, 2, 1)
    o["eb2"] = i["L0_ffn_b2"]
    o["dgu"] = np.concatenate([i[f"L1_cond_{k}"] for k in ("down_gamma", "down_beta", "up_gamma", "up_beta")], 1)
    o["wdc"] = i["L1_cond2_W_dec"].reshape(P, D + 1, KR).transpose(0, 2, 1)
    bd = i["L1_cond2_b_dec"].reshape(D + 1, KR)
    o["bdc"] = bd[0:D].reshape(K2, P, KR).transpose(1, 0, 2)
    o["bdl"] = bd[D].reshape(KR, 1)
    o["vv"] = i["L1_cond2_V"]
    o["dup"] = tiles(i["L1_cond_down_project"])
    o["upp"] = i["L1_cond_up_project"]
    o["wqkv"] = np.stack([tiles(i[f"L1_attn_W{k}"].T) for k in "qkv"], 1)
    o["wo1"] = tiles(i["L1_attn_Wo"].T)
    o["qkcol"] = np.stack([i[f"L1_attn_b{k}"].reshape(K2, P).T for k in "qk"], 1)
    orf = np.zeros((8, DH, 8, M), f)
    for h in range(8):
        orf[h, :, h, :] = i["L1_attn_orf"].T
    o["orfk"] = orf.reshape(P, 8 * M)
    nk = np.zeros((P, 8), f)
    nk[np.arange(P), np.arange(P) // DH] = -1.0 / 8
    o["nrmk"] = nk
    nq = np.zeros((P, P), f)
    for p in range(P):
        h = p // DH % 2
        nq[p, h * M:(h + 1) * M] = -1.0 / 8
    o["nrmq"] = nq
    o["wq8"] = np.ascontiguousarray(tiles(i["L1_ffn_weight_q"].T)).view(np.int32)
    o["rows1"] = np.concatenate([i["L1_attn_bv"], i["L1_attn_bo"], i["L1_ffn_weight_scale"], i["L1_ffn_bias"]])
    return {k: np.ascontiguousarray(v) for k, v in o.items()}


def kernel(**inputs):
    import concourse.bacc as bacc
    from concourse.bass_utils import run_bass_kernel_spmd

    nc = bacc.Bacc("TRN2", target_bir_lowering=False, num_devices=1)
    arrays = {f"in_{k}": v for k, v in layouts({k: np.asarray(v) for k, v in inputs.items()}).items()}
    a = {k[3:]: nc.dram_tensor(k, v.shape, mybir.dt.from_np(v.dtype), kind="ExternalInput").ap() for k, v in arrays.items()}
    out = nc.dram_tensor("out_0", (B, S, D), F32, kind="ExternalOutput").ap()
    program(nc, a, out)
    r = run_bass_kernel_spmd(nc, [arrays], core_ids=[0])
    return r.results[0]["out_0"]
```

```python
from contextlib import ExitStack

import numpy as np

import concourse.bass as bass
from concourse import mybir

F32 = mybir.dt.float32
BF16 = mybir.dt.bfloat16
I32 = mybir.dt.int32
I8 = mybir.dt.int8
U32 = mybir.dt.uint32
ALU = mybir.AluOpType
ACT = mybir.ActivationFunctionType
X = mybir.AxisListType.X

P = 128
B, S, D = 8, 512, 256
T = S // P
K2 = D // P
H, DH = 16, 16
HG = 4
E, CAP, HID = 8, 80, 1024
SLOTS = E * CAP
ROWS = B * CAP
ST = ROWS // P
KH = HID // P
M = 64
LN_EPS = 1e-5
MASKED = -1.0e30
ROUND = 12582912.0
NOFF = 6
KR = 30

ROWS0 = [("kb", D), ("bqk", 2 * D), ("bv", D), ("bout", D), ("b2", D), ("g", D), ("be", D),
         ("br", E), ("aw", 6), ("dl", H), ("bs", H)]
ROWS1 = [("bv", D), ("bo", D), ("ws", D), ("bias", D)]


AT = {"var1": -5, "z": -4, "h1": -3, "h1b": 0, "var2": 1, "kx": 0, "h2": 3,
      "x": -5, "kxmm": -4, "t": 5, "h": 8, "s": 11, "u": 14, "y": 20, "f": 27, "pos": 35, "disp": 43,
      "pair": 2, "full": 18, "turn1": 53}


def offsets(fields):
    out, at = {}, 0
    for name, n in fields:
        out[name] = (at, at + n)
        at += n
    return out, at


def spread(ap, at, n, step=0):
    dims = [list(d) for d in ap.ap]
    dims.insert(at, [step, n])
    return bass.AP(ap.tensor, ap.offset, dims)


def program(nc, a, out, scratch_kind="Internal", parts="ABC"):
    R0, n0 = offsets(ROWS0)
    R1, n1 = offsets(ROWS1)
    x1_d = nc.dram_tensor("x1_d", [B, P, T, D], F32, kind=scratch_kind).ap()
    gate_d = nc.dram_tensor("gate_d", [B, P, 4 * T], F32, kind=scratch_kind).ap()
    buf_d = nc.dram_tensor("buf_d", [E, P, K2, B, CAP], F32, kind=scratch_kind).ap()
    y_d = nc.dram_tensor("y_d", [E * ROWS, D], F32, kind=scratch_kind).ap()
    prow_d = nc.dram_tensor("prow_d", [B, 2 * D + 2 * M + 2 * D], F32, kind=scratch_kind).ap()
    wdec_d = nc.dram_tensor("wdec_d", [B, P, K2, D], F32, kind=scratch_kind).ap()
    PR = {"demk": (0, D), "dg": (D, D + M), "db": (D + M, D + 2 * M), "ug": (D + 2 * M, 2 * D + 2 * M),
          "ub": (2 * D + 2 * M, 3 * D + 2 * M), "bias": (3 * D + 2 * M, 4 * D + 2 * M)}

    top = ExitStack()
    with top:
        def sb_in(ctx, name, shape, dt=F32):
            return ctx.enter_context(nc.sbuf_tensor(name, shape, dt))

        bank = [top.enter_context(nc.psum_tensor(f"bank{i}", [P, 512], F32)) for i in range(8)]

        ident = sb_in(top, "ident", [P, P])
        pcol = sb_in(top, "pcol", [P, B, 8])
        eps_ln = sb_in(top, "eps_ln", [P, 2])

        class Sems:

            def __init__(self, ctx, prefix):
                self.ctx, self.prefix, self.by = ctx, prefix, {}

            def __call__(self, name):
                if name not in self.by:
                    self.by[name] = self.ctx.enter_context(nc.semaphore(f"{self.prefix}_{name}"))
                return self.by[name]

            def clear(self):
                nums = [s.num for s in self.by.values()]
                nc.all_engine_barrier(sems_to_clear=range(min(nums), max(nums) + 1))

        def chain_of(eng, sem):
            n = [0]

            def done(ins):
                n[0] += 1
                ins.then_inc(sem, 1)
                return n[0]

            def settle():
                eng.wait_ge(sem, n[0])

            return done, settle

        if True:
            l0 = ExitStack()
            with l0:
                sb = lambda name, shape, dt=F32: sb_in(l0, name, shape, dt)
                kow = sb("kow", [P, 2, K2, D])
                wqk = sb("wqk", [P, K2, 2 * D])
                wvl = sb("wvl", [P, K2, 2 * D])
                wout = sb("wout", [P, K2, D])
                wint = sb("wint", [P, 4 * K2, D])
                wint2 = sb("wint2", [P, K2, D])
                wr = sb("wr", [P, K2, E])
                rows = sb("rows", [P, n0])
                obcol = sb("obcol", [P, K2])
                tri = sb("tri", [P, P], BF16)
                ones = sb("ones", [P, P], BF16)
                negb = sb("negb", [P, P], BF16)
                identb = sb("identb", [P, P], BF16)
                iota = sb("iota", [P, SLOTS])
                wdiag = sb("wdiag", [P, H, P])
                facr = sb("facr", [P, H])
                facw = sb("facw", [P, H])
                fack = sb("fack", [P, HG, 5])
                sel = sb("sel", [H // 2, P])
                sign = sb("sign", [P, 2 * H, NOFF])
                row = lambda f: rows[:, R0[f][0]:R0[f][1]]

                st = ExitStack()
                with st:
                    sbt = lambda name, shape, dt=F32: sb_in(st, name, shape, dt)
                    cond = sbt("cond", [P, 3, B])
                    affw = sbt("affw", [P, 2, K2, P])
                    affb = sbt("affb", [P, 2, K2])
                    w1all = sbt("w1all", [P, 6 * K2, D])
                    m1 = sbt("m1", [P, 3, D])
                    m2 = sbt("m2", [P, 3, K2, D])
                    mrow = sbt("mrow", [B, 3, 4, D])
                    ib1 = sbt("ib1", [P, K2])
                    cst = sbt("cst", [P, 8])
                    posd = sbt("posd", [P, P])
                    low = sbt("low", [P, P])
                    dlr = sbt("dlr", [P, H + HG])
                    lnd = sbt("lnd", [P, H + HG])
                    tmp = sbt("tmp", [P, H + HG])
                    tmp2 = sbt("tmp2", [P, H + HG])
                    aws = sbt("aws", [P, 6])
                    awr = sbt("awr", [P, 4])
                    style2 = sbt("style2", [P, 2, K2, B])
                    kow2 = sbt("kow2", [P, 2, K2, D])
                    drow = sbt("drow", [B, D])
                    dco = sbt("dco", [P, K2, B])
                    g1 = sbt("g1", [B, 3, D])
                    g1t = sbt("g1t", [P, 3, K2, B])
                    g2 = sbt("g2", [B, 3, D])
                    g2t = sbt("g2t", [P, 3, K2, B])
                    mstat = sbt("mstat", [B, 3, 6])
                    mmv = sbt("mmv", [B, 3, 4])
                    dgu = sbt("dgu", [P, 2 * M + 2 * D])
                    dguo = sbt("dguo", [B, 2 * M + 2 * D])
                    wdc = sbt("wdc", [P, KR, D + 1])
                    bdc = sbt("bdc", [P, K2, KR])
                    bdl = sbt("bdl", [KR, 1])
                    vv = sbt("vv", [KR, D])
                    uu = sbt("uu", [P, K2, B, KR])
                    ul = sbt("ul", [KR, B])
                    ut = sbt("ut", [KR, 2, P])
                    wde = sbt("wde", [P, 2, D])
                    brow = sbt("brow", [B, D])
                    sctx = ExitStack()
                    with sctx:
                        s = Sems(sctx, "s0")
                        with nc.Block() as block:
                            @block.sync
                            def _(sp):
                                for dst, name in ((cond, "cond"), (affw, "affw"), (affb, "affb"), (kow, "kow"),
                                                  (dlr, "dlr"), (cst, "cst"), (ident, "ident")):
                                    sp.dma_start(dst[:], a[name]).then_inc(s("load1"), 16)
                                sp.dma_start(rows[:], spread(a["rows0"], 0, P)).then_inc(s("load1"), 16)
                                for dst, name in ((posd, "posd"), (low, "low"), (w1all, "w1all"), (m1, "m1"), (m2, "m2"),
                                                  (ib1, "ib1"), (wqk, "wqk")):
                                    sp.dma_start(dst[:], a[name]).then_inc(s("load2"), 16)
                                sp.dma_start(mrow[:], spread(a["mrow"], 0, B)).then_inc(s("load2"), 16)
                                for dst, name in ((dgu, "dgu"), (wdc, "wdc"), (bdc, "bdc"), (bdl, "bdl"), (vv, "vv")):
                                    sp.dma_start(dst[:], a[name]).then_inc(s("load3"), 16)
                                for dst, name in ((wvl, "wvl"), (wout, "wout"), (wint2, "wint2"), (wr, "wr"),
                                                  (obcol, "obcol"), (sel, "sel"), (tri, "tri"), (negb, "negb"), (identb, "identb")):
                                    sp.dma_start(dst[:], a[name]).then_inc(s("load4"), 16)
                                sp.dma_start(iota[:], spread(a["iota"], 0, P)).then_inc(s("load4"), 16)
                                sp.dma_start(sign[:], spread(a["sign"], 0, P)).then_inc(s("load4"), 16)
                                sp.wait_ge(s("drow_ok"), 1)
                                sp.dma_start(prow_d[:, 0:D], drow[:]).then_inc(s("stored"), 16)
                                sp.wait_ge(s("dguo_ok"), 1)
                                sp.dma_start(prow_d[:, D:3 * D + 2 * M], dguo[:]).then_inc(s("stored"), 16)
                                sp.wait_ge(s("brow_ok"), 1)
                                sp.dma_start(prow_d[:, 3 * D + 2 * M:], brow[:]).then_inc(s("stored"), 16)
                                for n in range(B * K2):
                                    sp.wait_ge(s("wde_ok"), n + 1)
                                    sp.dma_start(wdec_d[n // K2, :, n % K2, :], wde[:, n % 2, :]).then_inc(s(f"wstored{n % 2}"), 16)
                                sp.wait_ge(s("stored"), 48)
                                sp.wait_ge(s("wstored0"), 8 * B * K2)
                                sp.wait_ge(s("wstored1"), 8 * B * K2)
                                sp.wait_ge(s("load4"), 176)
                                sp.wait_ge(s("load1"), 128)
                                sp.wait_ge(s("load2"), 128)
                                sp.wait_ge(s("load3"), 80)

                            @block.gpsimd
                            def _(pool):
                                pool.memset(ones[:], 1.0).then_inc(s("ones_ok"), 1)
                                pool.memset(eps_ln[:, 0:1], LN_EPS).then_inc(s("ones_ok"), 1)
                                pool.memset(eps_ln[:, 1:2], 1e-8).then_inc(s("ones_ok"), 1)

                            @block.tensor
                            def _(pe):
                                pe.wait_ge(s("load1"), 128)
                                for w in range(2):
                                    for m in range(K2):
                                        mm = pe.matmul(bank[0][:, (w * K2 + m) * B:(w * K2 + m + 1) * B], affw[:, w, m, :],
                                                       cond[:, 0, :], start=True, stop=True)
                                mm.then_inc(s("style_mm"), 1)
                                pe.wait_ge(s("sq_ok"), 2)
                                for m in range(K2):
                                    mm = pe.matmul(bank[1][0:B, 0:D], style2[:, 0, m, :], kow2[:, 0, m, :],
                                                   start=(m == 0), stop=(m == K2 - 1))
                                mm.then_inc(s("dem_mm"), 1)
                                for o in range(K2):
                                    for m in range(K2):
                                        mm = pe.matmul(bank[2][:, o * B:(o + 1) * B], kow2[:, 1, m, o * P:(o + 1) * P],
                                                       style2[:, 1, m, :], start=(m == 0), stop=(m == K2 - 1))
                                mm.then_inc(s("dem_mm"), 1)
                                pe.wait_ge(s("load2"), 128)
                                for j, k in enumerate((P, 64, 32)):
                                    mm = pe.matmul(bank[3 + j][0:B, 0:D], cond[0:k, j, :], m1[0:k, j, :], start=True, stop=True)
                                    mm.then_inc(s("m1_mm"), 1)
                                pe.wait_ge(s("g1_ok"), 1)
                                for j in range(3):
                                    for m in range(K2):
                                        mm = pe.transpose(bank[6][:, (j * K2 + m) * B:(j * K2 + m + 1) * B],
                                                          g1[:, j, m * P:(m + 1) * P], ident[0:B, 0:B])
                                mm.then_inc(s("g1t_mm"), 1)
                                pe.wait_ge(s("g1t_ok"), 1)
                                for j in range(3):
                                    for m in range(K2):
                                        mm = pe.matmul(bank[3 + j][0:B, 0:D], g1t[:, j, m, :], m2[:, j, m, :],
                                                       start=(m == 0), stop=(m == K2 - 1))
                                mm.then_inc(s("m2_mm"), 1)
                                pe.wait_ge(s("g2_ok"), 1)
                                for j in range(3):
                                    for m in range(K2):
                                        mm = pe.transpose(bank[6][:, (j * K2 + m) * B:(j * K2 + m + 1) * B],
                                                          g2[:, j, m * P:(m + 1) * P], ident[0:B, 0:B])
                                mm.then_inc(s("g2t_mm"), 1)
                                pe.wait_ge(s("g2t_ok"), 1)
                                for o in range(K2):
                                    for n in range(3 * K2):
                                        j, m = n // K2, n % K2
                                        mm = pe.matmul(bank[7][:, o * B:(o + 1) * B],
                                                       w1all[:, (2 + j) * K2 + m, o * P:(o + 1) * P], g2t[:, j, m, :],
                                                       start=(n == 0), stop=(n == 3 * K2 - 1))
                                mm.then_inc(s("cvec_mm"), 1)
                                pe.wait_ge(s("load3"), 80)
                                hw = M + D
                                for n in range(2):
                                    mm = pe.matmul(bank[3 + n][0:B, 0:hw], cond[:, 0, :], dgu[:, n * hw:(n + 1) * hw],
                                                   start=True, stop=True)
                                mm.then_inc(s("dgu_mm"), 1)
                                for m in range(K2):
                                    for k in range(KR):
                                        mm = pe.matmul(bank[m][:, k * B:(k + 1) * B], wdc[:, k, m * P:(m + 1) * P],
                                                       cond[:, 0, :], start=True, stop=True)
                                mm = pe.matmul(bank[2][0:KR, 0:B], wdc[:, :, D], cond[:, 0, :], start=True, stop=True)
                                mm.then_inc(s("u_mm"), 1)
                                pe.wait_ge(s("u_ok"), 1)
                                pe.matmul(bank[5][0:B, 0:D], ul[:, :], vv[:, :], start=True, stop=True).then_inc(s("brow_mm"), 1)
                                for n in range(B * K2):
                                    if n >= 2:
                                        pe.wait_ge(s("ut_ok"), n - 1)
                                    pe.transpose(bank[n % 2][0:KR, 0:P], uu[:, n % K2, n // K2, :], ident[:, :]).then_inc(s("ut_mm"), 1)
                                    pe.wait_ge(s("ut_ok"), n + 1)
                                    if n >= 2:
                                        pe.wait_ge(s("wde_ok"), n - 1)
                                    pe.matmul(bank[6 + n % 2][:, 0:D], ut[:, n % 2, :], vv[:, :], start=True, stop=True)\
                                        .then_inc(s("wde_mm"), 1)

                            @block.scalar
                            def _(act):
                                done, settle = chain_of(act, s("act_own"))
                                act.wait_ge(s("ones_ok"), 3)
                                act.wait_ge(s("load1"), 128)
                                act.activation(kow2[:], kow[:], ACT.Square).then_inc(s("sq_ok"), 1)
                                act.wait_ge(s("absx"), 1)
                                act.activation(tmp[:], tmp[:], ACT.Exp, scale=-1.0).then_inc(s("expx"), 1)
                                act.wait_ge(s("awsub"), 1)
                                done(act.activation(aws[:], aws[:], ACT.Exp, accum_out=awr[:, 0:1]))
                                settle()
                                act.activation(tmp2[:], tmp[:], ACT.Ln, bias=1.0).then_inc(s("lnx"), 1)
                                act.wait_ge(s("lnd_ok"), 1)
                                act.wait_ge(s("load2"), 128)
                                for h in range(H):
                                    act.activation(wdiag[:, h, :], posd[:], ACT.Exp, scale=lnd[:, h:h + 1])
                                act.activation(facr[:], lnd[:, 0:H], ACT.Exp, scale=cst[:, 0:1])
                                act.activation(facw[:], lnd[:, 0:H], ACT.Exp, scale=cst[:, 1:2])
                                for v in range(3):
                                    last = act.activation(fack[:, :, v], lnd[:, H:H + HG], ACT.Exp, scale=float(P * v))
                                last.then_inc(s("pow_ok"), 1)
                                act.wait_ge(s("dem_mm"), 2)
                                act.activation(drow[:], bank[1][0:B, 0:D], ACT.Sqrt, bias=eps_ln[0:B, 1:2])
                                act.activation(dco[:], bank[2][:, 0:K2 * B].rearrange("p (o b) -> p o b", b=B), ACT.Sqrt,
                                               bias=eps_ln[:, 1:2]).then_inc(s("dem_sq"), 1)
                                act.wait_ge(s("g1_pre"), 1)
                                act.activation(g1[:], g1[:], ACT.Silu).then_inc(s("g1_ok"), 1)
                                act.wait_ge(s("mvar"), 1)
                                act.activation(mmv[:, :, 2:3], mmv[:, :, 1:2], ACT.Sqrt, bias=eps_ln[0:B, 0:1]).then_inc(s("msd"), 1)
                                for n in range(B * K2):
                                    act.wait_ge(s("ut_mm"), n + 1)
                                    if n >= 2:
                                        act.wait_ge(s("wde_mm"), n - 1)
                                    act.copy(ut[:, n % 2, :], bank[n % 2][0:KR, 0:P]).then_inc(s("ut_ok"), 1)

                            @block.vector
                            def _(dve):
                                done, settle = chain_of(dve, s("dve_own"))
                                dve.wait_ge(s("load1"), 128)
                                dve.tensor_scalar(tmp2[:], dlr[:], -1.0, None, ALU.mult).then_inc(s("neg"), 1)
                                done(dve.tensor_reduce(awr[:, 1:2], row("aw"), X, ALU.max))
                                dve.wait_ge(s("neg"), 1)
                                dve.tensor_tensor(tmp[:], dlr[:], tmp2[:], ALU.max).then_inc(s("absx"), 1)
                                settle()
                                dve.tensor_scalar(aws[:], row("aw"), awr[:, 1:2], None, ALU.subtract).then_inc(s("awsub"), 1)
                                done(dve.tensor_scalar(lnd[:], dlr[:], 0.0, None, ALU.min))
                                dve.wait_ge(s("style_mm"), 1)
                                for w in range(2):
                                    for m in range(K2):
                                        n = w * K2 + m
                                        done(dve.tensor_scalar(pcol[:, :, n], bank[0][:, n * B:(n + 1) * B],
                                                               affb[:, w, m:m + 1], None, ALU.add))
                                settle()
                                sty = pcol[:, :, 0:4].rearrange("p b (w m) -> p w m b", w=2)
                                for w in range(2):
                                    last = dve.tensor_tensor(style2[:, w], sty[:, w], sty[:, w], ALU.mult)
                                last.then_inc(s("sq_ok"), 1)
                                dve.wait_ge(s("lnx"), 1)
                                dve.tensor_tensor(lnd[:], lnd[:], tmp2[:], ALU.subtract).then_inc(s("lnd_ok"), 1)
                                dve.wait_ge(s("dem_sq"), 1)
                                dve.reciprocal(drow[:], drow[:]).then_inc(s("drow_ok"), 1)
                                dve.reciprocal(pcol[:, :, 4:6].rearrange("p b o -> p o b"), dco[:])
                                done(dve.reciprocal(awr[:, 2:3], awr[:, 0:1]))
                                settle()
                                done(dve.tensor_scalar(aws[:], aws[:], awr[:, 2:3], None, ALU.mult))
                                settle()
                                dve.wait_ge(s("load2"), 128)
                                for j in range(2, 5):
                                    done(dve.tensor_scalar(w1all[:, K2 * j:K2 * j + K2, :], w1all[:, K2 * j:K2 * j + K2, :],
                                                           aws[:, j:j + 1], None, ALU.mult))
                                for at, j in ((2, 5), (4, 1), (6, 0)):
                                    done(dve.tensor_scalar(wint[:, at:at + K2, :], w1all[:, K2 * j:K2 * j + K2, :],
                                                           aws[:, j:j + 1], None, ALU.mult))
                                settle()
                                done(dve.tensor_tensor(wint[:, 0:K2, :], w1all[:, 4:6, :], w1all[:, 6:8, :], ALU.add))
                                settle()
                                done(dve.tensor_tensor(wint[:, 0:K2, :], wint[:, 0:K2, :], w1all[:, 8:10, :], ALU.add))
                                done(dve.tensor_scalar(wqk[:, :, 0:D], wqk[:, :, 0:D], 0.25, None, ALU.mult))
                                q0 = R0["bqk"][0]
                                done(dve.tensor_scalar(rows[:, q0:q0 + D], rows[:, q0:q0 + D], 0.25, None, ALU.mult))
                                dve.wait_ge(s("pow_ok"), 1)
                                done(dve.tensor_tensor(wdiag[:], wdiag[:], spread(low[:], 1, H), ALU.mult))
                                done(dve.tensor_tensor(facr[:], facr[:], row("bs"), ALU.mult))
                                done(dve.tensor_scalar(fack[:, :, 0:3], fack[:, :, 0:3], cst[:, 3:4], cst[:, 2:3], ALU.mult, ALU.add))
                                done(dve.tensor_copy(fack[:, :, 3], spread(cst[:, 4:5], 1, HG)[:, :, 0]))
                                done(dve.tensor_copy(fack[:, :, 4], spread(cst[:, 2:3], 1, HG)[:, :, 0]))
                                dve.wait_ge(s("m1_mm"), 3)
                                for j in range(3):
                                    last = dve.tensor_tensor(g1[:, j, :], bank[3 + j][0:B, 0:D], mrow[:, j, 0, :], ALU.add)
                                last.then_inc(s("g1_pre"), 1)
                                dve.wait_ge(s("g1t_mm"), 1)
                                dve.tensor_copy(g1t[:].rearrange("p j m b -> p (j m b)"), bank[6][:, 0:3 * K2 * B]).then_inc(s("g1t_ok"), 1)
                                dve.wait_ge(s("m2_mm"), 1)
                                for j in range(3):
                                    done(dve.tensor_tensor(g2[:, j, :], bank[3 + j][0:B, 0:D], mrow[:, j, 1, :], ALU.add))
                                settle()
                                for j in range(3):
                                    done(dve.bn_stats(mstat[:, j, :], g2[:, j, :]))
                                settle()
                                for j in range(3):
                                    last = dve.bn_aggr(mmv[:, j, 0:2], mstat[:, j, :])
                                last.then_inc(s("mvar"), 1)
                                dve.wait_ge(s("msd"), 1)
                                done(dve.reciprocal(mmv[:, :, 3:4], mmv[:, :, 2:3]))
                                settle()
                                for j in range(3):
                                    done(dve.tensor_scalar(g2[:, j, :], g2[:, j, :], mmv[:, j, 0:1], mmv[:, j, 3:4],
                                                           ALU.subtract, ALU.mult))
                                settle()
                                done(dve.tensor_tensor(g2[:], g2[:], mrow[:, :, 2, :], ALU.mult))
                                settle()
                                dve.tensor_tensor(g2[:], g2[:], mrow[:, :, 3, :], ALU.add).then_inc(s("g2_ok"), 1)
                                dve.wait_ge(s("g2t_mm"), 1)
                                dve.tensor_copy(g2t[:].rearrange("p j m b -> p (j m b)"), bank[6][:, 0:3 * K2 * B]).then_inc(s("g2t_ok"), 1)
                                dve.wait_ge(s("cvec_mm"), 1)
                                for o in range(K2):
                                    dve.tensor_scalar(pcol[:, :, 6 + o], bank[7][:, o * B:(o + 1) * B], ib1[:, o:o + 1], None, ALU.add)
                                dve.wait_ge(s("dgu_mm"), 1)
                                hw = M + D
                                dve.tensor_copy(dguo[:, 0:hw], bank[3][0:B, 0:hw])
                                dve.tensor_copy(dguo[:, hw:2 * hw], bank[4][0:B, 0:hw]).then_inc(s("dguo_ok"), 1)
                                dve.wait_ge(s("u_mm"), 1)
                                for m in range(K2):
                                    dve.tensor_tensor(uu[:, m].rearrange("p b k -> p k b"),
                                                      bank[m][:, 0:KR * B].rearrange("p (k b) -> p k b", b=B),
                                                      spread(bdc[:, m, :], 2, B), ALU.add)
                                dve.tensor_scalar(ul[:], bank[2][0:KR, 0:B], bdl[:, 0:1], None, ALU.add).then_inc(s("u_ok"), 1)
                                dve.wait_ge(s("brow_mm"), 1)
                                dve.tensor_copy(brow[:], bank[5][0:B, 0:D]).then_inc(s("brow_ok"), 1)
                                for n in range(B * K2):
                                    dve.wait_ge(s("wde_mm"), n + 1)
                                    if n >= 2:
                                        dve.wait_ge(s(f"wstored{n % 2}"), 16 * (n // 2))
                                    dve.tensor_copy(wde[:, n % 2, :], bank[6 + n % 2][:, 0:D]).then_inc(s("wde_ok"), 1)
                        s.clear()

                cT = sb("cT", [P, K2, S + 1])
                x1 = sb("x1", [P, T, D])
                xt_na = sb("xt_na", [P, T * D])
                xT = xt_na[:].rearrange("p (m s) -> p m s", m=K2)
                nA1 = xt_na[:].rearrange("p (t f) -> p t f", t=T)
                kx = sb("kx", [P, T, 2 * D])
                big = sb("big", [P, 9 * D + T * H * 2 * H])
                prod = big[:, 0:9 * D].rearrange("p (o f) -> p o f", f=D)
                wk = big[:, 0:K2 * D].rearrange("p (m f) -> p m f", f=D)
                sc = big[:, 9 * D:].rearrange("p (t o h) -> p t o h", o=H, h=2 * H)
                pv = big[:, 0:H * D].rearrange("p (o f) -> p o f", f=D)
                ex_at = sb("ex_at", [P, T * D])
                ex = ex_at[:].rearrange("p (t o h) -> p t o h", o=H, h=H)
                aT1 = ex_at[:].rearrange("p (m s) -> p m s", m=K2)
                mx = sb("mx", [P, T, H])
                rs = sb("rs", [P, T, H])
                wo = sb("wo", [P, K2, D])
                demk = sb("demk", [P, D])
                pc1 = sb("pc1", [P, 8])
                pts = kx[:].rearrange("p t f -> p (t f)")[:, 0:T * D].rearrange("p (t f) -> p t f", t=T)
                vp = sb("vp", [P, T, H // 2, 3 * DH])
                v_of = lambda t, c: vp[:, t, :, 2 * DH * c:2 * DH * c + DH]
                att_buf = sb("att_buf", [P, T * 2 * H * 32])
                qk = att_buf[:].rearrange("p (t s h r) -> p t s h r", t=T, s=2, h=H)
                pr = att_buf[:, 0:3 * S].rearrange("p (n s) -> p n s", n=3)
                prT = att_buf[:, 3 * S:6 * S].rearrange("p (n s) -> p n s", n=3)
                dbias = att_buf[:, 6 * S:6 * S + 2 * P].rearrange("p (n k) -> p n k", k=P)
                rT = att_buf[0:H // 2, 6 * S + 2 * P:7 * S + 2 * P]
                qT = sb("qT", [P, HG, S])
                NKB = 4 * (T - 1) + T + 1
                kk = sb("kk", [P, HG, NKB * P])

                def blocks(g, at, n):
                    ap = kk[:, g, at * P:(at + 1) * P]
                    return ap if n == 1 else bass.AP(ap.tensor, ap.offset, [list(ap.ap[0]), [(T + 1) * P, n], list(ap.ap[-1])])

                tiles_of = lambda src, n: src[:, 0:P] if n == 1 else src[:, 0:n * P].rearrange("p (n k) -> p n k", k=P)
                KEYS = ((0, 4, 4), (1, 4, 3), (4, 3, 0), (8, 2, 1), (12, 1, 2))
                lines = qT[:].rearrange("p g s -> p (g s)")[:, 0:2 * T * 2 * H * NOFF].rearrange("p (n t s c) -> p n t s c", n=2, t=T, c=NOFF)
                la, lb = lines[:, 0], lines[:, 1]
                ln = sb("ln", [P, T, 2 * H])
                lf = sb("lf", [P, 4, T, H])
                nmax = sb("nmax", [P, 4])
                rsum = sb("rsum", [P, T, H])
                rinv = sb("rinv", [P, T, H])
                ids = sb("ids", [P, 3 * T], I32)
                boff = sb("boff", [P, 1])
                pc3 = sb("pc3", [P, 8])
                gac = sb("gac", [P, T, 2 * D])
                bfT = gac[:].rearrange("p t f -> p (t f)")[:, 0:K2 * SLOTS].rearrange("p (m c) -> p m c", m=K2)
                gb = sb("gb", [P, T, 4 * D])
                gbf = gb[:].rearrange("p t f -> p (t f)")
                aT3 = gbf[:, 0:K2 * S].rearrange("p (m s) -> p m s", m=K2)
                hT = gbf[:, K2 * S:2 * K2 * S].rearrange("p (m s) -> p m s", m=K2)
                cat = sb("cat", [P, 8, S])
                disp = cat[:].rearrange("p n s -> p (n s)")[:, 0:T * SLOTS].rearrange("p (t c) -> p t c", t=T)
                aT2 = cat[:].rearrange("p n s -> p (n s)")[:, T * SLOTS:T * SLOTS + K2 * S].rearrange("p (m s) -> p m s", m=K2)
                nA = sb("nA", [P, T, D])
                xN = nA
                nB = sb("nB", [P, T, D])
                stat = sb("stat", [P, T, 6])
                mv = sb("mv", [P, T, 4])
                pe8 = sb("pe8", [P, 8, T, E])
                picks = sb("picks", [P, T, E], BF16)
                sm = sb("sm", [P, 16, T])
                gi = sb("gi", [P, 4, T])
                units = [(2 * p + c, i) for p in range(H // 2) for i in (3, 0, 2, 1) for c in range(2)]
                N = len(units)
                long_before = [sum(i == T - 1 for _, i in units[0:u]) for u in range(N)]
                SIDE = (6, 7)

                def iteration(b1, b2, b3):
                    lctx = ExitStack()
                    with lctx:
                        s = Sems(lctx, "a")

                        def started(*streams):
                            return [[g, next(g)] for g in streams]

                        def advance(streams, slot):
                            for pair in streams:
                                while pair[1] is not None and pair[1] <= slot:
                                    pair[1] = next(pair[0], None)

                        def interleave(unit, streams):
                            for u in range(N):
                                if b2 is not None:
                                    unit(u)
                                advance(streams, u)
                            assert all(due is None for _, due in streams)

                        with nc.Block() as block:
                            @block.sync
                            def _(sp):
                                if b1 is not None:
                                    sp.dma_start(xT, a["xT"][b1].rearrange("p m s -> p m s")).then_inc(s("x_in"), 16)
                                    sp.dma_start(demk[:], spread(prow_d[b1, 0:D], 0, P)).then_inc(s("x_in"), 16)
                                if b3 is not None:
                                    sp.dma_start(ids[:], a["ids"][b3]).then_inc(s("ids_in"), 16)
                                    sp.dma_start(boff[:], spread(a["boff"][b3, :], 0, P)).then_inc(s("ids_in"), 16)
                                if b3 is not None:
                                    sp.dma_start(x1_d[b3], x1[:]).then_inc(s("x1_out"), 16)
                                    sp.wait_ge(s("ss_ok"), 1)
                                if b2 is not None:
                                    sp.dma_start(xN[:], a["xN"][b2]).then_inc(s("xn_in"), 16)
                                if b3 is not None:
                                    sp.wait_ge(s("gi_ok"), 1)
                                    sp.dma_start(gate_d[b3], gi[:].rearrange("p k t -> p (k t)")).then_inc(s("out3"), 16)
                                    for m in range(K2):
                                        sp.wait_ge(s("bf_ok"), 2 * m + 2)
                                        sp.dma_start(buf_d[:, :, m, b3, :].rearrange("e p c -> p e c"),
                                                     bfT[:, m, :].rearrange("p (e c) -> p e c", c=CAP)).then_inc(s("out3"), 16)
                                if b2 is not None:
                                    sp.wait_ge(s("x1_ok"), 1)
                                if b3 is not None:
                                    sp.wait_ge(s("x1_out"), 16)
                                    sp.wait_ge(s("out3"), 48)

                            @block.gpsimd
                            def _(pool):
                                def gather(src, dst, k):
                                    for t in range(T):
                                        if k:
                                            pool.wait_ge(s(f"gath{t}"), 16 * k)
                                        pool.indirect_dma_start(
                                            out=dst[:, t, :], out_offset=None, in_=src,
                                            in_offset=bass.IndirectOffsetOnAxis(ap=ids[:, k * T + t:k * T + t + 1].bitcast(U32), axis=0))\
                                            .then_inc(s(f"gath{t}"), 16)

                                if b2 is not None:
                                    pool.memset(cT[:, :, 0:1], 0.0).then_inc(s("c0_ok"), 1)
                                    for t in range(T):
                                        last = pool.memset(vp[:, t, :, DH:2 * DH], 0.0)
                                    last.then_inc(s("gap_ok"), 1)
                                    pool.memset(qk[:, :, :, :, 28:32], 0.0).then_inc(s("pad_ok"), 1)
                                if b3 is not None:
                                    pool.wait_ge(s("ids_in"), 32)
                                    gather(a["pw"], gac, 0)
                                    gather(a["cptm"], gb, 1)
                                if b2 is not None:
                                    pool.wait_ge(s("vl_ok"), T)
                                    for t in range(T):
                                        for c in range(2):
                                            last = pool.tensor_tensor(v_of(t, c), v_of(t, c), row("bv").rearrange("p (n c d) -> p n c d", c=2, d=DH)[:, :, c], ALU.add)
                                    last.then_inc(s("v_ok"), 1)
                                if b3 is not None:
                                    for t in range(T):
                                        pool.wait_ge(s(f"gath{t}"), 32)
                                    pool.wait_ge(s("z_ok"), T)
                                    tt, ss = gb[:, :, 2 * D:3 * D], gac[:, :, 0:D]
                                    pool.tensor_tensor(tt, nA[:], tt, ALU.mult).then_inc(s("pool_own"), 1)
                                    pool.wait_ge(s("pool_own"), 1)
                                    pool.tensor_tensor(tt, tt, gb[:, :, 3 * D:4 * D], ALU.add).then_inc(s("tt_ok"), 1)
                                    pool.wait_ge(s("h1_ok"), 1)
                                    gather(a["ms"], gac, 2)
                                    for t in range(T):
                                        pool.wait_ge(s(f"gath{t}"), 48)
                                    pool.tensor_tensor(ss, nA[:], ss, ALU.mult).then_inc(s("pool_own"), 1)
                                    pool.wait_ge(s("pool_own"), 2)
                                    pool.tensor_tensor(ss, ss, gac[:, :, D:2 * D], ALU.add).then_inc(s("ss_ok"), 1)
                                    for t in range(T):
                                        pool.dma_reset(range(s(f"gath{t}").num, s(f"gath{t}").num + 1))
                                if b2 is not None:
                                    pool.wait_ge(s("xn_in"), 16)
                                    pool.tensor_tensor(xN[:], xN[:], spread(row("bout"), 1, T), ALU.add).then_inc(s("xb_ok"), 1)
                                if b1 is not None:
                                    pool.wait_ge(s("sc_low"), 2 * T)
                                    pool.tensor_copy(sc[:, :, 1:8, H:2 * H], sc[:, :, 1:8, 0:H]).then_inc(s("sc_wide"), 1)
                                    pool.wait_ge(s("sc_wide"), 1)
                                    for d in range(1, 8):
                                        last = pool.tensor_copy(sc[:, :, H - d, 0:H], sc[:, :, d, H - d:2 * H - d])
                                    last.then_inc(s("sc_full"), 1)
                                    pool.wait_ge(s("ex_ok"), 1)
                                    for t in range(T):
                                        for c in range(2):
                                            if t:
                                                pool.wait_ge(s("pv_used"), 4 * (t - 1) + 2 * (c + 1))
                                            kv = kx[:, t, c * P:c * P + P].rearrange("p (h d) -> p h d", d=DH)
                                            pool.tensor_tensor(pv[:, :, c * P:(c + 1) * P].rearrange("p o (h d) -> p o h d", d=DH),
                                                               spread(ex[:, t, :, 8 * c:8 * c + 8], 3, DH), spread(kv, 1, H, DH), ALU.mult)\
                                                .then_inc(s("pv_ok"), 1)

                            @block.tensor
                            def _(pe):
                                def token_stream():
                                    yield AT["kxmm"]
                                    if b3 is not None:
                                        pe.wait_ge(s("cat_ok"), 2)
                                    pe.wait_ge(s("x_in"), 32)
                                    pe.wait_ge(s("wk_ok"), 1)
                                    for t in range(T):
                                        for m in range(K2):
                                            mm = pe.matmul(bank[SIDE[t // 2]][:, (t % 2) * D:(t % 2 + 1) * D],
                                                           xT[:, m, t * P:(t + 1) * P], wk[:, m, :],
                                                           start=(m == 0), stop=(m == K2 - 1))
                                    mm.then_inc(s("kx_mm"), 1)
                                    yield AT["turn1"]
                                    pe.wait_ge(s("on_ok"), 1)
                                    if b3 is not None:
                                        pe.wait_ge(s("bf_ok"), 4)
                                    for m in range(K2):
                                        for t in range(T):
                                            mm = pe.transpose(bank[SIDE[m]][:, t * P:(t + 1) * P], nA1[:, t, m * P:(m + 1) * P], ident[:])
                                        mm.then_inc(s("aT_mm"), 1)
                                    yield AT["turn1"] + 2
                                    pe.wait_ge(s("aT_ok"), 2)
                                    for o in range(K2):
                                        for m in range(K2):
                                            mm = pe.matmul(bank[SIDE[o]][:], wo[:, m, o * P:(o + 1) * P], aT1[:, m, :],
                                                           start=(m == 0), stop=(m == K2 - 1))
                                        mm.then_inc(s("c_mm"), 1)

                                def router_stream():
                                    srcs = ((x1, None, "x"), (gb[:, :, 2 * D:3 * D], "tt_ok", "t"), (nB, "h_ok", "h"),
                                            (gac[:, :, 0:D], "ss_ok", "s"))
                                    for n, (src, ready, at) in enumerate(srcs):
                                        yield AT[at]
                                        if ready:
                                            pe.wait_ge(s(ready), 1)
                                            pe.wait_ge(s("cat_ok"), 2 * n)
                                            if b1 is not None:
                                                pe.wait_ge(s("kx_half"), 1)
                                        for m in range(K2):
                                            for t in range(T):
                                                mm = pe.transpose(bank[SIDE[m]][:, t * P:(t + 1) * P], src[:, t, m * P:(m + 1) * P], ident[:])
                                            mm.then_inc(s("cat_mm"), 1)
                                    yield AT["u"]
                                    pe.wait_ge(s("cat_ok"), 8)
                                    order = (0, 1, 4, 5, 6, 7, 2, 3)
                                    for o in range(K2):
                                        for n in range(8):
                                            mm = pe.matmul(bank[SIDE[o]][:], wint[:, order[n], o * P:(o + 1) * P], cat[:, n, :],
                                                           start=(n == 0), stop=(n == 7))
                                            if n == 3:
                                                yield AT["u"] + 2 * o + 1
                                        mm.then_inc(s("u_mm"), 1)
                                        yield AT["u"] + 2 * o + 2
                                    yield AT["y"]
                                    pe.wait_ge(s("u_ok"), 2)
                                    for t in range(T):
                                        for m in range(K2):
                                            mm = pe.matmul(bank[SIDE[t // 2]][:, (t % 2) * D:(t % 2 + 1) * D], aT3[:, m, t * P:(t + 1) * P],
                                                           wint2[:, m, :], start=(m == 0), stop=(m == K2 - 1))
                                    mm.then_inc(s("y_mm"), 1)
                                    yield AT["f"]
                                    pe.wait_ge(s("f_ok"), 1)
                                    for m in range(K2):
                                        for t in range(T):
                                            mm = pe.transpose(bank[SIDE[m]][:, t * P:(t + 1) * P], nB[:, t, m * P:(m + 1) * P], ident[:])
                                        mm.then_inc(s("fT_mm"), 1)
                                    yield AT["f"] + 2
                                    pe.wait_ge(s("fT_ok"), 2)
                                    for t in range(T):
                                        for m in range(K2):
                                            mm = pe.matmul(bank[SIDE[0]][:, t * E:(t + 1) * E], hT[:, m, t * P:(t + 1) * P], wr[:, m, :],
                                                           start=(m == 0), stop=(m == K2 - 1))
                                    mm.then_inc(s("r_mm"), 1)
                                    yield AT["pos"]
                                    pe.wait_ge(s("pick_ok"), 1)
                                    for t in range(T):
                                        for j in range(t + 1):
                                            mm = pe.matmul(bank[SIDE[1]][:, t * E:(t + 1) * E], (tri if j == t else ones)[:], picks[:, j, :],
                                                           start=(j == 0), stop=(j == t))
                                    mm.then_inc(s("pos_mm"), 1)
                                    w = SLOTS // 2
                                    for m in range(K2):
                                        for c in range(2):
                                            yield AT["disp"] + 3 * m + c
                                            pe.wait_ge(s("disp_ok"), T)
                                            if m:
                                                pe.wait_ge(s("bf_ok"), c + 1)
                                            for t in range(T):
                                                mm = pe.matmul(bank[SIDE[c]][:, 0:w], nB[:, t, m * P:(m + 1) * P],
                                                               disp[:, t, c * w:(c + 1) * w], start=(t == 0), stop=(t == T - 1))
                                            mm.then_inc(s("bf_mm"), 1)

                                def project():
                                    pe.wait_ge(s("c0_ok"), 1)
                                    for t in range(T):
                                        if t >= 2:
                                            pe.wait_ge(s("qk_ev"), t - 1)
                                            pe.wait_ge(s("vl_ok"), t - 1)
                                        bq, bl = bank[2 * (t % 2)], bank[2 * (t % 2) + 1]
                                        now = lambda m: cT[:, m, 1 + t * P:1 + (t + 1) * P]
                                        before = lambda m: cT[:, m, t * P:(t + 1) * P]
                                        for lo, hi, at in ((0, 448, now), (448, 512, before)):
                                            for m in range(K2):
                                                mm = pe.matmul(bl[:, lo:hi], at(m), wvl[:, m, lo:hi],
                                                               start=(m == 0), stop=(m == K2 - 1))
                                        mm.then_inc(s("vl_mm"), 1)
                                        for m in range(K2):
                                            mm = pe.matmul(bq[:], now(m), wqk[:, m, :], start=(m == 0), stop=(m == K2 - 1))
                                        mm.then_inc(s("qk_mm"), 1)

                                def turn_features():
                                    pe.wait_ge(s("qk_ok"), 1)
                                    pe.wait_ge(s("pad_ok"), 1)
                                    for g in range(HG):
                                        for side in range(2):
                                            n = 2 * g + side
                                            if g >= 2:
                                                pe.wait_ge(s(f"qkT_ok{g % 2}"), side + 1)
                                            for t in range(T):
                                                src = qk[:, t, side, HG * g:HG * g + HG, :].rearrange("p h r -> p (h r)")
                                                mm = pe.transpose(bank[n % 4][:, t * P:(t + 1) * P], src, ident[:])
                                            mm.then_inc(s("qkT_mm"), 1)
                                    pe.wait_ge(s("qkT_ok0"), 4)
                                    pe.wait_ge(s("qkT_ok1"), 4)
                                    pe.wait_ge(s("v_ok"), 1)
                                    pe.wait_ge(s("gap_ok"), 1)

                                def score(u):
                                    h, i = units[u]
                                    g, r = h // HG, 32 * (h % HG)
                                    q = qT[r:r + 32, g, i * P:(i + 1) * P]
                                    if i == T - 1:
                                        if long_before[u]:
                                            pe.wait_ge(s("inc_used"), long_before[u])
                                        if u == N // 2 + 2 * T:
                                            pe.wait_ge(s("att_ok"), 1)
                                        pe.matmul(bank[2][:, 0:P], q, kk[r:r + 32, g, (NKB - 1) * P:NKB * P], start=True, stop=True)
                                    if u >= 2:
                                        pe.wait_ge(s("exp_ok"), u - 1)
                                    lg = bank[u % 2]
                                    n = min(i + 2, T) * P
                                    pe.matmul(lg[:, 0:n], q, kk[r:r + 32, g, T * i * P:T * i * P + n], start=True, stop=False)
                                    pe.matmul(lg[:, i * P:(i + 1) * P], identb[:], negb[:], start=False, stop=True)\
                                        .then_inc(s("score_mm"), 1)

                                def turn(u):
                                    h, i = units[u]
                                    pe.wait_ge(s("exp_ok"), u + 1)
                                    if u >= 2:
                                        pe.wait_ge(s("prT_ok"), u - 1)
                                    for j in range(i + 1):
                                        mm = pe.transpose(bank[3 + u % 2][:, j * P:(j + 1) * P], pr[:, u % 3, j * P:(j + 1) * P], ident[:])
                                    mm.then_inc(s("turn_mm"), 1)

                                def values(u):
                                    h, i = units[u]
                                    pe.wait_ge(s("prT_ok"), u + 1)
                                    if u == N // 2:
                                        pe.wait_ge(s("raw_ok"), 1)
                                    p, c = h // 2, h % 2
                                    r = 32 * (p % HG)
                                    for j in range(i + 1):
                                        mm = pe.matmul(bank[5][r:r + 32, i * P:(i + 1) * P], vp[:, j, p, DH * c:DH * c + 2 * DH],
                                                       prT[:, u % 3, j * P:(j + 1) * P], start=(c == 0 and j == 0), stop=(c == 1 and j == i))
                                    mm.then_inc(s("val_mm"), 1)

                                def turn_sums(c):
                                    pe.wait_ge(s("rinv_ok"), c + 1)
                                    pe.wait_ge(s("inc_used"), H // 2 + 2 if c == 0 else H)
                                    for t in range(T):
                                        mm = pe.transpose(bank[2][0:H // 2, t * P:(t + 1) * P], rinv[:, t, 8 * c:8 * c + 8], ident[:])
                                    mm.then_inc(s("rT_mm"), 1)

                                def broadcast_sums(c):
                                    pe.wait_ge(s("rT_ok"), c + 1)
                                    pe.matmul(bank[2][:], sel[:], rT, start=True, stop=True).then_inc(s("rb_mm"), 1)

                                def unit(u):
                                    turn(u)
                                    if u + 2 < N:
                                        score(u + 2)
                                    if u >= 1:
                                        values(u - 1)
                                    if u == N // 2 + 1:
                                        turn_sums(0)
                                    if u == N // 2 + 2:
                                        broadcast_sums(0)

                                side = started(*[g() for g, on in ((router_stream, b3), (token_stream, b1)) if on is not None])
                                advance(side, AT["x"])
                                if b2 is not None:
                                    project()
                                advance(side, AT["kxmm"])
                                if b2 is not None:
                                    turn_features()
                                    score(0)
                                    score(1)
                                interleave(unit, side)
                                if b2 is not None:
                                    turn_sums(1)
                                    values(N - 1)
                                    broadcast_sums(1)
                                    pe.wait_ge(s("att_ok"), 2)
                                    for c in range(2):
                                        for t in (2 * c, 2 * c + 1):
                                            for m in range(K2):
                                                mm = pe.matmul(bank[c][:, (t % 2) * D:(t % 2 + 1) * D], aT2[:, m, t * P:(t + 1) * P],
                                                               wout[:, m, :], start=(m == 0), stop=(m == K2 - 1))
                                        mm.then_inc(s("out_mm"), 1)

                            @block.scalar
                            def _(act):
                                done, settle = chain_of(act, s("act_own"))

                                def token_stream():
                                    yield AT["kx"]
                                    act.wait_ge(s("kx_half"), 1)
                                    act.copy(kx[:, :, D:2 * D], kx[:, :, 0:D]).then_inc(s("kx_dup"), 1)
                                    yield AT["full"] + 2
                                    act.wait_ge(s("ex_in"), 1)
                                    act.activation(ex[:], ex[:], ACT.Exp, scale=0.25).then_inc(s("ex_ok"), 1)
                                    yield AT["turn1"] + 1
                                    for m in range(K2):
                                        act.wait_ge(s("aT_mm"), m + 1)
                                        act.copy(aT1[:, m, :], bank[SIDE[m]][:]).then_inc(s("aT_ok"), 1)
                                    yield AT["turn1"] + 3
                                    act.wait_ge(s("wk_ok"), 1)
                                    if b2 is not None:
                                        act.wait_ge(s("qk_mm"), T)
                                    for o in range(K2):
                                        act.wait_ge(s("c_mm"), o + 1)
                                        act.activation(cT[:, o, 1:S + 1], bank[SIDE[o]][:], ACT.Identity,
                                                       bias=obcol[:, o:o + 1], scale=pc1[:, 4 + o:5 + o])

                                def router_stream():
                                    sd = lambda n: act.activation(mv[:, :, 2:3], mv[:, :, 1:2], ACT.Sqrt, bias=eps_ln[:, 0:1])\
                                        .then_inc(s(f"sd{n}"), 1)

                                    def out_of_bank(n):
                                        for m in range(K2):
                                            act.wait_ge(s("cat_mm"), 2 * n + m + 1)
                                            act.copy(cat[:, 2 * n + m, :], bank[SIDE[m]][:]).then_inc(s("cat_ok"), 1)

                                    yield AT["x"]
                                    act.wait_ge(s("var1"), 1)
                                    sd(1)
                                    out_of_bank(0)
                                    yield AT["var2"]
                                    act.wait_ge(s("var2"), 1)
                                    sd(2)
                                    yield AT["t"] + 1
                                    out_of_bank(1)
                                    yield AT["h"] + 1
                                    out_of_bank(2)
                                    yield AT["s"] + 1
                                    out_of_bank(3)
                                    yield AT["u"] + 5
                                    for o in range(K2):
                                        act.wait_ge(s("u_mm"), o + 1)
                                        act.activation(aT3[:, o, :], bank[SIDE[o]][:], ACT.Silu, bias=pc3[:, 6 + o:7 + o]).then_inc(s("u_ok"), 1)
                                    yield AT["y"] + 3
                                    act.wait_ge(s("var3"), 1)
                                    sd(3)
                                    yield AT["f"] + 1
                                    for m in range(K2):
                                        act.wait_ge(s("fT_mm"), m + 1)
                                        act.copy(hT[:, m, :], bank[SIDE[m]][:]).then_inc(s("fT_ok"), 1)
                                    yield AT["f"] + 4
                                    act.wait_ge(s("re_in"), 1)
                                    act.activation(pe8[:, 0], pe8[:, 0], ACT.Exp).then_inc(s("re_ok"), 1)
                                    w = SLOTS // 2
                                    for n in range(4):
                                        yield AT["disp"] + 3 * (n // 2) + n % 2 + 1
                                        act.wait_ge(s("bf_mm"), n + 1)
                                        act.copy(bfT[:, n // 2, (n % 2) * w:(n % 2 + 1) * w], bank[SIDE[n % 2]][:, 0:w]).then_inc(s("bf_ok"), 1)

                                def exps(u):
                                    h, i = units[u]
                                    n = (i + 1) * P
                                    act.wait_ge(s("max_ok"), u + 1)
                                    if u >= 3:
                                        act.wait_ge(s("turn_mm"), u - 2)
                                    act.activation(pr[:, u % 3, 0:n], bank[u % 2][:, 0:n], ACT.Exp, bias=nmax[:, u % 4:u % 4 + 1],
                                                   accum_out=rsum[:, i, h:h + 1]).then_inc(s("exp_ok"), 1)

                                def turned(u):
                                    n = (units[u][1] + 1) * P
                                    act.wait_ge(s("turn_mm"), u + 1)
                                    if u >= 3:
                                        act.wait_ge(s("val_mm"), u - 2)
                                    act.copy(prT[:, u % 3, 0:n], bank[3 + u % 2][:, 0:n]).then_inc(s("prT_ok"), 1)

                                def raw_out(c):
                                    act.wait_ge(s("val_mm"), (c + 1) * N // 2)
                                    act.copy(aT2[:, c, :], bank[5][:]).then_inc(s("raw_ok"), 1)

                                def sums_out(c):
                                    act.wait_ge(s("rT_mm"), c + 1)
                                    act.copy(rT, bank[2][0:H // 2, :]).then_inc(s("rT_ok"), 1)

                                def unit(u):
                                    if u + 1 < N:
                                        exps(u + 1)
                                    turned(u)
                                    if u == N // 2:
                                        raw_out(0)
                                    if u == N // 2 + 1:
                                        sums_out(0)

                                side = started(*[g() for g, on in ((router_stream, b3), (token_stream, b1)) if on is not None])
                                advance(side, AT["x"])
                                if b2 is not None:
                                    for t in range(T):
                                        act.wait_ge(s("vl_mm"), t + 1)
                                        bl = bank[2 * (t % 2) + 1]
                                        act.copy(bass.AP(vp, v_of(t, 0).offset, [list(v_of(t, 0).ap[0]), [3 * DH, H // 2], [2 * DH, 2], [1, DH]]),
                                                 bl[:, 0:D].rearrange("p (n c d) -> p n c d", c=2, d=DH))
                                        for dst, src in ((0, D), (64, D + 192), (128, D + 64)):
                                            n = 128 if dst == 128 else 64
                                            last = act.copy(pts[:, t, dst:dst + n], bl[:, src:src + n])
                                        last.then_inc(s("vl_ok"), 1)
                                    act.wait_ge(s("len2"), 1)
                                    act.activation(ln[:], ln[:], ACT.Sqrt).then_inc(s("len_ok"), 1)
                                    for g in (0, 2):
                                        act.wait_ge(s("qkT_mm"), 2 * g + 1)
                                        act.copy(qT[:, g, :], bank[(2 * g) % 4][:]).then_inc(s("qkT_ok0"), 1)
                                        act.wait_ge(s("qkT_mm"), 2 * g + 2)
                                        src = bank[(2 * g + 1) % 4]
                                        for at, n, v in KEYS:
                                            last = act.activation(blocks(g, at, n), tiles_of(src, n), ACT.Copy, scale=fack[:, g, v:v + 1])
                                        last.then_inc(s("qkT_ok0"), 1)
                                advance(side, -1)
                                if b2 is not None:
                                    exps(0)
                                interleave(unit, side)
                                if b2 is not None:
                                    sums_out(1)
                                    raw_out(1)

                            @block.vector
                            def _(dve):
                                done, settle = chain_of(dve, s("dve_own"))

                                def token_weights():
                                    done(dve.tensor_copy(pc1[:], pcol[:, b1, :]))
                                    settle()
                                    for m in range(K2):
                                        done(dve.tensor_scalar(wk[:, m, :], kow[:, 0, m, :], pc1[:, m:m + 1], None, ALU.mult))
                                        dve.tensor_scalar(wo[:, m, :], kow[:, 1, m, :], pc1[:, 2 + m:3 + m], None, ALU.mult)
                                    settle()
                                    dve.wait_ge(s("x_in"), 32)
                                    dve.tensor_tensor(wk, wk, spread(demk[:], 1, K2), ALU.mult).then_inc(s("wk_ok"), 1)

                                def token_stream():
                                    yield AT["kx"]
                                    dve.wait_ge(s("kx_mm"), 1)
                                    for c in range(2):
                                        last = dve.tensor_tensor(kx[:, 2 * c:2 * c + 2, 0:D],
                                                                 bank[SIDE[c]][:].rearrange("p (t f) -> p t f", t=2),
                                                                 spread(row("kb"), 1, 2), ALU.add)
                                    last.then_inc(s("kx_half"), 1)
                                    for t in range(T):
                                        parts = ((0, 5), (5, 9))
                                        for n, (lo, hi) in enumerate(parts):
                                            yield AT["pair"] + 4 * t + n
                                            dve.wait_ge(s("kx_dup"), 1)
                                            if t and n == 0:
                                                dve.wait_ge(s("sc_low"), 2 * t)
                                            done(dve.tensor_tensor(prod[:, lo:hi], spread(kx[:, t, 0:D], 1, hi - lo),
                                                                   spread(kx[:, t, DH * lo:DH * lo + D], 1, hi - lo, DH), ALU.mult))
                                        for n, (lo, hi) in enumerate(parts):
                                            yield AT["pair"] + 4 * t + 2 + n
                                            if n == 0:
                                                settle()
                                            dve.tensor_reduce(sc[:, t, lo:hi, 0:H], prod[:, lo:hi].rearrange("p o (h d) -> p o h d", d=DH),
                                                              X, ALU.add).then_inc(s("sc_low"), 1)
                                    yield AT["full"] + 1
                                    dve.wait_ge(s("sc_full"), 1)
                                    for t in range(T):
                                        done(dve.tensor_reduce(mx[:, t, :], sc[:, t, :, 0:H].rearrange("p o h -> p h o"), X, ALU.max))
                                    settle()
                                    for t in range(T):
                                        last = dve.tensor_tensor(ex[:, t], sc[:, t, :, 0:H], spread(mx[:, t, :], 1, H), ALU.subtract)
                                    last.then_inc(s("ex_in"), 1)
                                    yield AT["full"] + 3
                                    dve.wait_ge(s("ex_ok"), 1)
                                    for t in range(T):
                                        done(dve.tensor_reduce(mx[:, t, :], ex[:, t].rearrange("p o h -> p h o"), X, ALU.add))
                                    settle()
                                    done(dve.reciprocal(rs[:], mx[:]))
                                    for t in range(T):
                                        for c in range(4):
                                            yield AT["full"] + 6 + 6 * t + (0, 1, 3, 4)[c]
                                            dve.wait_ge(s("pv_ok"), 2 * t + c // 2 + 1)
                                            w = D // 4
                                            dve.tensor_reduce(nA1[:, t, c * w:(c + 1) * w], pv[:, :, c * w:(c + 1) * w].rearrange("p o f -> p f o"),
                                                              X, ALU.add).then_inc(s("pv_used"), 1)
                                    yield AT["turn1"] - 1
                                    settle()
                                    dve.wait_ge(s("pv_used"), 4 * T)
                                    nv = nA1.rearrange("p t (h d) -> p (t h) d", d=DH)
                                    dve.tensor_tensor(nv, nv, spread(rs[:].rearrange("p t h -> p (t h)"), 2, DH), ALU.mult)\
                                        .then_inc(s("on_ok"), 1)

                                def moments(src, var):
                                    for t in range(T):
                                        done(dve.bn_stats(stat[:, t, :], src[:, t, :]))
                                    settle()
                                    for t in range(T):
                                        last = dve.bn_aggr(mv[:, t, 0:2], stat[:, t, :])
                                    last.then_inc(s(var), 1)

                                def normed(dst, src, sd, ready=None):
                                    dve.wait_ge(s(sd), 1)
                                    done(dve.reciprocal(mv[:, :, 3:4], mv[:, :, 2:3]))
                                    settle()
                                    for t in range(T):
                                        ins = dve.tensor_scalar(dst[:, t, :], src[:, t, :], mv[:, t, 0:1], mv[:, t, 3:4],
                                                                ALU.subtract, ALU.mult)
                                        ins.then_inc(s(ready), 1) if ready else done(ins)
                                    if ready:
                                        dve.wait_ge(s(ready), T)
                                    else:
                                        settle()

                                def affine(dst, src, gain, off, second, ready):
                                    done(dve.tensor_tensor(dst[:], src, gain, ALU.mult))
                                    yield second
                                    settle()
                                    dve.tensor_tensor(dst[:], dst[:], off, ALU.add).then_inc(s(ready), 1)
                                    dve.wait_ge(s(ready), 1)

                                def router_stream():
                                    yield AT["var1"]
                                    moments(x1, "var1")
                                    done(dve.tensor_copy(pc3[:], pcol[:, b3, :]))
                                    yield AT["z"]
                                    normed(nA, x1, "sd1", "z_ok")
                                    yield AT["h1"]
                                    for t in range(T):
                                        dve.wait_ge(s(f"gath{t}"), 16)
                                    yield from affine(nB, nA[:], gac[:, :, 0:D], gac[:, :, D:2 * D], AT["h1b"], "h1_ok")
                                    yield AT["var2"]
                                    moments(nB, "var2")
                                    yield AT["h2"]
                                    normed(nB, nB, "sd2")
                                    yield AT["h2"] + 1
                                    for t in range(T):
                                        dve.wait_ge(s(f"gath{t}"), 32)
                                    yield from affine(nB, nB[:], gb[:, :, 0:D], gb[:, :, D:2 * D], AT["h2"] + 2, "h_ok")
                                    yield AT["y"] + 1
                                    dve.wait_ge(s("y_mm"), 1)
                                    for c in range(2):
                                        done(dve.tensor_tensor(nB[:, 2 * c:2 * c + 2, :], bank[SIDE[c]][:].rearrange("p (t f) -> p t f", t=2),
                                                               spread(row("b2"), 1, 2), ALU.add))
                                    settle()
                                    yield AT["y"] + 2
                                    moments(nB, "var3")
                                    yield AT["y"] + 4
                                    normed(nB, nB, "sd3")
                                    yield AT["y"] + 5
                                    yield from affine(nB, nB[:], spread(row("g"), 1, T), spread(row("be"), 1, T), AT["y"] + 6, "f_ok")
                                    q = lambda k: pe8[:, k]
                                    step = lambda ins: (done(ins), settle())
                                    yield AT["f"] + 3
                                    dve.wait_ge(s("r_mm"), 1)
                                    step(dve.tensor_tensor(q(0), bank[SIDE[0]][:, 0:T * E].rearrange("p (t e) -> p t e", e=E),
                                                           spread(row("br"), 1, T), ALU.add))
                                    step(dve.tensor_reduce(sm[:, 0], q(0), X, ALU.max))
                                    dve.tensor_tensor(q(0), q(0), spread(sm[:, 0], 2, E), ALU.subtract).then_inc(s("re_in"), 1)
                                    yield AT["f"] + 5
                                    dve.wait_ge(s("re_ok"), 1)
                                    step(dve.tensor_reduce(sm[:, 1], q(0), X, ALU.add))
                                    step(dve.reciprocal(sm[:, 1], sm[:, 1]))
                                    step(dve.tensor_tensor(q(0), q(0), spread(sm[:, 1], 2, E), ALU.mult))
                                    io = spread(iota[:, 0:E], 1, T)
                                    for k in range(2):
                                        yield AT["f"] + 6 + k
                                        pk, mk, ix, oh = q(0 if k == 0 else 3), sm[:, 2 + k], sm[:, 4 + k], q(1 + k)
                                        step(dve.tensor_reduce(mk, pk, X, ALU.max))
                                        step(dve.tensor_tensor(q(4), pk, spread(mk, 2, E), ALU.is_ge))
                                        step(dve.tensor_scalar(q(4), q(4), -float(E), float(E), ALU.mult, ALU.add))
                                        step(dve.tensor_tensor(q(4), q(4), io, ALU.add))
                                        step(dve.tensor_reduce(ix, q(4), X, ALU.min))
                                        step(dve.tensor_tensor(oh, io, spread(ix, 2, E), ALU.is_equal))
                                        if k == 0:
                                            step(dve.tensor_scalar(q(4), oh, -2.0, None, ALU.mult))
                                            step(dve.tensor_tensor(q(3), pk, q(4), ALU.add))
                                    dve.tensor_tensor(picks[:], q(1), q(2), ALU.add).then_inc(s("pick_ok"), 1)
                                    yield AT["pos"] + 1
                                    dve.wait_ge(s("pos_mm"), 1)
                                    step(dve.tensor_copy(q(6), bank[SIDE[1]][:, 0:T * E].rearrange("p (t e) -> p t e", e=E)))
                                    for k in range(2):
                                        yield AT["pos"] + 1 + k
                                        at, keep, slot = sm[:, 6 + k], sm[:, 8 + k], sm[:, 10 + k]
                                        step(dve.tensor_tensor(q(7), q(6), q(1 + k), ALU.mult))
                                        step(dve.tensor_reduce(at, q(7), X, ALU.add))
                                        step(dve.tensor_scalar(keep, at, float(CAP), None, ALU.is_lt))
                                        step(dve.tensor_scalar(at, at, float(CAP - 1), None, ALU.min))
                                        step(dve.tensor_scalar(slot, sm[:, 4 + k], float(CAP), 1.0, ALU.mult, ALU.add))
                                        step(dve.tensor_tensor(slot, slot, at, ALU.add))
                                        step(dve.tensor_tensor(slot, slot, keep, ALU.mult))
                                        step(dve.tensor_scalar(slot, slot, -1.0, None, ALU.add))
                                        if k == 0:
                                            dve.wait_ge(s("ids_in"), 32)
                                        done(dve.tensor_tensor(gi[:, k], sm[:, 2 + k], keep, ALU.mult))
                                        step(dve.tensor_scalar(sm[:, 12], sm[:, 4 + k], float(ROWS), boff[:, 0:1], ALU.mult, ALU.add))
                                        last = dve.tensor_tensor(gi[:, 2 + k], sm[:, 12], at, ALU.add)
                                        if k == 0:
                                            step(last)
                                        else:
                                            last.then_inc(s("gi_ok"), 1)
                                    for t in range(T):
                                        yield AT["disp"] - T + t
                                        step(dve.tensor_scalar(disp[:, t, :], iota[:], sm[:, 10, t:t + 1], None, ALU.is_equal))
                                        dve.scalar_tensor_tensor(disp[:, t, :], iota[:], sm[:, 11, t:t + 1], disp[:, t, :],
                                                                 ALU.is_equal, ALU.add).then_inc(s("disp_ok"), 1)

                                def features():
                                    for t in range(T):
                                        dve.wait_ge(s("qk_mm"), t + 1)
                                        dve.tensor_tensor(qk[:, t, :, :, 0:DH].rearrange("p s h d -> p (s h) d"),
                                                          bank[2 * (t % 2)][:].rearrange("p (s d) -> p s d", d=DH),
                                                          row("bqk").rearrange("p (s d) -> p s d", d=DH), ALU.add)\
                                            .then_inc(s("qk_ev"), 1)
                                        if t == 0:
                                            advance(side, AT["z"])
                                    dve.wait_ge(s("vl_ok"), T)
                                    pa = pts[:, :, 0:P].rearrange("p t (s c) -> p t s c", c=4)
                                    pb = pts[:, :, P:2 * P].rearrange("p t (s c) -> p t s c", c=4)
                                    for dst, u, v in ((la, pa, pb), (lb, pb, pa)):
                                        for c, lo, n in ((0, 0, 3), (1, 3, 2), (2, 5, 1)):
                                            done(dve.tensor_tensor(dst[:, :, :, lo:lo + n], spread(u[:, :, :, c], 3, n), v[:, :, :, c + 1:4], ALU.mult))
                                    settle()
                                    done(dve.tensor_tensor(la, la, lb, ALU.subtract))
                                    settle()
                                    done(dve.tensor_tensor(lb, la, la, ALU.mult))
                                    settle()
                                    dve.tensor_reduce(ln[:], lb, X, ALU.add).then_inc(s("len2"), 1)
                                    done(dve.tensor_tensor(la, la, spread(sign[:], 1, T), ALU.mult))
                                    dve.wait_ge(s("len_ok"), 1)
                                    done(dve.tensor_scalar(ln[:], ln[:], 1e-12, None, ALU.max))
                                    settle()
                                    done(dve.reciprocal(ln[:], ln[:]))
                                    settle()
                                    done(dve.tensor_tensor(lf[:, 0], ln[:, :, 0:H], spread(facr[:], 1, T), ALU.mult))
                                    done(dve.tensor_tensor(lf[:, 1], ln[:, :, 0:H], spread(row("bs"), 1, T), ALU.mult))
                                    done(dve.tensor_tensor(lf[:, 2], ln[:, :, H:2 * H], spread(facw[:], 1, T), ALU.mult))
                                    done(dve.tensor_copy(lf[:, 3], ln[:, :, H:2 * H]))
                                    settle()
                                    for n in range(4):
                                        line, at = n // 2, DH + NOFF * (n % 2)
                                        src = la[:, :, H * line:H * line + H, :]
                                        if line:
                                            src = src[:, :, :, ::-1]
                                        last = dve.tensor_tensor(qk[:, :, line, :, at:at + NOFF], src, spread(lf[:, n], 3, NOFF), ALU.mult)
                                    last.then_inc(s("qk_ok"), 1)
                                    advance(side, AT["h1"])
                                    for g in (1, 3):
                                        dve.wait_ge(s("qkT_mm"), 2 * g + 1)
                                        dve.tensor_copy(qT[:, g, :], bank[(2 * g) % 4][:]).then_inc(s("qkT_ok1"), 1)
                                        dve.wait_ge(s("qkT_mm"), 2 * g + 2)
                                        src = bank[(2 * g + 1) % 4]
                                        for at, n, v in KEYS:
                                            last = dve.tensor_scalar(blocks(g, at, n), tiles_of(src, n), fack[:, g, v:v + 1], None, ALU.mult)
                                        last.then_inc(s("qkT_ok1"), 1)

                                def invert(c):
                                    dve.wait_ge(s("exp_ok"), (c + 1) * N // 2)
                                    dve.reciprocal(rinv[:, :, 8 * c:8 * c + 8], rsum[:, :, 8 * c:8 * c + 8]).then_inc(s("rinv_ok"), 1)

                                def divide(c):
                                    dve.wait_ge(s("raw_ok"), c + 1)
                                    dve.wait_ge(s("rb_mm"), c + 1)
                                    dve.tensor_tensor(aT2[:, c, :], aT2[:, c, :], bank[2][:], ALU.mult).then_inc(s("att_ok"), 1)

                                def unit(u):
                                    h, i = units[u]
                                    dve.wait_ge(s("score_mm"), u + 1)
                                    lg = bank[u % 2]
                                    db = dbias[:, u % 2]
                                    if i == T - 1:
                                        dve.tensor_tensor(db, bank[2][:, 0:P], wdiag[:, h, :], ALU.mult).then_inc(s("inc_used"), 1)
                                        dve.wait_ge(s("inc_used"), long_before[u] + 1)
                                    else:
                                        done(dve.tensor_tensor(db, lg[:, (i + 1) * P:(i + 2) * P], wdiag[:, h, :], ALU.mult))
                                        settle()
                                    dg = lg[:, i * P:(i + 1) * P]
                                    done(dve.tensor_tensor(dg, dg, db, ALU.add))
                                    settle()
                                    if u >= 4:
                                        dve.wait_ge(s("exp_ok"), u - 3)
                                    dve.tensor_reduce(nmax[:, u % 4:u % 4 + 1], lg[:, 0:(i + 1) * P], X, ALU.max,
                                                      negate=True).then_inc(s("max_ok"), 1)
                                    if u == N // 2 + 1:
                                        invert(0)
                                    if u == N // 2 + 4:
                                        divide(0)

                                side = started(*[g() for g, on in ((router_stream, b3), (token_stream, b1)) if on is not None])
                                advance(side, AT["var1"])
                                if b1 is not None:
                                    token_weights()
                                if b2 is not None:
                                    features()
                                interleave(unit, side)
                                if b2 is not None:
                                    invert(1)
                                    divide(1)
                                    dve.wait_ge(s("xb_ok"), 1)
                                    if b3 is not None:
                                        dve.wait_ge(s("cat_mm"), 2)
                                        dve.wait_ge(s("x1_out"), 16)
                                    for c in range(2):
                                        dve.wait_ge(s("out_mm"), c + 1)
                                        last = dve.tensor_tensor(x1[:, 2 * c:2 * c + 2, :], bank[c][:].rearrange("p (t f) -> p t f", t=2),
                                                                 xN[:, 2 * c:2 * c + 2, :], ALU.add)
                                    last.then_inc(s("x1_ok"), 1)
                        s.clear()

                if "A" in parts:
                    iteration(0, None, None)
                    iteration(1, 0, None)
                    with nc.Fori(1, B - 1) as b:
                        iteration(b + 1, b, b - 1)
                    iteration(None, B - 1, B - 2)
                    iteration(None, None, B - 1)

        def expert_loop():
            ctx = ExitStack()
            with ctx:
                sb = lambda name, shape, dt=F32: sb_in(ctx, name, shape, dt)
                ew1 = sb("ew1", [P, 2, K2, HID])
                ew2 = sb("ew2", [P, 2, KH, D])
                eb1 = sb("eb1", [P, 2, KH])
                eb2 = sb("eb2", [P, 2, D])
                eb = sb("eb", [P, 2, K2, ROWS])
                hid = sb("hid", [P, KH, ROWS])
                yy = sb("yy", [P, 2, ST, D])
                W = ROWS // 2
                with nc.Fori(0, E // 2) as e2:
                    sctx = ExitStack()
                    with sctx:
                        s = Sems(sctx, "e")
                        with nc.Block() as block:
                            @block.sync
                            def _(sp):
                                for k in range(2):
                                    for dst, src in ((ew1[:, k], a["eW1"][2 * e2 + k]), (eb[:, k].rearrange("p m r -> p (m r)"),
                                                     buf_d[2 * e2 + k].rearrange("p m b c -> p (m b c)")),
                                                     (eb1[:, k], a["eb1"][2 * e2 + k]), (ew2[:, k], a["eW2"][2 * e2 + k]),
                                                     (eb2[:, k], spread(a["eb2"][2 * e2 + k, :], 0, P))):
                                        sp.dma_start(dst, src).then_inc(s(f"w_in{k}"), 16)
                                for k in range(2):
                                    sp.wait_ge(s("y_ok"), ST * (k + 1))
                                    sp.dma_start(y_d.rearrange("(e t p) d -> e p t d", p=P, t=ST)[2 * e2 + k], yy[:, k]).then_inc(s("y_out"), 16)
                                sp.wait_ge(s("y_out"), 32)

                            @block.tensor
                            def _(pe):
                                for k in range(2):
                                    pe.wait_ge(s(f"w_in{k}"), 80)
                                    for n in range(2 * KH):
                                        o, c = n // 2, n % 2
                                        if k * 2 * KH + n >= 4:
                                            pe.wait_ge(s("h_ok"), k * 2 * KH + n - 3)
                                        for m in range(K2):
                                            mm = pe.matmul(bank[n % 4][:, 0:W], ew1[:, k, m, o * P:(o + 1) * P],
                                                           eb[:, k, m, c * W:(c + 1) * W], start=(m == 0), stop=(m == K2 - 1))
                                        mm.then_inc(s("h_mm"), 1)
                                    pe.wait_ge(s("h_ok"), 2 * KH * (k + 1))
                                    for t in range(ST):
                                        n = k * ST + t
                                        if n >= 4:
                                            pe.wait_ge(s("y_ok"), n - 3)
                                        for m in range(KH):
                                            mm = pe.matmul(bank[4 + n % 4][:, 0:D], hid[:, m, t * P:(t + 1) * P], ew2[:, k, m, :],
                                                           start=(m == 0), stop=(m == KH - 1))
                                        mm.then_inc(s("y_mm"), 1)

                            @block.scalar
                            def _(act):
                                for k in range(2):
                                    act.wait_ge(s(f"w_in{k}"), 80)
                                    if k:
                                        act.wait_ge(s("y_mm"), ST * k)
                                    for n in range(2 * KH):
                                        act.wait_ge(s("h_mm"), k * 2 * KH + n + 1)
                                        act.activation(hid[:, n // 2, (n % 2) * W:(n % 2 + 1) * W], bank[n % 4][:, 0:W], ACT.Relu,
                                                       bias=eb1[:, k, n // 2:n // 2 + 1]).then_inc(s("h_ok"), 1)

                            @block.vector
                            def _(dve):
                                for k in range(2):
                                    dve.wait_ge(s(f"w_in{k}"), 80)
                                    for t in range(ST):
                                        n = k * ST + t
                                        dve.wait_ge(s("y_mm"), n + 1)
                                        dve.tensor_tensor(yy[:, k, t, :], bank[4 + n % 4][:, 0:D], eb2[:, k, :], ALU.add)\
                                            .then_inc(s("y_ok"), 1)
                        s.clear()

        if "B" in parts:
            expert_loop()
        if "C" in parts:
            layer1(nc, a, out, bank, ident, sb_in, Sems, chain_of, x1_d, gate_d, y_d, prow_d, wdec_d, PR, R1, n1)


ST_GI, ST_IN, ST_DN, ST_UP, ST_QK, ST_V, ST_KF = range(7)
ST_KV, ST_O, ST_OT, ST_X3, ST_X3T, ST_Y, ST_Q, ST_ACC, STAGES = range(ST_KF + 4, ST_KF + 13)


def layer1(nc, a, out, bank, ident, sb_in, Sems, chain_of, x1_d, gate_d, y_d, prow_d, wdec_d, PR, R1, n1):
    NP = H // 2
    V1 = DH + 1
    l1 = ExitStack()
    with l1:
        sb = lambda name, shape, dt=F32: sb_in(l1, name, shape, dt)
        dup = sb("dup", [P, K2, M])
        upp = sb("upp", [M, D])
        wqkv = sb("wqkv", [P, 3, K2, D])
        wo1 = sb("wo1", [P, K2, D])
        qkcol = sb("qkcol", [P, 2, K2])
        orfk = sb("orfk", [P, 2 * 256])
        nrmk = sb("nrmk", [P, 8])
        nrmq = sb("nrmq", [P, P])
        wq8 = sb("wq8", [P, K2, D // 4], I32)
        wqb = sb("wqb", [P, K2, D], BF16)
        rows = sb("rows1", [P, n1])
        identb = sb("identb1", [P, P], BF16)
        row = lambda f: rows[:, R1[f][0]:R1[f][1]]
        sctx = ExitStack()
        with sctx:
            s = Sems(sctx, "s1")
            with nc.Block() as block:
                @block.sync
                def _(sp):
                    loads = [(dup, "dup"), (upp, "upp"), (wqkv, "wqkv"), (wo1, "wo1"), (qkcol, "qkcol"), (orfk, "orfk"),
                             (nrmk, "nrmk"), (nrmq, "nrmq"), (identb, "identb"), (wq8, "wq8")]
                    for dst, name in loads:
                        sp.dma_start(dst[:], a[name]).then_inc(s("load"), 16)
                    sp.dma_start(rows[:], spread(a["rows1"], 0, P)).then_inc(s("load"), 16)
                    sp.wait_ge(s("load"), 16 * (len(loads) + 1))

                @block.vector
                def _(dve):
                    dve.wait_ge(s("load"), 16 * 11)
                    dve.tensor_copy(wqb[:], wq8[:].bitcast(I8)).then_inc(s("w_ok"), 1)
                    dve.tensor_scalar(orfk[:], orfk[:], 0.5, None, ALU.mult).then_inc(s("w_ok"), 1)
            s.clear()

        LANES = 2
        lane_bufs = []
        for n in range(LANES):
            f = lambda name, shape, dt=F32: sb(f"{name}_{n}", shape, dt)
            v = dict(x2=f("x2", [P, T, D]), gi=f("gi1", [P, 4, T]), gidx=f("gidx", [P, 2, T], I32), yg=f("yg", [P, 2, T, D]),
                     dgb=f("dgb", [P, 2, M]), ugb=f("ugb", [M, 2, D]), brow=f("brow1", [P, D]), wdn=f("wdn", [P, K2, M]),
                     wup=f("wup", [M, D]), wde=f("wde1", [P, K2, D]), xT=f("xT1", [P, K2, S]), dT=f("dT1", [M, S]),
                     hcT=f("hcT", [P, K2, S]), qT=f("qT1", [P, K2, S]), kT=f("kT1", [P, K2, S]), q2=f("q2", [P, K2, S]),
                     k2=f("k2", [P, K2, S]), vn=f("vn1", [P, T, H, V1]), kn=f("kn", [P, T, 2, 8]), kf=f("kf", [P, T, H, M]),
                     qf=f("qf", [P, NP, S]), kv=f("kv", [P, NP, 2 * V1]), den=f("den", [P, T, H]), xb=f("xb1", [P, T, D]),
                     ab=f("ab", [P, 3, T]), yb=f("yb", [P, T, D], BF16), qbT=f("qbT", [P, K2, S], BF16))
            v["x3"], v["fo"] = v["yg"][:, 0], v["yg"][:, 1]
            v["on"] = v["k2"][:].rearrange("p m (a f) -> p (m a) f", f=D)
            v["yq"] = v["x2"]
            v["bank"] = bank[4 * n:4 * n + 4]
            lane_bufs.append(v)

        with nc.Fori(0, B // LANES) as b2:
            sctx = ExitStack()
            with sctx:
                s = Sems(sctx, "c")

                def in_stages(program):
                    live = [program(n, lane_bufs[n], lambda name, n=n: s(f"{name}_{n}")) for n in range(LANES)]
                    due = [next(g) for g in live]
                    for stage in range(STAGES):
                        for n, g in enumerate(live):
                            while due[n] is not None and due[n] <= stage:
                                due[n] = next(g, None)
                    assert due == [None] * LANES

                with nc.Block() as block:
                    @block.sync
                    def _(sp):
                        for n, v in enumerate(lane_bufs):
                            b = LANES * b2 + n
                            sp.dma_start(v["gi"][:].rearrange("p k t -> p (k t)"), gate_d[b]).then_inc(s(f"gi_in_{n}"), 16)
                        for n, v in enumerate(lane_bufs):
                            b = LANES * b2 + n
                            sp.dma_start(v["x2"][:], x1_d[b]).then_inc(s(f"x_in_{n}"), 16)
                            for dst, src in ((v["dgb"][:].rearrange("p k h -> p (k h)"), spread(prow_d[b, PR["dg"][0]:PR["db"][1]], 0, P)),
                                             (v["ugb"][:].rearrange("p k h -> p (k h)"), spread(prow_d[b, PR["ug"][0]:PR["ub"][1]], 0, M)),
                                             (v["brow"][:], spread(prow_d[b, PR["bias"][0]:PR["bias"][1]], 0, P)),
                                             (v["wde"][:], wdec_d[b])):
                                sp.dma_start(dst, src).then_inc(s(f"p_in_{n}"), 16)
                        for n, v in enumerate(lane_bufs):
                            sp.wait_ge(s(f"fin_{n}"), 1)
                            sp.dma_start(out[LANES * b2 + n].rearrange("(t p) d -> p t d", p=P), v["fo"]).then_inc(s(f"out_{n}"), 16)
                        for n in range(LANES):
                            sp.wait_ge(s(f"out_{n}"), 16)

                    @block.gpsimd
                    def _(pool):
                        def lane(n, v, s):
                            yield ST_IN
                            pool.wait_ge(s("idx_ok"), 1)
                            for k in range(2):
                                for t in range(T):
                                    pool.indirect_dma_start(out=v["yg"][:, k, t, :], out_offset=None, in_=y_d,
                                                            in_offset=bass.IndirectOffsetOnAxis(ap=v["gidx"][:, k, t:t + 1].bitcast(U32), axis=0))\
                                        .then_inc(s(f"y_in{k}{t}"), 16)
                            yield ST_UP
                            pool.memset(v["vn"][:, :, :, DH:V1], 1.0).then_inc(s("one_ok"), 1)
                            pool.memset(v["kv"][:], 0.0).then_inc(s("kv0"), 1)
                            pool.wait_ge(s("x2_ok"), 1)
                            pool.tensor_tensor(v["xb"][:], v["x2"][:], spread(row("bo"), 1, T), ALU.add).then_inc(s("xb_ok"), 1)
                            for i in range(8):
                                yield ST_KF + i // 2
                                pool.wait_ge(s("kf_in"), i + 1)
                                part = v["kf"][:, i // 2, 8 * (i % 2):8 * (i % 2) + 8, :]
                                pool.tensor_scalar(part, part, 1e-6, None, ALU.add).then_inc(s("kf_ok"), 1)
                            yield ST_KV
                            for k in range(2):
                                for t in range(T):
                                    pool.wait_ge(s(f"y_in{k}{t}"), 16)
                                    pool.dma_reset(range(s(f"y_in{k}{t}").num, s(f"y_in{k}{t}").num + 1))
                            yield ST_X3
                            pool.wait_ge(s("x3_ok"), 1)
                            pool.tensor_tensor(v["xb"][:], v["x3"], spread(row("bias"), 1, T), ALU.add).then_inc(s("x3b_ok"), 1)
                        in_stages(lane)

                    @block.tensor
                    def _(pe):
                        def lane(n, v, s):
                            bk = v["bank"]

                            def transposes(src, name, eye=ident, of=lambda b: b[:]):
                                for m in range(K2):
                                    for t in range(T):
                                        mm = pe.transpose(of(bk[m])[:, t * P:(t + 1) * P], src[:, t, m * P:(m + 1) * P], eye[:])
                                    mm.then_inc(s(name), 1)

                            def tokens_major(lhs, w, name):
                                for t in range(T):
                                    for m in range(K2):
                                        mm = pe.matmul(bk[2 + t // 2][:, (t % 2) * D:(t % 2 + 1) * D], lhs[:, m, t * P:(t + 1) * P], w[:, m, :],
                                                       start=(m == 0), stop=(m == K2 - 1))
                                mm.then_inc(s(name), 1)

                            yield ST_IN
                            pe.wait_ge(s("x2_ok"), 1)
                            transposes(v["x2"], "xT_mm")
                            yield ST_DN
                            pe.wait_ge(s("xT_ok"), 2)
                            pe.wait_ge(s("wud_ok"), 1)
                            for m in range(K2):
                                mm = pe.matmul(bk[2][0:M, :], v["wdn"][:, m, :], v["xT"][:, m, :], start=(m == 0), stop=(m == K2 - 1))
                            mm.then_inc(s("dn_mm"), 1)
                            yield ST_UP
                            pe.wait_ge(s("dn_ok"), 1)
                            for m in range(K2):
                                pe.matmul(bk[m][:], v["wup"][:, m * P:(m + 1) * P], v["dT"][:], start=True, stop=True).then_inc(s("up_mm"), 1)
                            yield ST_QK
                            pe.wait_ge(s("hc_ok"), 2)
                            for i in range(4):
                                w, o = 1 - i // 2, i % 2
                                for m in range(K2):
                                    mm = pe.matmul(bk[(3, 2, 0, 1)[i]][:], wqkv[:, w, m, o * P:(o + 1) * P], v["hcT"][:, m, :],
                                                   start=(m == 0), stop=(m == K2 - 1))
                                mm.then_inc(s("qk_mm"), 1)
                            yield ST_V
                            pe.wait_ge(s("sq_ok"), 2)
                            tokens_major(v["hcT"], wqkv[:, 2], "v_mm")
                            pe.wait_ge(s("sq_ok"), 4)
                            for t in range(T):
                                for m in range(K2):
                                    mm = pe.matmul(bk[0][:, (2 * t + m) * 8:(2 * t + m + 1) * 8], v["k2"][:, m, t * P:(t + 1) * P], nrmk[:],
                                                   start=True, stop=True)
                            mm.then_inc(s("kn_mm"), 1)
                            for i in range(8):
                                yield ST_KF + i // 2
                                t, m = i // 2, i % 2
                                if i == 0:
                                    pe.wait_ge(s("v_ok"), 1)
                                    pe.wait_ge(s("kn_ok"), 1)
                                if i >= 2:
                                    pe.wait_ge(s("kf_sub"), i - 1)
                                pe.matmul(bk[(1, 3)[i % 2]][:], v["kT"][:, m, t * P:(t + 1) * P], orfk[:], start=True, stop=True)\
                                    .then_inc(s("kf_mm"), 1)
                                m, r = i // 4, 32 * (i % 4)
                                if i >= 2:
                                    pe.wait_ge(s("qf_in"), i - 1)
                                dst = bk[(2, 0)[i % 2]][:]
                                pe.matmul(dst, orfk[r:r + 32, (i % 4) * P:(i % 4 + 1) * P], v["qT"][r:r + 32, m, :], start=True, stop=False)
                                pe.matmul(dst, nrmq[r:r + 32, :], v["q2"][r:r + 32, m, :], start=False, stop=True).then_inc(s("qf_mm"), 1)
                            yield ST_KV
                            pe.wait_ge(s("kf_ok"), 8)
                            for i in range(NP):
                                for t in range(T):
                                    mm = pe.matmul(bk[1][:, i * 2 * V1:(i + 1) * 2 * V1], v["kf"][:, t, 2 * i:2 * i + 2, :].rearrange("p h m -> p (h m)"),
                                                   v["vn"][:, t, 2 * i:2 * i + 2, :].rearrange("p h d -> p (h d)"), start=(t == 0), stop=(t == T - 1))
                            mm.then_inc(s("kv_mm"), 1)
                            yield ST_O
                            pe.wait_ge(s("kv_ok"), 1)
                            pe.wait_ge(s("qf_ok"), NP)
                            for t in range(T):
                                for i in range(NP):
                                    mm = pe.matmul(bk[t][:, i * 2 * V1:(i + 1) * 2 * V1], v["qf"][:, i, t * P:(t + 1) * P], v["kv"][:, i, :],
                                                   start=True, stop=True)
                                mm.then_inc(s("o_mm"), 1)
                            yield ST_OT
                            pe.wait_ge(s("on_ok"), T)
                            transposes(v["on"], "oT_mm")
                            yield ST_X3
                            pe.wait_ge(s("oT_ok"), 2)
                            tokens_major(v["xT"], wo1, "wo_mm")
                            yield ST_X3T
                            pe.wait_ge(s("x3_ok"), 1)
                            transposes(v["x3"], "x3T_mm")
                            yield ST_Y
                            pe.wait_ge(s("x3T_ok"), 2)
                            tokens_major(v["hcT"], v["wde"], "yq_mm")
                            yield ST_Q
                            pe.wait_ge(s("yb_ok"), 1)
                            transposes(v["yb"], "qbT_mm", identb, lambda b: b[:].bitcast(BF16))
                            yield ST_ACC
                            pe.wait_ge(s("qbT_ok"), 2)
                            tokens_major(v["qbT"], wqb, "acc_mm")
                        in_stages(lane)

                    @block.scalar
                    def _(act):
                        def lane(n, v, s):
                            bk = v["bank"]
                            yield ST_IN
                            for m in range(K2):
                                act.wait_ge(s("xT_mm"), m + 1)
                                act.copy(v["xT"][:, m, :], bk[m][:]).then_inc(s("xT_ok"), 1)
                            yield ST_DN
                            act.wait_ge(s("dn_mm"), 1)
                            act.activation(v["dT"][:], bk[2][0:M, :], ACT.Relu).then_inc(s("dn_ok"), 1)
                            yield ST_QK
                            for i in range(4):
                                w, o = 1 - i // 2, i % 2
                                src = bk[(3, 2, 0, 1)[i]][:]
                                dst, sq = ((v["qT"], v["q2"]), (v["kT"], v["k2"]))[w]
                                act.wait_ge(s("qk_mm"), i + 1)
                                act.activation(dst[:, o, :], src, ACT.Identity, bias=qkcol[:, w, o:o + 1])
                                act.activation(sq[:, o, :], src, ACT.Square, bias=qkcol[:, w, o:o + 1]).then_inc(s("sq_ok"), 1)
                            for i in range(8):
                                yield ST_KF + i // 2
                                part = v["kf"][:, i // 2, 8 * (i % 2):8 * (i % 2) + 8, :]
                                act.wait_ge(s("kf_sub"), i + 1)
                                act.activation(part, part, ACT.Exp).then_inc(s("kf_in"), 1)
                                act.wait_ge(s("qf_mm"), i + 1)
                                act.activation(v["qf"][:, i, :], bk[(2, 0)[i % 2]][:], ACT.Exp).then_inc(s("qf_in"), 1)
                            yield ST_OT
                            for m in range(K2):
                                act.wait_ge(s("oT_mm"), m + 1)
                                act.copy(v["xT"][:, m, :], bk[m][:]).then_inc(s("oT_ok"), 1)
                            yield ST_X3T
                            for m in range(K2):
                                act.wait_ge(s("x3T_mm"), m + 1)
                                act.copy(v["hcT"][:, m, :], bk[m][:]).then_inc(s("x3T_ok"), 1)
                            yield ST_Q
                            for m in range(K2):
                                act.wait_ge(s("qbT_mm"), m + 1)
                                act.copy(v["qbT"][:, m, :], bk[m][:].bitcast(BF16)[:, 0:S]).then_inc(s("qbT_ok"), 1)
                        in_stages(lane)

                    @block.vector
                    def _(dve):
                        def lane(n, v, s):
                            done, settle = chain_of(dve, s("dve_own"))
                            bk, x2, kf, qf, yq, ab, fo = v["bank"], v["x2"], v["kf"], v["qf"], v["yq"], v["ab"], v["fo"]
                            two = lambda bank: bank[:].rearrange("p (t f) -> p t f", t=2)
                            yield ST_GI
                            dve.wait_ge(s("gi_in"), 16)
                            dve.tensor_copy(v["gidx"][:], v["gi"][:, 2:4, :]).then_inc(s("idx_ok"), 1)
                            yield ST_IN
                            dve.wait_ge(s("p_in"), 64)
                            done(dve.tensor_tensor(v["wdn"][:], dup[:], spread(v["dgb"][:, 0, :], 1, K2), ALU.mult))
                            done(dve.tensor_tensor(v["wup"][:], upp[:], v["ugb"][:, 0, :], ALU.mult))
                            settle()
                            dve.tensor_tensor(v["wdn"][:], v["wdn"][:], spread(v["dgb"][:, 1, :], 1, K2), ALU.add)
                            dve.tensor_tensor(v["wup"][:], v["wup"][:], v["ugb"][:, 1, :], ALU.add).then_inc(s("wud_ok"), 1)
                            dve.wait_ge(s("x_in"), 16)
                            for k in range(2):
                                if k:
                                    settle()
                                for t in range(T):
                                    dve.wait_ge(s(f"y_in{k}{t}"), 16)
                                    ins = dve.scalar_tensor_tensor(x2[:, t, :], v["yg"][:, k, t, :], v["gi"][:, k, t:t + 1], x2[:, t, :],
                                                                   ALU.mult, ALU.add)
                                    if k == 0:
                                        done(ins)
                            ins.then_inc(s("x2_ok"), 1)
                            yield ST_UP
                            for m in range(K2):
                                dve.wait_ge(s("up_mm"), m + 1)
                                dve.wait_ge(s("xT_ok"), 2)
                                dve.tensor_tensor(v["hcT"][:, m, :], bk[m][:], v["xT"][:, m, :], ALU.add).then_inc(s("hc_ok"), 1)
                            yield ST_V
                            dve.wait_ge(s("v_mm"), 1)
                            dve.wait_ge(s("one_ok"), 1)
                            for c in range(2):
                                last = dve.tensor_tensor(v["vn"][:, 2 * c:2 * c + 2, :, 0:DH].rearrange("p t h d -> p (t h) d"),
                                                         bk[2 + c][:].rearrange("p (h d) -> p h d", d=DH),
                                                         spread(row("bv"), 1, 2).rearrange("p t (h d) -> p t h d", d=DH), ALU.add)
                            last.then_inc(s("v_ok"), 1)
                            dve.wait_ge(s("kn_mm"), 1)
                            dve.tensor_copy(v["kn"][:].rearrange("p t m h -> p (t m h)"), bk[0][:, 0:T * H]).then_inc(s("kn_ok"), 1)
                            dve.wait_ge(s("kn_ok"), 1)
                            for i in range(8):
                                yield ST_KF + i // 2
                                dve.wait_ge(s("kf_mm"), i + 1)
                                dve.tensor_tensor(kf[:, i // 2, 8 * (i % 2):8 * (i % 2) + 8, :],
                                                  bk[(1, 3)[i % 2]][:].rearrange("p (h m) -> p h m", m=M),
                                                  spread(v["kn"][:, i // 2, i % 2, :], 2, M), ALU.add).then_inc(s("kf_sub"), 1)
                                if i:
                                    dve.wait_ge(s("qf_in"), i)
                                    dve.tensor_scalar(qf[:, i - 1, :], qf[:, i - 1, :], 1e-6, None, ALU.add).then_inc(s("qf_ok"), 1)
                            yield ST_KV
                            dve.wait_ge(s("qf_in"), NP)
                            dve.tensor_scalar(qf[:, NP - 1, :], qf[:, NP - 1, :], 1e-6, None, ALU.add).then_inc(s("qf_ok"), 1)
                            dve.wait_ge(s("kv0"), 1)
                            dve.wait_ge(s("kv_mm"), 1)
                            src = bk[1][:, 0:NP * 2 * V1].rearrange("p (n c) -> p n c", c=2 * V1)
                            dve.tensor_copy(v["kv"][0:M, :, 0:V1], src[0:M, :, 0:V1])
                            dve.tensor_copy(v["kv"][M:P, :, V1:2 * V1], src[M:P, :, V1:2 * V1]).then_inc(s("kv_ok"), 1)
                            yield ST_O
                            for t in range(T):
                                o = bk[t][:, 0:NP * 2 * V1].rearrange("p (h c) -> p h c", c=V1)
                                dve.wait_ge(s("o_mm"), t + 1)
                                done(dve.reciprocal(v["den"][:, t, :], o[:, :, DH]))
                                settle()
                                dve.tensor_tensor(v["on"][:, t, :].rearrange("p (h d) -> p h d", d=DH), o[:, :, 0:DH],
                                                  spread(v["den"][:, t, :], 2, DH), ALU.mult).then_inc(s("on_ok"), 1)
                            yield ST_X3
                            dve.wait_ge(s("wo_mm"), 1)
                            dve.wait_ge(s("xb_ok"), 1)
                            for c in range(2):
                                last = dve.tensor_tensor(v["x3"][:, 2 * c:2 * c + 2, :], two(bk[2 + c]), v["xb"][:, 2 * c:2 * c + 2, :], ALU.add)
                            last.then_inc(s("x3_ok"), 1)
                            yield ST_Y
                            dve.wait_ge(s("yq_mm"), 1)
                            for c in range(2):
                                done(dve.tensor_tensor(yq[:, 2 * c:2 * c + 2, :], two(bk[2 + c]), spread(v["brow"][:], 1, 2), ALU.add))
                            settle()
                            done(dve.tensor_reduce(ab[:, 0, :], yq[:], X, ALU.max, apply_absolute_value=True))
                            settle()
                            done(dve.tensor_scalar(ab[:, 1, :], ab[:, 0, :], 1e-6, 1.0 / 127.0, ALU.max, ALU.mult))
                            settle()
                            done(dve.reciprocal(ab[:, 2, :], ab[:, 1, :]))
                            settle()
                            for t in range(T):
                                done(dve.tensor_scalar(yq[:, t, :], yq[:, t, :], ab[:, 2, t:t + 1], ROUND, ALU.mult, ALU.add))
                            settle()
                            dve.tensor_scalar(v["yb"][:], yq[:], ROUND, 127.0, ALU.subtract, ALU.min).then_inc(s("yb_ok"), 1)
                            yield ST_ACC
                            dve.wait_ge(s("acc_mm"), 1)
                            for t in range(T):
                                done(dve.scalar_tensor_tensor(fo[:, t, :], bk[2 + t // 2][:, (t % 2) * D:(t % 2 + 1) * D], ab[:, 1, t:t + 1],
                                                              row("ws"), ALU.mult, ALU.mult))
                            settle()
                            dve.wait_ge(s("x3b_ok"), 1)
                            dve.tensor_tensor(fo, fo, v["xb"][:], ALU.add).then_inc(s("fin"), 1)
                        in_stages(lane)
                s.clear()


def layouts(i):
    f = np.float32

    def tiles(w):
        return w.reshape(-1, P, w.shape[1]).transpose(1, 0, 2)

    def padded(w, rows=P):
        o = np.zeros((rows,) + w.shape[1:], w.dtype)
        o[:w.shape[0]] = w
        return o

    o = {}
    x = i["x"]
    o["xT"] = x.transpose(0, 2, 1).reshape(B, K2, P, S).transpose(0, 2, 1, 3)
    o["xN"] = x.reshape(B, T, P, D).transpose(0, 2, 1, 3)
    o["ids"] = np.concatenate([i[k].reshape(B, T, P).transpose(0, 2, 1)
                               for k in ("itok_BxS_0_999", "itok_BxS_0_4", "mask_BxS_ik0")], 2)
    o["boff"] = (CAP * np.arange(B)).astype(f).reshape(B, 1)
    o["cond"] = np.stack([padded(i[k].T) for k in ("cond_512", "cond_64", "fside_Bx32_0")], 1)
    o["affw"] = np.stack([i[f"L0_cond_{k}_aff_w"].T.reshape(P, K2, P) for k in "ko"], 1)
    o["affb"] = np.stack([i[f"L0_cond_{k}_aff_b"].reshape(K2, P).T for k in "ko"], 1)
    o["kow"] = np.stack([tiles(i[f"L0_cond_{k}_w"].T) for k in "ko"], 1)
    o["obcol"] = i["L0_cond_o_b"].reshape(K2, P).T
    wqkv = i["L0_attn_w_qkv"].T
    bqkv = i["L0_attn_b_qkv"]
    o["wqk"] = tiles(wqkv[:, 0:2 * D])
    o["wvl"] = tiles(np.concatenate([wqkv[:, 2 * D:]] + [i[f"L0_attn_{k}"].T for k in
                                    ("w1_read", "w2_read", "w2_write", "w1_write")], 1))
    o["wout"] = tiles(i["L0_attn_w_out"].T)
    dl, bs = i["L0_attn_decay_logits"], i["L0_attn_bias_scale"]
    o["dlr"] = np.concatenate([np.broadcast_to(dl, (P, H)), np.repeat(dl.reshape(HG, HG).T, 32, 0)], 1)
    aw = i["L0_cond2_aw"]
    c2 = lambda k: i[f"L0_cond2_{k}"]
    o["rows0"] = np.concatenate([i["L0_cond_k_b"], bqkv[0:2 * D], bqkv[2 * D:], i["L0_attn_b_out"], c2("int_b2"),
                                 c2("int_g"), c2("int_be"), i["L0_ffn_br"], aw, dl, bs])
    q = np.arange(P, dtype=f)
    r = np.arange(P) % 32
    o["cst"] = np.stack([q, P - q, (r < DH), (r >= DH) & (r < DH + NOFF), (r >= DH + NOFF) & (r < DH + 2 * NOFF),
                         0 * q, 0 * q, 0 * q], 1).astype(f)
    o["ident"] = np.eye(P, dtype=f)
    o["identb"] = np.eye(P, dtype=mybir.dt.np(BF16))
    dist = q[:, None] - q[None, :]
    o["posd"] = np.maximum(dist, 0).astype(f)
    o["low"] = (dist > 0).astype(f)
    o["tri"] = (dist < 0).astype(mybir.dt.np(BF16))
    o["sel"] = np.repeat(np.eye(H // 2, dtype=f), DH, 1)
    o["negb"] = np.where(dist < 0, MASKED, 0.0).astype(mybir.dt.np(BF16))
    o["iota"] = np.arange(SLOTS, dtype=f)
    sg = np.ones((2 * H, NOFF), f)
    sg[H:, 1] = sg[H:, 4] = -1
    o["sign"] = sg
    o["w1all"] = tiles(c2("int_W1"))
    o["wint2"] = tiles(c2("int_W2"))
    o["ib1"] = c2("int_b1").reshape(K2, P).T
    o["m1"] = np.stack([padded(c2(f"{k}_W1")) for k in ("mem", "noi", "res")], 1)
    o["m2"] = np.stack([tiles(c2(f"{k}_W2")) for k in ("mem", "noi", "res")], 1)
    o["mrow"] = np.stack([np.stack([c2(f"{k}_{n}") for n in ("b1", "b2", "g", "be")]) for k in ("mem", "noi", "res")])
    o["pw"] = np.concatenate([c2("pw_g"), c2("pw_b")], 1)
    o["cptm"] = np.concatenate([c2("cp_g"), c2("cp_b"), c2("tm_g"), c2("tm_b")], 1)
    o["ms"] = np.concatenate([c2("ms_g"), c2("ms_b")], 1)
    o["wr"] = tiles(i["L0_ffn_Wr"])
    o["eW1"] = i["L0_ffn_W1"].reshape(E, K2, P, HID).transpose(0, 2, 1, 3)
    o["eW2"] = i["L0_ffn_W2"].reshape(E, KH, P, D).transpose(0, 2, 1, 3)
    o["eb1"] = i["L0_ffn_b1"].reshape(E, KH, P).transpose(0, 2, 1)
    o["eb2"] = i["L0_ffn_b2"]
    o["dgu"] = np.concatenate([i[f"L1_cond_{k}"] for k in ("down_gamma", "down_beta", "up_gamma", "up_beta")], 1)
    o["wdc"] = i["L1_cond2_W_dec"].reshape(P, D + 1, KR).transpose(0, 2, 1)
    bd = i["L1_cond2_b_dec"].reshape(D + 1, KR)
    o["bdc"] = bd[0:D].reshape(K2, P, KR).transpose(1, 0, 2)
    o["bdl"] = bd[D].reshape(KR, 1)
    o["vv"] = i["L1_cond2_V"]
    o["dup"] = tiles(i["L1_cond_down_project"])
    o["upp"] = i["L1_cond_up_project"]
    o["wqkv"] = np.stack([tiles(i[f"L1_attn_W{k}"].T) for k in "qkv"], 1)
    o["wo1"] = tiles(i["L1_attn_Wo"].T)
    o["qkcol"] = np.stack([i[f"L1_attn_b{k}"].reshape(K2, P).T for k in "qk"], 1)
    orf = np.zeros((8, DH, 8, M), f)
    for h in range(8):
        orf[h, :, h, :] = i["L1_attn_orf"].T
    o["orfk"] = orf.reshape(P, 8 * M)
    nk = np.zeros((P, 8), f)
    nk[np.arange(P), np.arange(P) // DH] = -1.0 / 8
    o["nrmk"] = nk
    nq = np.zeros((P, P), f)
    for p in range(P):
        h = p // DH % 2
        nq[p, h * M:(h + 1) * M] = -1.0 / 8
    o["nrmq"] = nq
    o["wq8"] = np.ascontiguousarray(tiles(i["L1_ffn_weight_q"].T)).view(np.int32)
    o["rows1"] = np.concatenate([i["L1_attn_bv"], i["L1_attn_bo"], i["L1_ffn_weight_scale"], i["L1_ffn_bias"]])
    return {k: np.ascontiguousarray(v) for k, v in o.items()}


def kernel(**inputs):
    import concourse.bacc as bacc
    from concourse.bass_utils import run_bass_kernel_spmd

    nc = bacc.Bacc("TRN2", target_bir_lowering=False, num_devices=1)
    arrays = {f"in_{k}": v for k, v in layouts({k: np.asarray(v) for k, v in inputs.items()}).items()}
    a = {k[3:]: nc.dram_tensor(k, v.shape, mybir.dt.from_np(v.dtype), kind="ExternalInput").ap() for k, v in arrays.items()}
    out = nc.dram_tensor("out_0", (B, S, D), F32, kind="ExternalOutput").ap()
    program(nc, a, out)
    r = run_bass_kernel_spmd(nc, [arrays], core_ids=[0])
    return r.results[0]["out_0"]
```
